# Optimizing a Trainium2 kernel written in Bass

```python
import numpy as np
import jax
import jax.numpy as jnp

def _softmax(x, axis=-1):
    return jax.nn.softmax(x, axis=axis)

def _gelu(x):
    return jax.nn.gelu(x, approximate=True)

def _silu(x):
    return jax.nn.silu(x)

def _sigmoid(x):
    return jax.nn.sigmoid(x)

def _layernorm(x, axis=-1, eps=1e-05):
    m = jnp.mean(x, axis=axis, keepdims=True)
    v = jnp.var(x, axis=axis, keepdims=True)
    return (x - m) / jnp.sqrt(v + eps)

def _scatter_add(tgt, idx, src, axis=0):
    return tgt.at[idx].add(src)

def _segment_sum(src, seg, n):
    return jax.ops.segment_sum(src, seg, n)
kernel_name = 'mk_xattn_ffn_d2_seqx_r4_a54dd8'

def setup_inputs(seed: int=0):
    np.random.seed(seed)
    _w = jnp.asarray

    def _rec_inputs():
        import jax
        import jax.numpy as jnp
        _rk = jax.random.key(seed)
        x = 7.22e-05 + 1 * jax.random.normal(jax.random.fold_in(_rk, 1), (32, 100, 256), jnp.float32)
        _lenS = 100 - jax.random.randint(jax.random.fold_in(_rk, 7), (32,), 0, max(1, 100 // 4) + 1, jnp.int32)
        _lenS2 = 361 - jax.random.randint(jax.random.fold_in(_rk, 8), (32,), 0, max(1, 361 // 4) + 1, jnp.int32)
        _ctx_1024P = jax.random.normal(jax.random.fold_in(_rk, 11), (32, 16, 256), jnp.float32)
        _ctx_1024c = jax.random.dirichlet(jax.random.fold_in(_rk, 511), 0.3 * jnp.ones((16,), jnp.float32), (32, 361))
        _ctx_1024t = jnp.einsum('bsk,bkd->bsd', _ctx_1024c, _ctx_1024P)
        _ctx_1024t = _ctx_1024t * jax.lax.rsqrt(jnp.mean(jnp.square(_ctx_1024t)) + 1e-12) * 0.953939
        ctx_1024 = 4.13588e-05 + 0.999923 * (_ctx_1024t + 0.3 * jax.random.normal(jax.random.fold_in(_rk, 611), (32, 361, 256), jnp.float32))
        return (x, ctx_1024)
    x, ctx_1024 = _rec_inputs()

    def _L0_xattn_setup():
        import jax, jax.numpy as jnp
        import numpy as np
        D_MODEL = 256
        NUM_HEADS = 16
        D_K = D_MODEL // NUM_HEADS

        def _split_heads(x):
            B, S, _ = x.shape
            return x.reshape(B, S, NUM_HEADS, D_K).transpose(0, 2, 1, 3)
        key = jax.random.key(seed)
        ks = jax.random.split(key, 11)
        B, S = (4, 512)
        s = 1.0 / np.sqrt(D_MODEL)
        return {'Q': jax.random.normal(ks[0], (B, S, D_MODEL), jnp.float32), 'K': jax.random.normal(ks[1], (B, S, D_MODEL), jnp.float32), 'V': jax.random.normal(ks[2], (B, S, D_MODEL), jnp.float32), 'Wq': jax.random.normal(ks[3], (D_MODEL, D_MODEL), jnp.float32) * s, 'bq': jax.random.normal(ks[4], (D_MODEL,), jnp.float32) * 0.01, 'Wk': jax.random.normal(ks[5], (D_MODEL, D_MODEL), jnp.float32) * s, 'bk': jax.random.normal(ks[6], (D_MODEL,), jnp.float32) * 0.01, 'Wv': jax.random.normal(ks[7], (D_MODEL, D_MODEL), jnp.float32) * s, 'bv': jax.random.normal(ks[8], (D_MODEL,), jnp.float32) * 0.01, 'Wo': jax.random.normal(ks[9], (D_MODEL, D_MODEL), jnp.float32) * s, 'bo': jax.random.normal(ks[10], (D_MODEL,), jnp.float32) * 0.01}
    _L0_xattn_all = _L0_xattn_setup()
    _L0_xattn_in = {k: v for k, v in _L0_xattn_all.items() if k in ('Wq', 'bq', 'Wk', 'bk', 'Wv', 'bv', 'Wo', 'bo')}
    del _L0_xattn_all

    def _L0_ffn_setup():
        import jax, jax.numpy as jnp
        import numpy as np
        E = 8
        EPS = 1e-05
        key = jax.random.key(seed)
        ks = jax.random.split(key, 6)
        d, f = (256, 1024)
        B, S = (2, 256)
        x = jax.random.normal(ks[0], (B, S, d), dtype=jnp.float32)
        c = jax.random.normal(ks[1], (d, E), dtype=jnp.float32)
        q, _ = jnp.linalg.qr(c)
        centroids = (0.1 * q.T).astype(jnp.float32)
        w1 = jax.random.normal(ks[2], (E, d, f), dtype=jnp.float32) / np.sqrt(d).astype(np.float32)
        b1 = jnp.zeros((E, f), dtype=jnp.float32)
        w2 = jax.random.normal(ks[3], (E, f, d), dtype=jnp.float32) * 0.02
        b2 = jnp.zeros((E, d), dtype=jnp.float32)
        gamma = jnp.ones((E, d), dtype=jnp.float32)
        beta = jnp.zeros((E, d), dtype=jnp.float32)
        return dict(x=x, centroids=centroids, w1=w1, b1=b1, w2=w2, b2=b2, gamma=gamma, beta=beta)
    _L0_ffn_all = _L0_ffn_setup()
    _L0_ffn_in = {k: v for k, v in _L0_ffn_all.items() if k in ('centroids', 'w1', 'b1', 'w2', 'b2', 'gamma', 'beta')}
    del _L0_ffn_all

    def _L1_xattn_setup():
        import jax, jax.numpy as jnp
        import numpy as np
        HEADS = 8
        DIM_HEAD = 64
        DIM = 256
        CTX_DIM = 256
        HIDDEN = HEADS * DIM_HEAD
        key = jax.random.key(seed)
        ks = jax.random.split(key, 7)
        b, n, m = (2, 512, 512)
        x = jax.random.normal(ks[0], (b, n, DIM), dtype=jnp.float32)
        context = jax.random.normal(ks[1], (b, m, CTX_DIM), dtype=jnp.float32)
        Wq = jax.random.normal(ks[2], (DIM, HIDDEN), dtype=jnp.float32) * (1.0 / np.sqrt(DIM))
        Wk = jax.random.normal(ks[3], (CTX_DIM, HIDDEN), dtype=jnp.float32) * (1.0 / np.sqrt(CTX_DIM))
        Wv = jax.random.normal(ks[4], (CTX_DIM, HIDDEN), dtype=jnp.float32) * (1.0 / np.sqrt(CTX_DIM))
        Wo = jax.random.normal(ks[5], (HIDDEN, DIM), dtype=jnp.float32) * (1.0 / np.sqrt(HIDDEN))
        bo = jax.random.normal(ks[6], (DIM,), dtype=jnp.float32) * 0.01
        return {'x': x, 'context': context, 'Wq': Wq, 'Wk': Wk, 'Wv': Wv, 'Wo': Wo, 'bo': bo}
    _L1_xattn_all = _L1_xattn_setup()
    _L1_xattn_in = {k: v for k, v in _L1_xattn_all.items() if k in ('Wq', 'Wk', 'Wv', 'Wo', 'bo')}
    del _L1_xattn_all

    def _L1_ffn_setup():
        import jax, jax.numpy as jnp
        import numpy as np
        B, S, D = (4, 256, 256)
        I = 128
        E = 32
        TOP_K = 8
        N_GROUP = 8
        TOPK_GROUP = 4

        def _group_topk(scores):
            T = scores.shape[0]
            epg = E // N_GROUP
            group_scores = scores.reshape(T, N_GROUP, epg).sum(axis=-1)
            _, top_groups = jax.lax.top_k(group_scores, TOPK_GROUP)
            group_mask = jnp.zeros((T, N_GROUP), scores.dtype).at[jnp.arange(T)[:, None], top_groups].set(1.0)
            expert_mask = jnp.repeat(group_mask, epg, axis=1)
            masked_scores = scores * expert_mask
            topk_w, topk_i = jax.lax.top_k(masked_scores, TOP_K)
            return (topk_w, topk_i)

        def _reference_tuple_inner(hidden_states, gate_w, expert_gate, expert_up, expert_down, shared_gate_w, shared_up_w, shared_down_w):
            b, s, d = hidden_states.shape
            flat = hidden_states.reshape(-1, d)
            T = flat.shape[0]
            logits = flat @ gate_w.T
            scores = jax.nn.sigmoid(logits)
            topk_w, topk_i = _group_topk(scores)
            topk_w = topk_w / jnp.clip(topk_w.sum(axis=-1, keepdims=True), 1e-12)
            combine = jnp.zeros((T, E), flat.dtype).at[jnp.arange(T)[:, None], topk_i].add(topk_w)

            def body(acc, expert):
                wg, wu, wd, w = expert
                h = jax.nn.silu(flat @ wg.T) * (flat @ wu.T)
                return (acc + w[:, None] * (h @ wd.T), None)
            out, _ = jax.lax.scan(body, jnp.zeros_like(flat), (expert_gate, expert_up, expert_down, combine.T))
            shared = jax.nn.silu(flat @ shared_gate_w.T) * (flat @ shared_up_w.T) @ shared_down_w.T
            out = out + shared
            return (out.reshape(b, s, d), logits)
        key = jax.random.key(seed)
        ks = jax.random.split(key, 8)
        scale = 0.02
        return {'hidden_states': jax.random.normal(ks[0], (B, S, D), jnp.float32), 'gate_w': jax.random.normal(ks[1], (E, D), jnp.float32) * scale, 'expert_gate': jax.random.normal(ks[2], (E, I, D), jnp.float32) * scale, 'expert_up': jax.random.normal(ks[3], (E, I, D), jnp.float32) * scale, 'expert_down': jax.random.normal(ks[4], (E, D, I), jnp.float32) * scale, 'shared_gate_w': jax.random.normal(ks[5], (I, D), jnp.float32) * scale, 'shared_up_w': jax.random.normal(ks[6], (I, D), jnp.float32) * scale, 'shared_down_w': jax.random.normal(ks[7], (D, I), jnp.float32) * scale}
    _L1_ffn_all = _L1_ffn_setup()
    _L1_ffn_in = {k: v for k, v in _L1_ffn_all.items() if k in ('gate_w', 'expert_gate', 'expert_up', 'expert_down', 'shared_gate_w', 'shared_up_w', 'shared_down_w')}
    del _L1_ffn_all
    return {'x': x, 'ctx_1024': ctx_1024, 'L0_xattn_Wq': _L0_xattn_in['Wq'], 'L0_xattn_bq': _L0_xattn_in['bq'], 'L0_xattn_Wk': _L0_xattn_in['Wk'], 'L0_xattn_bk': _L0_xattn_in['bk'], 'L0_xattn_Wv': _L0_xattn_in['Wv'], 'L0_xattn_bv': _L0_xattn_in['bv'], 'L0_xattn_Wo': _L0_xattn_in['Wo'], 'L0_xattn_bo': _L0_xattn_in['bo'], 'L0_ffn_centroids': _L0_ffn_in['centroids'], 'L0_ffn_w1': _L0_ffn_in['w1'], 'L0_ffn_b1': _L0_ffn_in['b1'], 'L0_ffn_w2': _L0_ffn_in['w2'], 'L0_ffn_b2': _L0_ffn_in['b2'], 'L0_ffn_gamma': _L0_ffn_in['gamma'], 'L0_ffn_beta': _L0_ffn_in['beta'], 'L1_xattn_Wq': _L1_xattn_in['Wq'], 'L1_xattn_Wk': _L1_xattn_in['Wk'], 'L1_xattn_Wv': _L1_xattn_in['Wv'], 'L1_xattn_Wo': _L1_xattn_in['Wo'], 'L1_xattn_bo': _L1_xattn_in['bo'], 'L1_ffn_gate_w': _L1_ffn_in['gate_w'], 'L1_ffn_expert_gate': _L1_ffn_in['expert_gate'], 'L1_ffn_expert_up': _L1_ffn_in['expert_up'], 'L1_ffn_expert_down': _L1_ffn_in['expert_down'], 'L1_ffn_shared_gate_w': _L1_ffn_in['shared_gate_w'], 'L1_ffn_shared_up_w': _L1_ffn_in['shared_up_w'], 'L1_ffn_shared_down_w': _L1_ffn_in['shared_down_w']}

def reference(x, ctx_1024, L0_xattn_Wq, L0_xattn_bq, L0_xattn_Wk, L0_xattn_bk, L0_xattn_Wv, L0_xattn_bv, L0_xattn_Wo, L0_xattn_bo, L0_ffn_centroids, L0_ffn_w1, L0_ffn_b1, L0_ffn_w2, L0_ffn_b2, L0_ffn_gamma, L0_ffn_beta, L1_xattn_Wq, L1_xattn_Wk, L1_xattn_Wv, L1_xattn_Wo, L1_xattn_bo, L1_ffn_gate_w, L1_ffn_expert_gate, L1_ffn_expert_up, L1_ffn_expert_down, L1_ffn_shared_gate_w, L1_ffn_shared_up_w, L1_ffn_shared_down_w):
    import jax
    import jax.numpy as jnp

    def _L0_xattn_ref(Q, K, V, Wq, bq, Wk, bk, Wv, bv, Wo, bo):
        import jax, jax.numpy as jnp
        import numpy as np
        D_MODEL = 256
        NUM_HEADS = 16
        D_K = D_MODEL // NUM_HEADS

        def _split_heads(x):
            B, S, _ = x.shape
            return x.reshape(B, S, NUM_HEADS, D_K).transpose(0, 2, 1, 3)
        q = _split_heads(Q @ Wq.T + bq)
        k = _split_heads(K @ Wk.T + bk)
        v = _split_heads(V @ Wv.T + bv)
        scale = 1.0 / jnp.sqrt(jnp.asarray(D_K, jnp.float32))
        scores = jnp.einsum('bhqd,bhkd->bhqk', q, k) * scale
        attn = jax.nn.softmax(scores, axis=-1)
        ctx = jnp.einsum('bhqk,bhkd->bhqd', attn, v)
        B, H, S, Dk = ctx.shape
        ctx = ctx.transpose(0, 2, 1, 3).reshape(B, S, H * Dk)
        return ctx @ Wo.T + bo

    def _L0_ffn_ref(x, centroids, w1, b1, w2, b2, gamma, beta):
        import jax, jax.numpy as jnp
        import numpy as np
        E = 8
        EPS = 1e-05
        B, S, d = x.shape
        feats = x.reshape(-1, d)
        aff = feats @ centroids.T
        eid = jnp.argmax(aff, axis=1)
        mu = jnp.mean(feats, axis=-1, keepdims=True)
        var = jnp.var(feats, axis=-1, keepdims=True)
        xhat = (feats - mu) * jax.lax.rsqrt(var + EPS)
        out = jnp.zeros_like(feats)
        for e in range(E):
            mask = (eid == e).astype(feats.dtype)[:, None]
            h = xhat * gamma[e] + beta[e]
            y = feats + jax.nn.relu(h @ w1[e] + b1[e]) @ w2[e] + b2[e]
            alpha = jax.nn.sigmoid(feats @ centroids[e])[:, None]
            out = out + mask * (alpha * y + (1.0 - alpha) * feats)
        return out.reshape(B, S, d)

    def _L1_xattn_ref(x, context, Wq, Wk, Wv, Wo, bo):
        import jax, jax.numpy as jnp
        import numpy as np
        HEADS = 8
        DIM_HEAD = 64
        DIM = 256
        CTX_DIM = 256
        HIDDEN = HEADS * DIM_HEAD
        b, n, _ = x.shape
        m = context.shape[1]
        scale = DIM_HEAD ** (-0.5)
        q = (x @ Wq).reshape(b, n, HEADS, DIM_HEAD).transpose(0, 2, 1, 3)
        k = (context @ Wk).reshape(b, m, HEADS, DIM_HEAD).transpose(0, 2, 1, 3)
        v = (context @ Wv).reshape(b, m, HEADS, DIM_HEAD).transpose(0, 2, 1, 3)
        scores = jnp.einsum('bhnd,bhmd->bhnm', q, k) * scale
        attn = jax.nn.softmax(scores, axis=-1)
        out = jnp.einsum('bhnm,bhmd->bhnd', attn, v)
        out = out.transpose(0, 2, 1, 3).reshape(b, n, HIDDEN)
        return out @ Wo + bo

    def _L1_ffn_ref(hidden_states, gate_w, expert_gate, expert_up, expert_down, shared_gate_w, shared_up_w, shared_down_w):
        import jax, jax.numpy as jnp
        import numpy as np
        B, S, D = (4, 256, 256)
        I = 128
        E = 32
        TOP_K = 8
        N_GROUP = 8
        TOPK_GROUP = 4

        def _group_topk(scores):
            T = scores.shape[0]
            epg = E // N_GROUP
            group_scores = scores.reshape(T, N_GROUP, epg).sum(axis=-1)
            _, top_groups = jax.lax.top_k(group_scores, TOPK_GROUP)
            group_mask = jnp.zeros((T, N_GROUP), scores.dtype).at[jnp.arange(T)[:, None], top_groups].set(1.0)
            expert_mask = jnp.repeat(group_mask, epg, axis=1)
            masked_scores = scores * expert_mask
            topk_w, topk_i = jax.lax.top_k(masked_scores, TOP_K)
            return (topk_w, topk_i)

        def _reference_tuple_inner(hidden_states, gate_w, expert_gate, expert_up, expert_down, shared_gate_w, shared_up_w, shared_down_w):
            b, s, d = hidden_states.shape
            flat = hidden_states.reshape(-1, d)
            T = flat.shape[0]
            logits = flat @ gate_w.T
            scores = jax.nn.sigmoid(logits)
            topk_w, topk_i = _group_topk(scores)
            topk_w = topk_w / jnp.clip(topk_w.sum(axis=-1, keepdims=True), 1e-12)
            combine = jnp.zeros((T, E), flat.dtype).at[jnp.arange(T)[:, None], topk_i].add(topk_w)

            def body(acc, expert):
                wg, wu, wd, w = expert
                h = jax.nn.silu(flat @ wg.T) * (flat @ wu.T)
                return (acc + w[:, None] * (h @ wd.T), None)
            out, _ = jax.lax.scan(body, jnp.zeros_like(flat), (expert_gate, expert_up, expert_down, combine.T))
            shared = jax.nn.silu(flat @ shared_gate_w.T) * (flat @ shared_up_w.T) @ shared_down_w.T
            out = out + shared
            return (out.reshape(b, s, d), logits)
        return _reference_tuple_inner(hidden_states, gate_w, expert_gate, expert_up, expert_down, shared_gate_w, shared_up_w, shared_down_w)[0]
    x = x + _L0_xattn_ref(_layernorm(x, axis=-1), ctx_1024, ctx_1024, L0_xattn_Wq, L0_xattn_bq, L0_xattn_Wk, L0_xattn_bk, L0_xattn_Wv, L0_xattn_bv, L0_xattn_Wo, L0_xattn_bo)
    x = x + _L0_ffn_ref(_layernorm(x, axis=-1), L0_ffn_centroids, L0_ffn_w1, L0_ffn_b1, L0_ffn_w2, L0_ffn_b2, L0_ffn_gamma, L0_ffn_beta)
    x = x + _L1_xattn_ref(_layernorm(x, axis=-1), ctx_1024, L1_xattn_Wq, L1_xattn_Wk, L1_xattn_Wv, L1_xattn_Wo, L1_xattn_bo)
    x = x + _L1_ffn_ref(_layernorm(x, axis=-1), L1_ffn_gate_w, L1_ffn_expert_gate, L1_ffn_expert_up, L1_ffn_expert_down, L1_ffn_shared_gate_w, L1_ffn_shared_up_w, L1_ffn_shared_down_w)
    return x

_drawn_inputs = setup_inputs


def setup_inputs(seed=0):
    import zlib

    import numpy as np

    out = dict(_drawn_inputs(seed))
    spreads = {'L0_ffn_b1': (0.0, 0.713),
     'L0_ffn_b2': (0.0, 0.326),
     'L0_ffn_gamma': (1.0, 0.6),
     'L0_ffn_beta': (0.0, 0.732)}
    factors = {'L0_xattn_bq': 8.0,
     'L0_xattn_bk': 8.0,
     'L0_xattn_bv': 3.824,
     'L0_xattn_bo': 4.314,
     'L1_xattn_bo': 8.0,
     'L1_ffn_gate_w': 8.0,
     'L1_ffn_expert_gate': 8.0,
     'L1_ffn_expert_up': 8.0,
     'L1_ffn_expert_down': 8.0,
     'L1_ffn_shared_gate_w': 8.0,
     'L1_ffn_shared_up_w': 8.0,
     'L1_ffn_shared_down_w': 8.0}
    for name, (base, spread) in spreads.items():
        noise = np.random.default_rng([zlib.crc32(name.encode()), seed]).standard_normal(out[name].shape)
        drawn = base * np.exp(spread * noise) if base else spread * noise
        out[name] = jnp.asarray(drawn.astype(out[name].dtype))
    for name, factor in factors.items():
        out[name] = (out[name] * factor).astype(out[name].dtype)
    return out
```

```python
from contextlib import ExitStack

import concourse.bass as bass
from concourse import mybir

F32 = mybir.dt.float32
F32R = mybir.dt.float32r
I32 = mybir.dt.int32
ALU = mybir.AluOpType
ACT = mybir.ActivationFunctionType
AX = mybir.AxisListType
ds = bass.ds

P = 128
NB, S, D = 32, 100, 256
NK = 361
KC = 3
NKP = KC * P
NKE = NK + 1
DC = D // P
T = NB * S
E0, F0, FC = 8, 1024, 8
SLOT_TILE = 256
SLOT_SHIFT = 8
N_ST = (T + E0 * (SLOT_TILE - 1)) // SLOT_TILE
SLOTS = N_ST * SLOT_TILE
E1, G1, GE = 32, 8, 4
TOP_G, TOP_K = 4, 8
TT = T // P
EPS = 1e-5
NEVER = 3.0e38


def peeled(engine, n, body):
    body(0, 0, 0)
    body(1, 0, 1)
    pairs = (n - 3) // 2
    with engine.Fori(0, pairs) as i:
        body(i * 2 + 2, i + 1, 0)
        body(i * 2 + 3, i + 1, 1)
    for k in range(2 * pairs + 2, n):
        body(k, k // 2, k % 2)


def split_product(nc, out, lhs, rhs, first, last):
    parts = ((lhs[0], rhs[0]), (lhs[0], rhs[1]), (lhs[1], rhs[0]))
    for n, (x, y) in enumerate(parts):
        ins = nc.tensor.matmul(out, x, y, start=first and n == 0, stop=last and n == len(parts) - 1)
    return ins


class Memory:

    def __init__(self, nc, ctx, stage):
        self.nc, self.ctx, self.stage = nc, ctx, stage

    def sb(self, name, shape, dt=F32):
        return self.ctx.enter_context(self.nc.sbuf_tensor(f"{self.stage}_{name}", shape, dt))

    def ps(self, name, shape=(P, 512)):
        return self.ctx.enter_context(self.nc.psum_tensor(f"{self.stage}_{name}", list(shape), F32))

    def sem(self, name):
        return self.ctx.enter_context(self.nc.semaphore(f"{self.stage}_{name}"))


def queries_block(nc, lvl, x, q_t, ident, nch, wq_dram, bq_dram, scale, x_dram):
    G = 4
    with ExitStack() as ctx:
        m = Memory(nc, ctx, f"q{lvl}")
        wq = m.sb("wq", [P, DC, nch * P])
        bq = m.sb("bq", [P, nch])
        stats = m.sb("stats", [S, NB, 6])
        mv = m.sb("mv", [S, NB, 2])
        sd = m.sb("sd", [S, NB])
        rstd = m.sb("rstd", [S, NB])
        xn = [m.sb(f"xn{j}", [S, D]) for j in range(2)]
        xg = [m.sb(f"xg{j}", [P, DC, G * S]) for j in range(2)]
        ps_t = [m.ps(f"ps_t{j}") for j in range(2)]
        ps_q = [m.ps(f"ps_q{j}") for j in range(4)]
        loaded, stats_done, var_ready, sd_ready, rstd_ready, xn_ready, t_done, t_evac, q_done, q_evac = (
            m.sem(n) for n in ("loaded", "stats_done", "var_ready", "sd_ready", "rstd_ready", "xn_ready",
                               "t_done", "t_evac", "q_done", "q_evac"))
        n_loads = 1 + (bq_dram is not None) + (x_dram is not None)
        block = ctx.enter_context(nc.Block())

        @block.sync
        def _(sp):
            if x_dram is not None:
                sp.dma_start(x[:, :, :], x_dram.rearrange("b s d -> s b d")).then_inc(loaded, 16)
            sp.dma_start(wq[:, :, :], wq_dram).then_inc(loaded, 16)
            if bq_dram is not None:
                sp.dma_start(bq[:, :], bq_dram).then_inc(loaded, 16)

        @block.vector
        def _(dve):
            dve.wait_ge(loaded, 16 * n_loads)
            with nc.vector.Fori(0, NB) as b:
                nc.vector.bn_stats(stats[:, ds(b, 1), :].rearrange("p o s -> p (o s)"),
                                   x[:, ds(b, 1), :].rearrange("p o d -> p (o d)")).then_inc(stats_done, 1)
            dve.wait_ge(stats_done, NB)
            for b in range(NB):
                last = nc.vector.bn_aggr(mv[:, b, :], stats[:, b, :])
            last.then_inc(stats_done, 1)
            dve.wait_ge(stats_done, NB + 1)
            nc.vector.tensor_scalar_add(sd[:, :], mv[:, :, 1], EPS).then_inc(var_ready, 1)
            dve.wait_ge(sd_ready, 1)
            nc.vector.reciprocal(rstd[:, :], sd[:, :]).then_inc(rstd_ready, 1)
            dve.wait_ge(rstd_ready, 1)

            def normalise(b, j):
                if not isinstance(b, int) or b >= 2:
                    dve.wait_ge(t_done, b - 1)
                nc.vector.tensor_scalar(xn[j][:, :], x[:, ds(b, 1), :].rearrange("p o d -> p (o d)"),
                                        mv[:, ds(b, 1), 0:1].rearrange("p o s -> p (o s)"), rstd[:, ds(b, 1)],
                                        ALU.subtract, ALU.mult).then_inc(xn_ready, 1)

            def evacuate(g, half, gp):
                for c in range(nch):
                    dve.wait_ge(q_done, g * nch + c + 1)
                    bank = ps_q[(gp * nch + c) % 4]
                    out = q_t[:, c, ds(g * (G * S), G * S)]
                    if bq_dram is not None:
                        ins = nc.vector.tensor_scalar(out, bank[:, 0:G * S], bq[:, c:c + 1], scale, ALU.add, ALU.mult)
                    else:
                        ins = nc.vector.tensor_scalar(out, bank[:, 0:G * S], scale, None, ALU.mult)
                    ins.then_inc(q_evac, 1)

            def group(g, half, gp):
                for k in range(G):
                    normalise(g * G + k, k % 2)
                    if k == 3 and not (isinstance(g, int) and g == 0):
                        evacuate(g - 1, None, 1 - gp)
            peeled(nc.vector, NB // G, group)
            evacuate(NB // G - 1, None, 1)

        @block.scalar
        def _(act):
            act.wait_ge(var_ready, 1)
            nc.scalar.activation(sd[:, :], sd[:, :], ACT.Sqrt).then_inc(sd_ready, 1)

            def group(g, half, gp):
                if not isinstance(g, int) or g >= 2:
                    act.wait_ge(q_done, (g - 1) * nch)
                for k in range(G):
                    act.wait_ge(t_done, g * G + k + 1)
                    nc.scalar.copy(xg[gp][:, :, k * S:(k + 1) * S],
                                   ps_t[k % 2][:, 0:DC * S].rearrange("p (c s) -> p c s", c=DC)).then_inc(t_evac, 1)
            peeled(nc.scalar, NB // G, group)

        @block.tensor
        def _(pe):
            def project(g, half, gp):
                pe.wait_ge(t_evac, (g + 1) * G)
                if not (isinstance(g, int) and g == 0):
                    pe.wait_ge(q_evac, g * nch)
                for c in range(nch):
                    bank = ps_q[(gp * nch + c) % 4]
                    for k in range(DC):
                        ins = nc.tensor.matmul(bank[:, 0:G * S], wq[:, k, c * P:(c + 1) * P], xg[gp][:, k, :],
                                               start=(k == 0), stop=(k == DC - 1))
                    ins.then_inc(q_done, 1)

            def group(g, half, gp):
                for k in range(G):
                    pe.wait_ge(xn_ready, g * G + k + 1)
                    if k >= 2 or not (isinstance(g, int) and g == 0):
                        pe.wait_ge(t_evac, g * G + k - 1)
                    for c in range(DC):
                        ins = nc.tensor.transpose(ps_t[k % 2][:, c * S:(c + 1) * S], xn[k % 2][:, c * P:(c + 1) * P],
                                                  ident[0:S, 0:S])
                    ins.then_inc(t_done, 1)
                    if k == 1 and not (isinstance(g, int) and g == 0):
                        project(g - 1, None, 1 - gp)
            pe.wait_ge(loaded, 16 * n_loads)
            peeled(nc.tensor, NB // G, group)
            project(NB // G - 1, None, 1)


def attention_block(nc, lvl, x, q_t, ident, heads, ctx_dram, wk_dram, wv_dram, wo_dram, bk_dram, bv_dram,
                    bo_dram, hmask_dram):
    dk = D // heads if lvl == 0 else 64
    H = heads
    nch = H * dk // P
    HPC = P // dk
    TRANSPOSE_LAG, PV_LAG = 2, 4
    if lvl == 0:
        tasks = [(3, "LT", 0, 0), (6, "OP", 0, 1), (7, "K", 0, 0), (8, "K", 1, 1), (10, "V", 0, 0), (12, "V", 1, 1),
                 (14, "V", 2, 0)]
    else:
        tasks = [(0, "K", 0, 0), (1, "K", 1, 1), (2, "K", 2, 0), (3, "LT", 0, 1), (3, "K", 3, 0), (5, "OP", 0, 1),
                 (5, "V", 0, 0), (6, "V", 1, 1), (7, "V", 2, 0)]
    LT_STEP = next(s for s, k, _, _ in tasks if k == "LT")
    OP_STEP = next(s for s, k, _, _ in tasks if k == "OP")

    with ExitStack() as ctx:
        m = Memory(nc, ctx, f"a{lvl}")
        w_raw = m.sb("w_raw", [P, DC, nch * P])
        wk_s = [m.sb(f"wk_s{j}", [P, DC, nch * P], F32R) for j in range(2)]
        wv_s = [m.sb(f"wv_s{j}", [P, DC, nch * P], F32R) for j in range(2)]
        wo = m.sb("wo", [P, nch, D])
        bk = m.sb("bk", [P, nch])
        bv = m.sb("bv", [P, nch * P]) if bv_dram is not None else None
        bo = m.sb("bo", [S, D])
        hmask = m.sb("hmask", [P, HPC])
        ctx_t = [m.sb(f"ctx{j}", [P, DC, NKP]) for j in range(2)]
        ctx_s = [[m.sb(f"ctx{j}_s{i}", [P, DC, NKP], F32R) for i in range(2)] for j in range(2)]
        kt = [[m.sb(f"kt{j}_s{i}", [P, nch, NKE], F32R) for i in range(2)] for j in range(2)]
        vm = [m.sb(f"vm{j}", [P, KC, H * P]) for j in range(2)]
        qm = m.sb("qm", [P, H, S])
        qs = [[m.sb(f"qs{j}_s{i}", [P, H, S], F32R) for i in range(2)] for j in range(2)]
        neg_max = m.sb("neg_max", [S, 2, H])
        row_sum = m.sb("row_sum", [S, 2, H])
        row_inv = m.sb("row_inv", [S, H])
        prob = [m.sb(f"prob{j}", [S, NKP]) for j in range(4)]
        prob_t = [m.sb(f"prob_t{j}", [P, KC * S]) for j in range(4)]
        inv_wide = m.sb("inv_wide", [S, H, dk])
        ones = m.sb("ones", [S, 1, dk])
        inv_t = m.sb("inv_t", [P, nch * S])
        o_t = m.sb("o_t", [P, nch, S])
        ps_s = [m.ps(f"ps_s{j}") for j in range(2)]
        ps_p = [m.ps(f"ps_p{j}") for j in range(2)]
        ps_o = [m.ps(f"ps_o{j}") for j in range(2)]
        ps_x = [m.ps(f"ps_x{j}") for j in range(2)]
        names = ("loaded", "cleared", "w_loaded", "w_ready", "ctx_hi", "ctx_ready", "qm_done", "q_hi", "q_ready", "k_done", "k_hi", "k_ready", "v_done", "v_ready", "xb_ready",
                 "scores_done", "max_ready", "prob_ready", "pt_done", "pt_ready", "pv_done", "inv_ready",
                 "wide_ready", "lt_done", "lt_ready", "ot_ready", "out_done", "x_ready")
        (loaded, cleared, w_loaded, w_ready, ctx_hi, ctx_ready, qm_done, q_hi, q_ready, k_done, k_hi, k_ready, v_done, v_ready,
         xb_ready, scores_done, max_ready, prob_ready,
         pt_done, pt_ready, pv_done, inv_ready, wide_ready, lt_done, lt_ready, ot_ready, out_done, x_ready) = (
            m.sem(n) for n in names)
        ctx_loaded = [m.sem(f"ctx_loaded{j}") for j in range(2)]
        loads = [(wo, wo_dram), (hmask, hmask_dram)]
        if bk_dram is not None:
            loads += [(bk, bk_dram), (bv, bv_dram.partition_broadcast(P))]
        loads.append((bo, bo_dram.partition_broadcast(S)))
        LOADED = 16 * len(loads)
        CLEARED = 9

        def has_prev(b):
            return not (isinstance(b, int) and b == 0)

        def has_cur(b):
            return not (isinstance(b, int) and b >= NB)

        def has_next(b):
            return not (isinstance(b, int) and b >= NB - 1)

        def has_next2(b):
            return not (isinstance(b, int) and b >= NB - 2)

        def lagged(b, h, lag):
            if h >= lag:
                return b, h - lag, has_cur(b)
            return b - 1, H + h - lag, has_prev(b)

        def other(half, p):
            return half + p

        def vm_slots(p, kc):
            a = vm[p][:, kc, :]
            return bass.AP(a.tensor, a.offset, [list(a.ap[0]), [HPC * P, nch], [P + dk, HPC], [1, dk]])

        block = ctx.enter_context(nc.Block())

        @block.sync
        def _(sp):
            def load_ctx(b, p):
                sp.dma_start(ctx_t[p][:, :, 0:NK],
                             ctx_dram[ds(b, 1)].rearrange("o p c s -> p (o c) s")).then_inc(ctx_loaded[p], 16)
            sp.dma_start(w_raw[:, :, :], wk_dram).then_inc(w_loaded, 16)
            load_ctx(0, 0)
            for dst, src in loads:
                sp.dma_start(dst[tuple(slice(None) for _ in dst.shape)], src).then_inc(loaded, 16)
            load_ctx(1, 1)
            sp.wait_ge(w_ready, 2)
            sp.dma_start(w_raw[:, :, :], wv_dram).then_inc(w_loaded, 16)
            with nc.sync.Fori(0, NB // 2 - 1) as i:
                for p in range(2):
                    sp.wait_ge(ctx_ready, i * 2 + p + 1)
                    load_ctx(i * 2 + 2 + p, p)

        @block.gpsimd
        def _(pool):
            nc.gpsimd.memset(vm[1][:, :, :], 0.0).then_inc(cleared, 1)
            nc.gpsimd.memset(ones[:, :, :], 1.0).then_inc(cleared, 1)
            pool.wait_ge(cleared, CLEARED)
            pool.wait_ge(loaded, LOADED)

            def spread_q(b, p):
                if not isinstance(b, int) or b >= 1:
                    pool.wait_ge(q_hi, b)
                    pool.wait_ge(q_ready, b)
                for c in range(nch):
                    ins = nc.gpsimd.tensor_tensor(
                        qm[:, c * HPC:(c + 1) * HPC, :],
                        q_t[:, c, ds(b * S, S)].unsqueeze(1).to_broadcast([P, HPC, S]),
                        hmask[:, :].unsqueeze(2).to_broadcast([P, HPC, S]), ALU.mult)
                ins.then_inc(qm_done, 1)
                pool.wait_ge(q_hi, b + 1)
                nc.gpsimd.tensor_tensor(qs[p][1][:, :, :], qm[:, :, :], qs[p][0][:, :, :].bitcast(F32),
                                        ALU.subtract).then_inc(q_ready, 1)

            def split_ctx(b, p):
                pool.wait_ge(ctx_hi, b + 1)
                nc.gpsimd.tensor_tensor(ctx_s[p][1][:, :, :], ctx_t[p][:, :, :], ctx_s[p][0][:, :, :].bitcast(F32),
                                        ALU.subtract).then_inc(ctx_ready, 1)

            def add_bo(b):
                xb = x[:, ds(b, 1), :].rearrange("p o d -> p (o d)")
                nc.gpsimd.tensor_tensor(xb, xb, bo[:, :], ALU.add).then_inc(xb_ready, 1)

            def widen_inv(b):
                pool.wait_ge(inv_ready, b)
                if not (isinstance(b, int) and b == 1):
                    pool.wait_ge(lt_done, b - 1)
                nc.gpsimd.tensor_tensor(inv_wide[:, :, :], row_inv[:, :].unsqueeze(2).to_broadcast([S, H, dk]),
                                        ones[:, :, :].to_broadcast([S, H, dk]), ALU.mult).then_inc(wide_ready, 1)

            def split_w(w_s, n):
                pool.wait_ge(w_ready, 2 * n + 1)
                nc.gpsimd.tensor_tensor(w_s[1][:, :, :], w_raw[:, :, :], w_s[0][:, :, :].bitcast(F32),
                                        ALU.subtract).then_inc(w_ready, 1)
            split_w(wk_s, 0)
            split_ctx(0, 0)
            split_w(wv_s, 1)
            spread_q(0, 0)
            split_ctx(1, 1)

            def batch(b, half, p):
                if has_prev(b):
                    widen_inv(b)
                add_bo(b)
                if has_next(b):
                    if has_prev(b):
                        pool.wait_ge(scores_done, b * H)
                    spread_q(b + 1, 1 - p)
                if has_next2(b):
                    split_ctx(b + 2, p)
            peeled(nc.gpsimd, NB, batch)
            widen_inv(NB)

        @block.vector
        def _(dve):
            for j in range(2):
                nc.vector.memset(ctx_t[j][:, :, NK:NKP], 0.0).then_inc(cleared, 1)
            for j in range(4):
                nc.vector.memset(prob[j][:, NK:NKP], 0.0).then_inc(cleared, 1)
            nc.vector.memset(vm[0][:, :, :], 0.0).then_inc(cleared, 1)
            dve.wait_ge(cleared, CLEARED)
            dve.wait_ge(loaded, LOADED)

            def evac_v(b, p, kc):
                dve.wait_ge(v_done, b * KC + kc + 1)
                bank = ps_x[next(k for _, kind, i, k in tasks if kind == "V" and i == kc)]
                src = bank[:, 0:nch * P].rearrange("p (c j d) -> p c j d", c=nch, j=HPC)
                if bv_dram is not None:
                    ins = nc.vector.tensor_tensor(vm_slots(p, kc), src,
                                                  bv[:, :].rearrange("p (c j d) -> p c j d", c=nch, j=HPC), ALU.add)
                else:
                    ins = nc.vector.tensor_copy(vm_slots(p, kc), src)
                ins.then_inc(v_ready, 1)

            def evac_k(b, p, c):
                dve.wait_ge(k_hi, b * nch + c + 1)
                bank = ps_x[next(k for _, kind, i, k in tasks if kind == "K" and i == c)]
                high = kt[p][0][:, c, :].bitcast(F32)
                if bk_dram is not None:
                    ins = nc.vector.scalar_tensor_tensor(kt[p][1][:, c, :], bank[:, 0:NKE], bk[:, c:c + 1], high,
                                                         ALU.add, ALU.subtract)
                else:
                    ins = nc.vector.tensor_tensor(kt[p][1][:, c, :], bank[:, 0:NKE], high, ALU.subtract)
                ins.then_inc(k_ready, 1)

            for n, (_, kind, i, _) in enumerate(tasks):
                if kind == "K":
                    evac_k(0, 0, i)
                elif kind == "V":
                    evac_v(0, 0, i)

            def step(b, half, p, h):
                g = b * H + h
                if has_cur(b):
                    dve.wait_ge(scores_done, g + 1)
                    nc.vector.tensor_reduce(neg_max[:, p, h:h + 1], ps_s[h % 2][0:S, 0:NK], AX.X, ALU.max,
                                            negate=True).then_inc(max_ready, 1)
                bt, ht, exists = lagged(b, h, TRANSPOSE_LAG)
                if exists:
                    gt = bt * H + ht
                    dve.wait_ge(pt_done, gt + 1)
                    if not isinstance(gt, int) or gt >= 4:
                        dve.wait_ge(pv_done, gt - 3)
                    nc.vector.tensor_copy(prob_t[ht % 4][:, :], ps_p[ht % 2][:, 0:KC * S]).then_inc(pt_ready, 1)
                if has_prev(b) and h == 2:
                    dve.wait_ge(prob_ready, b * H)
                    if not (isinstance(b, int) and b == 1):
                        dve.wait_ge(wide_ready, b - 1)
                    nc.vector.reciprocal(row_inv[:, :], row_sum[:, 1 - p, :]).then_inc(inv_ready, 1)
                if has_prev(b) and h == LT_STEP + 1:
                    dve.wait_ge(pv_done, b * H)
                    dve.wait_ge(lt_ready, b)
                    if not (isinstance(b, int) and b == 1):
                        dve.wait_ge(out_done, b - 1)
                    nc.vector.tensor_tensor(o_t[:, :, :].rearrange("p c s -> p (c s)"), ps_o[1 - p][:, 0:nch * S],
                                            inv_t[:, :], ALU.mult).then_inc(ot_ready, 1)
                if has_next(b):
                    for s, kind, i, _ in tasks:
                        if s == h and kind == "K":
                            evac_k(b + 1, 1 - p, i)
                        if s == h and kind == "V":
                            if has_prev(b):
                                dve.wait_ge(pv_done, b * H)
                            evac_v(b + 1, 1 - p, i)
                if has_prev(b) and h == OP_STEP:
                    dve.wait_ge(out_done, b)
                    dve.wait_ge(xb_ready, b)
                    xb = x[:, ds(b - 1, 1), :].rearrange("p o d -> p (o d)")
                    bank = ps_x[next(k for _, kind, _, k in tasks if kind == "OP")]
                    nc.vector.tensor_tensor(xb, bank[0:S, 0:D], xb, ALU.add).then_inc(x_ready, 1)

            def batch(b, half, p):
                for h in range(H):
                    step(b, half, p, h)
            peeled(nc.vector, NB, batch)
            for h in range(OP_STEP + 1):
                step(NB, NB // 2, 0, h)

        @block.scalar
        def _(act):
            act.wait_ge(loaded, LOADED)
            act.wait_ge(cleared, CLEARED)

            def evac_k(b, p, c):
                act.wait_ge(k_done, b * nch + c + 1)
                bank = ps_x[next(k for _, kind, i, k in tasks if kind == "K" and i == c)]
                if bk_dram is not None:
                    ins = nc.scalar.activation(kt[p][0][:, c, :], bank[:, 0:NKE], ACT.Identity, bias=bk[:, c:c + 1])
                else:
                    ins = nc.scalar.copy(kt[p][0][:, c, :], bank[:, 0:NKE])
                ins.then_inc(k_hi, 1)

            def split_ctx(b, half, p):
                act.wait_ge(ctx_loaded[p], half * 16 + 16)
                if not isinstance(b, int) or b >= 2:
                    act.wait_ge(v_done, (b - 1) * KC)
                nc.scalar.copy(ctx_s[p][0][:, :, :], ctx_t[p][:, :, :]).then_inc(ctx_hi, 1)

            def split_q(b, p):
                act.wait_ge(qm_done, b + 1)
                nc.scalar.copy(qs[p][0][:, :, :], qm[:, :, :]).then_inc(q_hi, 1)

            def split_w(w_s, n):
                act.wait_ge(w_loaded, 16 * n + 16)
                nc.scalar.copy(w_s[0][:, :, :], w_raw[:, :, :]).then_inc(w_ready, 1)
            split_w(wk_s, 0)
            split_ctx(0, 0, 0)
            split_w(wv_s, 1)
            split_q(0, 0)
            split_ctx(1, 0, 1)
            for c in range(nch):
                evac_k(0, 0, c)

            def step(b, half, p, h):
                g = b * H + h
                if has_cur(b):
                    act.wait_ge(max_ready, g + 1)
                    if not isinstance(g, int) or g >= 4:
                        act.wait_ge(pt_done, g - 3)
                    if h == 0 and not (isinstance(b, int) and b < 2):
                        act.wait_ge(inv_ready, b - 1)
                    nc.scalar.activation(prob[h % 4][:, 0:NK], ps_s[h % 2][0:S, 0:NK], ACT.Exp,
                                         bias=neg_max[:, p, h:h + 1],
                                         accum_out=row_sum[:, p, h:h + 1]).then_inc(prob_ready, 1)
                if has_prev(b) and h == LT_STEP:
                    act.wait_ge(lt_done, b)
                    if not (isinstance(b, int) and b == 1):
                        act.wait_ge(ot_ready, b - 1)
                    bank = ps_x[next(k for _, kind, _, k in tasks if kind == "LT")]
                    nc.scalar.copy(inv_t[:, :], bank[:, 0:nch * S]).then_inc(lt_ready, 1)
                if has_next(b):
                    for s, kind, i, _ in tasks:
                        if s == h and kind == "K":
                            evac_k(b + 1, 1 - p, i)
                    if h == H // 2:
                        split_q(b + 1, 1 - p)
                if has_next2(b) and h == H - 3:
                    split_ctx(b + 2, half + 1, p)

            def batch(b, half, p):
                for h in range(H):
                    step(b, half, p, h)
            peeled(nc.scalar, NB, batch)
            for h in range(LT_STEP + 1):
                step(NB, NB // 2, 0, h)

        @block.tensor
        def _(pe):
            def evacuated(kind, i, b):
                return {"K": (k_ready, (b + 1) * nch + i + 1), "V": (v_ready, (b + 1) * KC + i + 1),
                        "LT": (lt_ready, b), "OP": (x_ready, b)}[kind]

            def bank_free(n, b):
                at, bb = n, b
                while True:
                    at -= 1
                    if at < 0:
                        at, bb = len(tasks) - 1, bb - 1
                        if isinstance(bb, int) and bb < -1:
                            return
                    _, kind, i, bank = tasks[at]
                    exists = has_next(bb) if kind in "KV" else has_prev(bb) and not (isinstance(bb, int) and bb < 0)
                    if exists and bank == tasks[n][3]:
                        pe.wait_ge(*evacuated(kind, i, bb))
                        return

            def project_k(b, half, p, c, bank):
                if c == 0:
                    pe.wait_ge(ctx_ready, b + 1)
                for k in range(DC):
                    ins = split_product(nc, bank[:, 0:NKE], [w[:, k, c * P:(c + 1) * P] for w in wk_s],
                                        [t[:, k, 0:NKE] for t in ctx_s[p]], k == 0, k == DC - 1)
                ins.then_inc(k_done, 1)

            def project_v(p, kc, bank):
                for k in range(DC):
                    ins = split_product(nc, bank[:, 0:nch * P], [t[:, k, kc * P:(kc + 1) * P] for t in ctx_s[p]],
                                        [w[:, k, :] for w in wv_s], k == 0, k == DC - 1)
                ins.then_inc(v_done, 1)

            def side(n, b, half, p):
                _, kind, i, bank_at = tasks[n]
                bank = ps_x[bank_at]
                if kind in "KV":
                    if not has_next(b):
                        return
                    bank_free(n, b)
                    if kind == "K":
                        project_k(b + 1, other(half, p), 1 - p, i, bank)
                    else:
                        project_v(1 - p, i, bank)
                    return
                if not has_prev(b):
                    return
                bank_free(n, b)
                if kind == "LT":
                    pe.wait_ge(wide_ready, b)
                    for c in range(nch):
                        ins = nc.tensor.transpose(
                            bank[:, c * S:(c + 1) * S],
                            inv_wide[:, c * HPC:(c + 1) * HPC, :].rearrange("p h d -> p (h d)"), ident[0:S, 0:S])
                    ins.then_inc(lt_done, 1)
                else:
                    pe.wait_ge(ot_ready, b)
                    for c in range(nch):
                        ins = nc.tensor.matmul(bank[0:S, 0:D], o_t[:, c, :], wo[:, c, :], start=(c == 0),
                                               stop=(c == nch - 1))
                    ins.then_inc(out_done, 1)

            def step(b, half, p, h):
                g = b * H + h
                if has_cur(b):
                    if h == 0:
                        pe.wait_ge(k_ready, b * nch + nch)
                        pe.wait_ge(q_ready, b + 1)
                    if not isinstance(g, int) or g >= 2:
                        pe.wait_ge(prob_ready, g - 1)
                    split_product(nc, ps_s[h % 2][0:S, 0:NKE], [q[:, h, :] for q in qs[p]],
                                  [k[:, h // HPC, :] for k in kt[p]], True, True).then_inc(scores_done, 1)
                bv_, hv, exists = lagged(b, h, PV_LAG)
                if exists:
                    gv, pv = bv_ * H + hv, p if h >= PV_LAG else 1 - p
                    if hv == 0:
                        pe.wait_ge(v_ready, bv_ * KC + KC)
                        if not (isinstance(bv_, int) and bv_ < 2):
                            pe.wait_ge(ot_ready, bv_ - 1)
                    pe.wait_ge(pt_ready, gv + 1)
                    c, j = divmod(hv, HPC)
                    for kc in range(KC):
                        ins = nc.tensor.matmul(ps_o[pv][:, c * S:(c + 1) * S], vm[pv][:, kc, hv * P:(hv + 1) * P],
                                               prob_t[hv % 4][:, kc * S:(kc + 1) * S], start=(j == 0 and kc == 0),
                                               stop=(j == HPC - 1 and kc == KC - 1))
                    ins.then_inc(pv_done, 1)
                for n, t in enumerate(tasks):
                    if t[0] == h:
                        side(n, b, half, p)
                bt, ht, exists = lagged(b, h, TRANSPOSE_LAG)
                if exists:
                    gt = bt * H + ht
                    pe.wait_ge(prob_ready, gt + 1)
                    if not isinstance(gt, int) or gt >= 2:
                        pe.wait_ge(pt_ready, gt - 1)
                    for kc in range(KC):
                        ins = nc.tensor.transpose(ps_p[ht % 2][:, kc * S:(kc + 1) * S],
                                                  prob[ht % 4][:, kc * P:(kc + 1) * P], ident[0:S, 0:S])
                    ins.then_inc(pt_done, 1)

            pe.wait_ge(loaded, LOADED)
            pe.wait_ge(cleared, CLEARED)
            pe.wait_ge(w_ready, 4)
            for n, (_, kind, i, bank) in enumerate(tasks):
                if kind in "KV":
                    bank_free(n, -1)
                    if kind == "K":
                        project_k(0, 0, 0, i, ps_x[bank])
                    else:
                        project_v(0, i, ps_x[bank])

            def batch(b, half, p):
                for h in range(H):
                    step(b, half, p, h)
            peeled(nc.tensor, NB, batch)
            for h in range(OP_STEP + 1):
                step(NB, NB // 2, 0, h)


def norm_chain(nc, dve, x_of, n, stats, mv, sd, stats_done, var_ready, var_before, rows=S):
    with nc.vector.Fori(0, n) as b:
        nc.vector.bn_stats(stats[:, ds(b, 1), :].rearrange("p o s -> p (o s)"), x_of(b)).then_inc(stats_done, 1)
    base = var_before * (n + 1)
    dve.wait_ge(stats_done, base + n)
    for b in range(n):
        last = nc.vector.bn_aggr(mv[:, b, :], stats[:, b, :])
    last.then_inc(stats_done, 1)
    dve.wait_ge(stats_done, base + n + 1)
    nc.vector.tensor_scalar_add(sd[:, :], mv[:, :, 1], EPS).then_inc(var_ready, 1)


def route_block(nc, x, alpha, slot, tile_expert, ident, xs_dram, cent_dram, tri_dram, prio_dram, starts_dram):
    with ExitStack() as ctx:
        m = Memory(nc, ctx, "rt")
        zero = m.sb("zero", [P, SLOTS // P // 4, D])
        cent = m.sb("cent", [P, DC, E0])
        tri = m.sb("tri", [S, S])
        prio = m.sb("prio", [S, E0])
        starts = m.sb("starts", [1, N_ST])
        ones = m.sb("ones", [S, P])
        f = m.sb("f", [S, NB, D])
        fs = [m.sb(f"fs{j}", [S, D]) for j in range(2)]
        ft = [m.sb(f"ft{j}", [P, DC, S]) for j in range(2)]
        stats = m.sb("stats", [S, NB, 6])
        mv = m.sb("mv", [S, NB, 2])
        sd = m.sb("sd", [S, NB])
        rstd = m.sb("rstd", [S, NB])
        aff = m.sb("aff", [S, NB, E0])
        best = m.sb("best", [S, NB])
        hot = m.sb("hot", [S, NB, E0])
        rank = m.sb("rank", [S, NB, E0])
        total = m.sb("total", [S, E0, NB])
        before = m.sb("before", [S, E0, NB])
        count = m.sb("count", [S, E0])
        count_i = m.sb("count_i", [S, E0], I32)
        padded = m.sb("padded", [S, E0])
        end = m.sb("end", [S, E0])
        base = m.sb("base", [S, E0])
        slot_f = m.sb("slot_f", [S, NB])
        past = m.sb("past", [1, N_ST, E0])
        te_f = m.sb("te_f", [1, N_ST])
        ps_t = [m.ps(f"ps_t{j}") for j in range(2)]
        ps_a = [m.ps(f"ps_a{j}") for j in range(2)]
        ps_rank, ps_total = m.ps("ps_rank"), m.ps("ps_total")
        names = ("loaded", "zero_set", "zeroed", "stats_done", "var_ready", "sd_ready", "f_ready", "x_ready", "fs_ready",
                 "t_done", "ft_ready", "aff_done", "aff_ready", "chain", "best_ready", "hot_ready", "counted",
                 "slot_ready", "xh_ready", "scattered", "ones_set")
        (loaded, zero_set, zeroed, stats_done, var_ready, sd_ready, f_ready, x_ready, fs_ready, t_done, ft_ready,
         aff_done, aff_ready, chain, best_ready, hot_ready, counted, slot_ready, xh_ready, scattered, ones_set) = (
            m.sem(n) for n in names)
        block = ctx.enter_context(nc.Block())

        def one(t, b):
            return t[:, ds(b, 1), :].rearrange("p o d -> p (o d)")

        @block.sync
        def _(sp):
            sp.dma_start(cent[:, :, :], cent_dram).then_inc(loaded, 16)
            sp.dma_start(tri[:, :], tri_dram).then_inc(loaded, 16)
            sp.dma_start(prio[:, :], prio_dram.partition_broadcast(S)).then_inc(loaded, 16)
            sp.dma_start(starts[:, :], starts_dram.rearrange("(o n) -> o n", o=1)).then_inc(loaded, 16)
            sp.wait_ge(zero_set, 1)
            zv = xs_dram.rearrange("(q p r) d -> q p (r d)", q=4, p=P)
            for k in range(4):
                sp.dma_start(zv[k], zero[:, :, :].rearrange("p r d -> p (r d)")).then_inc(zeroed, 16)

        @block.gpsimd
        def _(pool):
            nc.gpsimd.memset(zero[:, :, :], 0.0).then_inc(zero_set, 1)
            with nc.gpsimd.Fori(0, NB) as b:
                pool.wait_ge(f_ready, b + 1)
                nc.gpsimd.tensor_tensor(one(x, b), one(x, b), one(f, b), ALU.add).then_inc(x_ready, 1)
            pool.wait_ge(zeroed, 64)
            pool.wait_ge(slot_ready, 1)
            pool.wait_ge(xh_ready, NB)
            for b in range(NB):
                nc.gpsimd.indirect_dma_start(
                    out=xs_dram, out_offset=bass.IndirectOffsetOnAxis(ap=slot[:, b:b + 1], axis=0),
                    in_=f[:, b, :], in_offset=None, bounds_check=SLOTS - 1).then_inc(scattered, 16)
            pool.wait_ge(scattered, 16 * NB)

        @block.vector
        def _(dve):
            links = [0]

            def link(ins):
                links[0] += 1
                ins.then_inc(chain, 1)
                dve.wait_ge(chain, links[0])

            nc.vector.memset(ones[:, :], 1.0).then_inc(ones_set, 1)
            norm_chain(nc, dve, lambda b: one(x, b), NB, stats, mv, sd, stats_done, var_ready, 0)
            dve.wait_ge(sd_ready, 1)
            link(nc.vector.reciprocal(rstd[:, :], sd[:, :]))
            with nc.vector.Fori(0, NB) as b:
                nc.vector.tensor_scalar(one(f, b), one(x, b), one(mv, b)[:, 0:1], rstd[:, ds(b, 1)],
                                        ALU.subtract, ALU.mult).then_inc(f_ready, 1)
            dve.wait_ge(f_ready, NB)
            norm_chain(nc, dve, lambda b: one(f, b), NB, stats, mv, sd, stats_done, var_ready, 1)

            def affinity(b, half, p):
                dve.wait_ge(aff_done, b + 1)
                nc.vector.tensor_copy(one(aff, b), ps_a[p][0:S, 0:E0]).then_inc(aff_ready, 1)
            peeled(nc.vector, NB, affinity)
            dve.wait_ge(aff_ready, NB)
            dve.wait_ge(loaded, 64)
            nc.vector.tensor_reduce(best[:, :], aff[:, :, :], AX.X, ALU.max).then_inc(best_ready, 1)
            dve.wait_ge(best_ready, 1)
            link(nc.vector.tensor_tensor(hot[:, :, :], aff[:, :, :],
                                         best[:, :].unsqueeze(2).to_broadcast([S, NB, E0]), ALU.is_equal))
            link(nc.vector.tensor_tensor(aff[:, :, :], hot[:, :, :],
                                         prio[:, :].unsqueeze(1).to_broadcast([S, NB, E0]), ALU.mult))
            link(nc.vector.tensor_reduce(slot_f[:, :], aff[:, :, :], AX.X, ALU.max))
            nc.vector.tensor_tensor(hot[:, :, :], aff[:, :, :],
                                    slot_f[:, :].unsqueeze(2).to_broadcast([S, NB, E0]),
                                    ALU.is_equal).then_inc(hot_ready, 1)
            dve.wait_ge(sd_ready, 2)
            link(nc.vector.reciprocal(rstd[:, :], sd[:, :]))
            dve.wait_ge(x_ready, NB)
            dve.wait_ge(fs_ready, NB)
            with nc.vector.Fori(0, NB) as b:
                nc.vector.tensor_scalar(one(f, b), one(f, b), one(mv, b)[:, 0:1], rstd[:, ds(b, 1)],
                                        ALU.subtract, ALU.mult).then_inc(xh_ready, 1)
            dve.wait_ge(counted, 2)
            link(nc.vector.tensor_copy(rank[:, :, :].rearrange("p b e -> p (b e)"), ps_rank[0:S, 0:NB * E0]))
            link(nc.vector.tensor_copy(total[:, :, :].rearrange("p e b -> p b e"),
                                       ps_total[0:S, 0:NB * E0].rearrange("p (b e) -> p b e", e=E0)))
            for e in range(E0):
                ins = nc.vector.tensor_tensor_scan(before[:, e, :], ones[:, 0:NB], total[:, e, :], 0.0, ALU.mult,
                                                   ALU.add)
            link(ins)
            link(nc.vector.tensor_scalar_add(count[:, :], before[:, :, NB - 1], float(SLOT_TILE - 1)))
            link(nc.vector.tensor_copy(count_i[:, :], count[:, :]))
            link(nc.vector.tensor_scalar(count_i[:, :], count_i[:, :], SLOT_SHIFT, SLOT_SHIFT,
                                         ALU.logical_shift_right, ALU.logical_shift_left))
            link(nc.vector.tensor_copy(padded[:, :], count_i[:, :]))
            link(nc.vector.tensor_tensor_scan(end[:, :], ones[:, 0:E0], padded[:, :], 0.0, ALU.mult, ALU.add))
            link(nc.vector.tensor_tensor(base[:, :], end[:, :], padded[:, :], ALU.subtract))
            link(nc.vector.tensor_tensor(before[:, :, :], before[:, :, :], total[:, :, :], ALU.subtract))
            link(nc.vector.tensor_tensor(before[:, :, :], before[:, :, :],
                                         base[:, :].unsqueeze(2).to_broadcast([S, E0, NB]), ALU.add))
            link(nc.vector.tensor_tensor(rank[:, :, :], rank[:, :, :],
                                         before[:, :, :].rearrange("p e b -> p b e"), ALU.add))
            link(nc.vector.tensor_tensor(rank[:, :, :], rank[:, :, :], hot[:, :, :], ALU.mult))
            link(nc.vector.tensor_reduce(slot_f[:, :], rank[:, :, :], AX.X, ALU.add))
            nc.vector.tensor_copy(slot[:, :], slot_f[:, :]).then_inc(slot_ready, 1)
            link(nc.vector.tensor_tensor(past[:, :, :], end[0:1, :].unsqueeze(1).to_broadcast([1, N_ST, E0]),
                                         starts[:, :].unsqueeze(2).to_broadcast([1, N_ST, E0]), ALU.is_le))
            link(nc.vector.tensor_reduce(te_f[:, :], past[:, :, :], AX.X, ALU.add))
            link(nc.vector.tensor_scalar_min(te_f[:, :], te_f[:, :], float(E0 - 1)))
            link(nc.vector.tensor_copy(tile_expert[:, :], te_f[:, :]))

        @block.scalar
        def _(act):
            for k in range(2):
                act.wait_ge(var_ready, k + 1)
                nc.scalar.activation(sd[:, :], sd[:, :], ACT.Sqrt).then_inc(sd_ready, 1)
                if k:
                    break

                def step(b, half, p):
                    act.wait_ge(f_ready, b + 1)
                    if not isinstance(b, int) or b >= 2:
                        act.wait_ge(t_done, b - 1)
                    nc.scalar.copy(fs[p][:, :], one(f, b)).then_inc(fs_ready, 1)
                    act.wait_ge(t_done, b + 1)
                    if not isinstance(b, int) or b >= 2:
                        act.wait_ge(aff_done, b - 1)
                    nc.scalar.copy(ft[p][:, :, :].rearrange("p c s -> p (c s)"),
                                   ps_t[p][:, 0:DC * S]).then_inc(ft_ready, 1)
                peeled(nc.scalar, NB, step)
            act.wait_ge(best_ready, 1)
            nc.scalar.activation(alpha[:, :], best[:, :], ACT.Sigmoid)

        @block.tensor
        def _(pe):
            pe.wait_ge(loaded, 64)

            def affinity(b, p):
                pe.wait_ge(ft_ready, b + 1)
                if not isinstance(b, int) or b >= 2:
                    pe.wait_ge(aff_ready, b - 1)
                for c in range(DC):
                    ins = nc.tensor.matmul(ps_a[p][0:S, 0:E0], ft[p][:, c, :], cent[:, c, :], start=(c == 0),
                                           stop=(c == DC - 1))
                ins.then_inc(aff_done, 1)

            def step(b, half, p):
                pe.wait_ge(fs_ready, b + 1)
                if not isinstance(b, int) or b >= 2:
                    pe.wait_ge(ft_ready, b - 1)
                for c in range(DC):
                    ins = nc.tensor.transpose(ps_t[p][:, c * S:(c + 1) * S], fs[p][:, c * P:(c + 1) * P],
                                              ident[0:S, 0:S])
                ins.then_inc(t_done, 1)
                affinity(b, p)
            peeled(nc.tensor, NB, step)
            pe.wait_ge(hot_ready, 1)
            pe.wait_ge(ones_set, 1)
            hot_flat = hot[:, :, :].rearrange("p b e -> p (b e)")
            nc.tensor.matmul(ps_rank[0:S, 0:NB * E0], tri[:, :], hot_flat, start=True, stop=True).then_inc(counted, 1)
            nc.tensor.matmul(ps_total[0:S, 0:NB * E0], ones[:, 0:S], hot_flat, start=True,
                             stop=True).then_inc(counted, 1)


def experts0_block(nc, tile_expert, ident, xs_dram, ys_dram, w1_dram, w2_dram, affine_dram, b2_dram):
    H2 = SLOT_TILE // P
    with ExitStack() as ctx:
        m = Memory(nc, ctx, "e0")
        two = range(2)
        xs = [m.sb(f"xs{j}", [P, H2, D]) for j in two]
        w1 = [m.sb(f"w1{j}", [P, DC, F0]) for j in two]
        w2 = [m.sb(f"w2{j}", [P, FC, D]) for j in two]
        affine = [m.sb(f"affine{j}", [P, FC + 2 * DC]) for j in two]
        b2 = [m.sb(f"b2{j}", [P, D]) for j in two]
        h_t = [m.sb(f"h_t{j}", [P, DC, SLOT_TILE]) for j in two]
        hid = [m.sb(f"hid{j}", [P, FC, SLOT_TILE]) for j in two]
        y = [m.sb(f"y{j}", [P, H2, D]) for j in two]
        ps_t = [m.ps(f"ps_t{j}") for j in two]
        ps_u = [m.ps(f"ps_u{j}") for j in range(4)]
        ps_y = [m.ps(f"ps_y{j}") for j in range(H2)]
        UG = FC // 4
        (t_done, h_ready, u_done, hid_ready, y_done, y_ready) = (
            m.sem(n) for n in ("t_done", "h_ready", "u_done", "hid_ready", "y_done", "y_ready"))
        xs_loaded = [m.sem(f"xs_loaded{j}") for j in two]
        w1_loaded = [m.sem(f"w1_loaded{j}") for j in two]
        w2_loaded = [m.sem(f"w2_loaded{j}") for j in two]
        stored = [m.sem(f"stored{j}") for j in two]
        block = ctx.enter_context(nc.Block())

        def later(j, n):
            return not isinstance(j, int) or j >= n

        @block.sync
        def _(sp):
            def load(j, half, p):
                if later(j, 2):
                    sp.wait_ge(y_ready, (j - 1) * H2)
                e = nc.sync.value_load(tile_expert[0:1, ds(j, 1)], min_val=0, max_val=E0 - 1)
                sp.dma_start(xs[p][:, :, :], xs_dram[ds(j * SLOT_TILE, SLOT_TILE), :].rearrange(
                    "(s p) d -> p s d", p=P)).then_inc(xs_loaded[p], 16)
                sp.dma_start(affine[p][:, :], affine_dram[ds(e, 1)].rearrange("o p n -> p (o n)")
                             ).then_inc(xs_loaded[p], 16)
                sp.dma_start(w1[p][:, :, :], w1_dram[ds(e, 1)].rearrange("o p c n -> p (o c) n")
                             ).then_inc(w1_loaded[p], 16)
                sp.dma_start(w2[p][:, :, :], w2_dram[ds(e, 1)].rearrange("o p c n -> p (o c) n")
                             ).then_inc(w2_loaded[p], 16)
                sp.dma_start(b2[p][:, :], b2_dram[ds(e, 1), :].rearrange("o d -> (o d)").partition_broadcast(P)
                             ).then_inc(w2_loaded[p], 16)
            peeled(nc.sync, N_ST, load)

        @block.gpsimd
        def _(pool):
            def store(j, half, p):
                pool.wait_ge(y_ready, (j + 1) * H2)
                pool.dma_start(ys_dram[ds(j * SLOT_TILE, SLOT_TILE), :].rearrange("(s p) d -> p s d", p=P),
                               y[p][:, :, :]).then_inc(stored[p], 16)
            peeled(nc.gpsimd, N_ST, store)
            for p in two:
                pool.wait_ge(stored[p], 16 * N_ST // 2)

        @block.vector
        def _(dve):
            def scale_in(j, half, p):
                dve.wait_ge(t_done, j + 1)
                if later(j, 2):
                    dve.wait_ge(u_done, (j - 1) * 4)
                for c in range(DC):
                    ins = nc.vector.tensor_scalar(h_t[p][:, c, :], ps_t[p][:, c * SLOT_TILE:(c + 1) * SLOT_TILE],
                                                  affine[p][:, FC + c:FC + c + 1],
                                                  affine[p][:, FC + DC + c:FC + DC + c + 1], ALU.mult, ALU.add)
                ins.then_inc(h_ready, 1)

            def tile(j, half, p):
                if not isinstance(j, int) or j < N_ST - 1:
                    scale_in(j + 1, half + p, 1 - p)
                if later(j, 2) or not isinstance(j, int):
                    dve.wait_ge(stored[p], half * 16)
                for s in range(H2):
                    dve.wait_ge(y_done, j * H2 + s + 1)
                    nc.vector.tensor_tensor(y[p][:, s, :], ps_y[s][:, 0:D], b2[p][:, :], ALU.add).then_inc(y_ready, 1)
            scale_in(0, 0, 0)
            peeled(nc.vector, N_ST, tile)

        @block.scalar
        def _(act):
            def tile(j, half, p):
                if later(j, 2):
                    act.wait_ge(y_done, (j - 1) * H2)
                for fc in range(FC):
                    act.wait_ge(u_done, j * 4 + fc // UG + 1)
                    o = fc % UG * SLOT_TILE
                    nc.scalar.activation(hid[p][:, fc, :], ps_u[fc // UG][:, o:o + SLOT_TILE], ACT.Relu,
                                         bias=affine[p][:, fc:fc + 1]).then_inc(hid_ready, 1)
            peeled(nc.scalar, N_ST, tile)

        @block.tensor
        def _(pe):
            def transposes(j, half, p):
                pe.wait_ge(xs_loaded[p], half * 32 + 32)
                if later(j, 2):
                    pe.wait_ge(h_ready, j - 1)
                for c in range(DC):
                    for s in range(H2):
                        o = c * SLOT_TILE + s * P
                        ins = nc.tensor.transpose(ps_t[p][:, o:o + P], xs[p][:, s, c * P:(c + 1) * P], ident[:, :])
                ins.then_inc(t_done, 1)

            def tile(j, half, p):
                pe.wait_ge(h_ready, j + 1)
                pe.wait_ge(w1_loaded[p], half * 16 + 16)
                for g in range(4):
                    if later(j, 1):
                        pe.wait_ge(hid_ready, j * FC + (g + 1 - 4) * UG)
                    for fc in range(g * UG, (g + 1) * UG):
                        o = fc % UG * SLOT_TILE
                        for c in range(DC):
                            ins = nc.tensor.matmul(ps_u[g][:, o:o + SLOT_TILE], w1[p][:, c, fc * P:(fc + 1) * P],
                                                   h_t[p][:, c, :], start=(c == 0), stop=(c == DC - 1))
                    ins.then_inc(u_done, 1)
                if not isinstance(j, int) or j < N_ST - 1:
                    transposes(j + 1, half + p, 1 - p)
                pe.wait_ge(hid_ready, (j + 1) * FC)
                pe.wait_ge(w2_loaded[p], half * 32 + 32)
                for s in range(H2):
                    if later(j, 1):
                        pe.wait_ge(y_ready, j * H2 + s + 1 - H2)
                    for fc in range(FC):
                        ins = nc.tensor.matmul(ps_y[s][:, 0:D], hid[p][:, fc, s * P:(s + 1) * P], w2[p][:, fc, :],
                                               start=(fc == 0), stop=(fc == FC - 1))
                    ins.then_inc(y_done, 1)
            transposes(0, 0, 0)
            peeled(nc.tensor, N_ST, tile)


def combine_block(nc, x, alpha, slot, ys_dram):
    NG = 8
    with ExitStack() as ctx:
        m = Memory(nc, ctx, "cb")
        y = m.sb("y", [S, NB, D])
        gathered = [m.sem(f"gathered{j}") for j in range(NG)]
        block = ctx.enter_context(nc.Block())

        @block.gpsimd
        def _(pool):
            for b in range(NB):
                nc.gpsimd.indirect_dma_start(
                    out=y[:, b, :], out_offset=None, in_=ys_dram,
                    in_offset=bass.IndirectOffsetOnAxis(ap=slot[:, b:b + 1], axis=0),
                    bounds_check=SLOTS - 1).then_inc(gathered[b // (NB // NG)], 16)

        @block.vector
        def _(dve):
            for j in range(NG):
                dve.wait_ge(gathered[j], 16 * NB // NG)
                for b in range(j * NB // NG, (j + 1) * NB // NG):
                    nc.vector.scalar_tensor_tensor(x[:, b, :], y[:, b, :], alpha[:, b:b + 1], x[:, b, :], ALU.mult,
                                                   ALU.add)


def tokens_block(nc, x, acc, x_s, comb, ident, x3_dram, gate_dram, lower_dram):
    with ExitStack() as ctx:
        m = Memory(nc, ctx, "tk")
        gate = m.sb("gate", [P, DC, E1])
        lower = m.sb("lower", [P, G1 * G1])
        stats = m.sb("stats", [P, TT, 6])
        mv = m.sb("mv", [P, TT, 2])
        sd = m.sb("sd", [P, TT])
        rstd = m.sb("rstd", [P, TT])
        xn = [m.sb(f"xn{j}", [P, D]) for j in range(2)]
        xf = [m.sb(f"xf{j}", [P, DC, P]) for j in range(2)]
        logit = m.sb("logit", [P, TT, E1])
        score = m.sb("score", [P, TT, E1])
        group = m.sb("group", [P, TT, G1])
        more = m.sb("more", [P, TT, G1, G1])
        same = m.sb("same", [P, TT, G1, G1])
        g_rank = m.sb("g_rank", [P, TT, G1])
        g_sel = m.sb("g_sel", [P, TT, G1])
        top = m.sb("top", [P, TT, TOP_K])
        rest = m.sb("rest", [P, TT, E1])
        den = m.sb("den", [P, TT])
        den_inv = m.sb("den_inv", [P, TT])
        ps_t = [m.ps(f"ps_t{j}") for j in range(2)]
        ps_l = [m.ps(f"ps_l{j}") for j in range(2)]
        (saved, loaded, x_loaded, stats_done, var_ready, sd_ready, rstd_ready, xn_ready, t_done, xf_ready, high_ready,
         low_ready, l_done, l_ready, score_ready, chain) = (
            m.sem(n) for n in ("saved", "loaded", "x_loaded", "stats_done", "var_ready", "sd_ready", "rstd_ready",
                               "xn_ready", "t_done", "xf_ready", "high_ready", "low_ready", "l_done", "l_ready",
                               "score_ready", "chain"))
        block = ctx.enter_context(nc.Block())

        def one(t, k):
            return t[:, ds(k, 1), :].rearrange("p o d -> p (o d)")

        @block.sync
        def _(sp):
            sp.dma_start(x3_dram.rearrange("(b s) d -> s b d", s=S), x[:, :, :]).then_inc(saved, 16)
            sp.dma_start(gate[:, :, :], gate_dram).then_inc(loaded, 16)
            sp.dma_start(lower[:, :], lower_dram.partition_broadcast(P)).then_inc(loaded, 16)
            sp.wait_ge(saved, 16)
            sp.dma_start(acc[:, :, :], x3_dram.rearrange("(t p) d -> p t d", p=P)).then_inc(x_loaded, 16)

        @block.vector
        def _(dve):
            links = [0]

            def link(ins):
                links[0] += 1
                ins.then_inc(chain, 1)
                dve.wait_ge(chain, links[0])

            dve.wait_ge(x_loaded, 16)
            norm_chain(nc, dve, lambda k: one(acc, k), TT, stats, mv, sd, stats_done, var_ready, 0)
            dve.wait_ge(sd_ready, 1)
            nc.vector.reciprocal(rstd[:, :], sd[:, :]).then_inc(rstd_ready, 1)
            dve.wait_ge(rstd_ready, 1)

            def logits(k, p):
                dve.wait_ge(l_done, k + 1)
                nc.vector.tensor_copy(one(logit, k), ps_l[p][:, 0:E1]).then_inc(l_ready, 1)

            def tile(k, half, p):
                if not isinstance(k, int) or k >= 2:
                    dve.wait_ge(t_done, k - 1)
                nc.vector.tensor_scalar(xn[p][:, :], one(acc, k), one(mv, k)[:, 0:1], rstd[:, ds(k, 1)],
                                        ALU.subtract, ALU.mult).then_inc(xn_ready, 1)
                if not isinstance(k, int) or k >= 1:
                    logits(k - 1, 1 - p)
            peeled(nc.vector, TT, tile)
            logits(TT - 1, (TT - 1) % 2)

            dve.wait_ge(score_ready, 1)
            dve.wait_ge(loaded, 32)
            link(nc.vector.tensor_reduce(group[:, :, :], score[:, :, :].rearrange("p t (g e) -> p t g e", g=G1),
                                         AX.X, ALU.add))
            of_j = group[:, :, :].unsqueeze(2).to_broadcast([P, TT, G1, G1])
            of_i = group[:, :, :].unsqueeze(3).to_broadcast([P, TT, G1, G1])
            nc.vector.tensor_tensor(more[:, :, :, :], of_j, of_i, ALU.is_gt)
            link(nc.vector.tensor_tensor(same[:, :, :, :], of_j, of_i, ALU.is_equal))
            flat = same[:, :, :, :].rearrange("p t i j -> p t (i j)")
            link(nc.vector.tensor_tensor(flat, flat, lower[:, :].unsqueeze(1).to_broadcast([P, TT, G1 * G1]), ALU.mult))
            link(nc.vector.tensor_tensor(more[:, :, :, :].rearrange("p t i j -> p (t i j)"),
                                         more[:, :, :, :].rearrange("p t i j -> p (t i j)"),
                                         same[:, :, :, :].rearrange("p t i j -> p (t i j)"), ALU.add))
            link(nc.vector.tensor_reduce(g_rank[:, :, :], more[:, :, :, :], AX.X, ALU.add))
            link(nc.vector.tensor_scalar(g_sel[:, :, :], g_rank[:, :, :], float(TOP_G), None, ALU.is_lt))
            by_group = score[:, :, :].rearrange("p t (g e) -> p (t g) e", g=G1)
            link(nc.vector.tensor_tensor(by_group, by_group,
                                         g_sel[:, :, :].rearrange("p t g -> p (t g)").unsqueeze(2).to_broadcast(
                                             [P, TT * G1, GE]), ALU.mult))
            for k in range(TT):
                ins = nc.vector.max(top[:, k, :], score[:, k, :])
            link(ins)
            for k in range(TT):
                ins = nc.vector.match_replace(rest[:, k, :], top[:, k, :], score[:, k, :], -1.0)
            link(ins)
            link(nc.vector.tensor_tensor(rest[:, :, :], rest[:, :, :], score[:, :, :], ALU.not_equal))
            link(nc.vector.tensor_tensor(score[:, :, :], score[:, :, :], rest[:, :, :], ALU.mult))
            link(nc.vector.tensor_reduce(den[:, :], score[:, :, :], AX.X, ALU.add))
            link(nc.vector.tensor_scalar_max(den[:, :], den[:, :], 1e-12))
            link(nc.vector.reciprocal(den_inv[:, :], den[:, :]))
            nc.vector.tensor_tensor(comb[:, 0:E1, :].rearrange("p e t -> p t e"), score[:, :, :],
                                    den_inv[:, :].unsqueeze(2).to_broadcast([P, TT, E1]), ALU.mult)
            nc.vector.memset(comb[:, E1, :], 1.0)

        @block.gpsimd
        def _(pool):
            def low_part(k, half, p):
                pool.wait_ge(xf_ready, k + 1)
                pool.wait_ge(high_ready, k + 1)
                nc.gpsimd.tensor_tensor(x_s[1][:, :, ds(k * P, P)], xf[p][:, :, :],
                                        x_s[0][:, :, ds(k * P, P)].bitcast(F32), ALU.subtract).then_inc(low_ready, 1)
            peeled(nc.gpsimd, TT, low_part)

        @block.scalar
        def _(act):
            act.wait_ge(var_ready, 1)
            nc.scalar.activation(sd[:, :], sd[:, :], ACT.Sqrt).then_inc(sd_ready, 1)

            def tile(k, half, p):
                act.wait_ge(t_done, k + 1)
                if not isinstance(k, int) or k >= 2:
                    act.wait_ge(l_done, k - 1)
                    act.wait_ge(low_ready, k - 1)
                src = ps_t[p][:, 0:DC * P].rearrange("p (c s) -> p c s", c=DC)
                nc.scalar.copy(x_s[0][:, :, ds(k * P, P)], src).then_inc(high_ready, 1)
                nc.scalar.copy(xf[p][:, :, :], src).then_inc(xf_ready, 1)
            peeled(nc.scalar, TT, tile)
            act.wait_ge(l_ready, TT)
            nc.scalar.activation(score[:, :, :].rearrange("p t e -> p (t e)"),
                                 logit[:, :, :].rearrange("p t e -> p (t e)"), ACT.Sigmoid).then_inc(score_ready, 1)

        @block.tensor
        def _(pe):
            pe.wait_ge(loaded, 32)

            def logits(k, p):
                pe.wait_ge(xf_ready, k + 1)
                if not isinstance(k, int) or k >= 1:
                    pe.wait_ge(l_ready, k)
                for c in range(DC):
                    ins = nc.tensor.matmul(ps_l[p][:, 0:E1], xf[p][:, c, :], gate[:, c, :], start=(c == 0),
                                           stop=(c == DC - 1))
                ins.then_inc(l_done, 1)

            def tile(k, half, p):
                pe.wait_ge(xn_ready, k + 1)
                if not isinstance(k, int) or k >= 2:
                    pe.wait_ge(xf_ready, k - 1)
                for c in range(DC):
                    ins = nc.tensor.transpose(ps_t[p][:, c * P:(c + 1) * P], xn[p][:, c * P:(c + 1) * P], ident[:, :])
                ins.then_inc(t_done, 1)
                if not isinstance(k, int) or k >= 1:
                    logits(k - 1, 1 - p)
            peeled(nc.tensor, TT, tile)
            logits(TT - 1, (TT - 1) % 2)


def experts1_block(nc, acc, x_s, comb, w_dram, out_dram):
    NE = E1 + 1
    UNITS = [4, 4, 4, 4, 3, 3, 3]
    NU = len(UNITS)
    START = [sum(UNITS[:u]) for u in range(NU)]
    SPLIT_W = 3
    with ExitStack() as ctx:
        m = Memory(nc, ctx, "e1")
        two = range(2)
        W = 2 * DC * P + D
        w = [m.sb(f"w{j}", [P, W]) for j in two]
        w_s = [[m.sb(f"w{j}_s{i}", [P, W], F32R) for i in two] for j in two]
        wt = [m.sb(f"wt{j}", [P, TT]) for j in two]
        sg = [m.sb(f"sg{j}", [P, 512]) for j in two]
        hid = [m.sb(f"hid{j}", [P, 512]) for j in two]
        hid_s = [[m.sb(f"hid{j}_s{i}", [P, 512], F32R) for i in two] for j in two]
        ps_g = [m.ps(f"ps_g{j}") for j in two]
        ps_u = [m.ps(f"ps_u{j}") for j in two]
        ps_d = [m.ps(f"ps_d{j}") for j in range(4)]
        (w_high, w_low, g_done, u_done, s_ready, hid_ready, hid_high, hid_low, d_done, wt_ready, acc_ready, stored) = (
            m.sem(n) for n in ("w_high", "w_low", "g_done", "u_done", "s_ready", "hid_ready", "hid_high", "hid_low",
                               "d_done", "wt_ready", "acc_ready", "stored"))
        w_loaded = [m.sem(f"w_loaded{j}") for j in two]
        block = ctx.enter_context(nc.Block())

        def later(e, n):
            return not isinstance(e, int) or e >= n

        def before(e, u):
            if u:
                return e, u - 1
            return (e - 1, NU - 1) if later(e, 1) else None

        @block.sync
        def _(sp):
            def load(e, half, p):
                if later(e, 2):
                    sp.wait_ge(w_low, e - 1)
                sp.dma_start(w[p][:, :], w_dram[ds(e, 1)].rearrange("o p n -> p (o n)")).then_inc(w_loaded[p], 16)
            peeled(nc.sync, NE, load)
            out = out_dram.rearrange("(t p) d -> p t d", p=P)
            for u in range(NU):
                end = START[u] + UNITS[u]
                sp.wait_ge(acc_ready, (NE - 1) * TT + end)
                sp.dma_start(out[:, START[u]:end, :], acc[:, START[u]:end, :]).then_inc(stored, 16)
            sp.wait_ge(stored, 16 * NU)

        @block.gpsimd
        def _(pool):
            def split_w(e, p):
                pool.wait_ge(w_high, e + 1)
                nc.gpsimd.tensor_tensor(w_s[p][1][:, :], w[p][:, :], w_s[p][0][:, :].bitcast(F32),
                                        ALU.subtract).then_inc(w_low, 1)

            def expert(e, half, p):
                for u in range(NU):
                    n, q = e * NU + u, (p * NU + u) % 2
                    cols = UNITS[u] * P
                    pool.wait_ge(hid_high, n + 1)
                    nc.gpsimd.tensor_tensor(hid_s[q][1][:, 0:cols], hid[q][:, 0:cols],
                                            hid_s[q][0][:, 0:cols].bitcast(F32), ALU.subtract).then_inc(hid_low, 1)
                    if u == SPLIT_W and not (isinstance(e, int) and e == NE - 1):
                        split_w(e + 1, 1 - p)
            split_w(0, 0)
            peeled(nc.gpsimd, NE, expert)

        @block.vector
        def _(dve):
            def accumulate(e, p, u):
                for k in range(UNITS[u]):
                    t = START[u] + k
                    dve.wait_ge(d_done, e * TT + t + 1)
                    nc.vector.scalar_tensor_tensor(acc[:, t, :], ps_d[k][:, 0:D], wt[p][:, t:t + 1], acc[:, t, :],
                                                   ALU.mult, ALU.add).then_inc(acc_ready, 1)

            def expert(e, half, p):
                if later(e, 2):
                    dve.wait_ge(acc_ready, (e - 1) * TT)
                nc.vector.tensor_copy(wt[p][:, :], comb[:, ds(e, 1), :].rearrange("p o t -> p (o t)")
                                      ).then_inc(wt_ready, 1)
                dve.wait_ge(wt_ready, e + 1)
                for u in range(NU):
                    n, q = e * NU + u, (p * NU + u) % 2
                    cols = UNITS[u] * P
                    dve.wait_ge(s_ready, n + 1)
                    dve.wait_ge(u_done, n + 1)
                    if not isinstance(n, int) or n >= 2:
                        dve.wait_ge(hid_low, n - 1)
                    nc.vector.tensor_tensor(hid[q][:, 0:cols], sg[q][:, 0:cols], ps_u[q][:, 0:cols],
                                            ALU.mult).then_inc(hid_ready, 1)
                    prev = before(e, u)
                    if prev:
                        accumulate(prev[0], p if u else 1 - p, prev[1])
            peeled(nc.vector, NE, expert)
            accumulate(NE - 1, (NE - 1) % 2, NU - 1)

        @block.scalar
        def _(act):
            def split_w(e, half, p):
                act.wait_ge(w_loaded[p], half * 16 + 16)
                if later(e, 2) or not isinstance(e, int):
                    act.wait_ge(d_done, (e - 1) * TT)
                nc.scalar.copy(w_s[p][0][:, :], w[p][:, :]).then_inc(w_high, 1)

            def expert(e, half, p):
                for u in range(NU):
                    n, q = e * NU + u, (p * NU + u) % 2
                    cols = UNITS[u] * P
                    act.wait_ge(g_done, n + 1)
                    if not isinstance(n, int) or n >= 2:
                        act.wait_ge(hid_ready, n - 1)
                    nc.scalar.activation(sg[q][:, 0:cols], ps_g[q][:, 0:cols], ACT.Silu).then_inc(s_ready, 1)
                    act.wait_ge(hid_ready, n + 1)
                    if not isinstance(n, int) or n >= 2:
                        bu = before(e, u)
                        be, bu = before(*bu)
                        act.wait_ge(d_done, be * TT + START[bu] + UNITS[bu])
                    nc.scalar.copy(hid_s[q][0][:, 0:cols], hid[q][:, 0:cols]).then_inc(hid_high, 1)
                    if u == SPLIT_W and not (isinstance(e, int) and e == NE - 1):
                        split_w(e + 1, half + p, 1 - p)
            split_w(0, 0, 0)
            peeled(nc.scalar, NE, expert)

        @block.tensor
        def _(pe):
            def down(e, p, u):
                q = (p * NU + u) % 2
                pe.wait_ge(hid_low, e * NU + u + 1)
                for k in range(UNITS[u]):
                    t = START[u] + k
                    at = before(e, u)
                    while at and UNITS[at[1]] <= k:
                        at = before(*at)
                    if at:
                        pe.wait_ge(acc_ready, at[0] * TT + START[at[1]] + k + 1)
                    split_product(nc, ps_d[k][:, 0:D], [h[:, k * P:(k + 1) * P] for h in hid_s[q]],
                                  [v[:, 2 * DC * P:] for v in w_s[p]], True, True).then_inc(d_done, 1)

            def expert(e, half, p):
                pe.wait_ge(w_low, e + 1)
                for u in range(NU):
                    n, q = e * NU + u, (p * NU + u) % 2
                    cols, t0 = UNITS[u] * P, START[u] * P
                    for k, (bank, sem_done) in enumerate(((ps_g[q], g_done), (ps_u[q], u_done))):
                        if not isinstance(n, int) or n >= 2:
                            pe.wait_ge((s_ready, hid_ready)[k], n - 1)
                        for c in range(DC):
                            o = (k * DC + c) * P
                            ins = split_product(nc, bank[:, 0:cols], [v[:, o:o + P] for v in w_s[p]],
                                                [v[:, c, t0:t0 + cols] for v in x_s], c == 0, c == DC - 1)
                        ins.then_inc(sem_done, 1)
                    prev = before(e, u)
                    if prev:
                        down(prev[0], p if u else 1 - p, prev[1])
            peeled(nc.tensor, NE, expert)
            down(NE - 1, (NE - 1) % 2, NU - 1)


def program(nc, a):
    xs_dram = nc.dram_tensor("sorted_in", [SLOTS, D], F32).ap()
    ys_dram = nc.dram_tensor("sorted_out", [SLOTS, D], F32).ap()
    x3_dram = nc.dram_tensor("x3", [T, D], F32).ap()
    with ExitStack() as ctx:
        m = Memory(nc, ctx, "all")
        ident = m.sb("ident", [P, P])
        loaded = m.sem("loaded")
        x = m.sb("x", [S, NB, D])
        with nc.Block() as block:
            @block.sync
            def _(sp):
                sp.dma_start(ident[:, :], a["ident"]).then_inc(loaded, 16)
                sp.wait_ge(loaded, 16)
        with ExitStack() as c:
            q_t = Memory(nc, c, "l0").sb("q_t", [P, 2, T])
            queries_block(nc, 0, x, q_t, ident, 2, a["wq0"], a["bq0"], 16 ** -0.5, a["x"])
            attention_block(nc, 0, x, q_t, ident, 16, a["ctx"], a["wk0"], a["wv0"], a["wo0"], a["bk0"], a["bv0"],
                            a["bo0"], a["hmask0"])
        with ExitStack() as c:
            mr = Memory(nc, c, "r")
            alpha = mr.sb("alpha", [S, NB])
            slot = mr.sb("slot", [S, NB], I32)
            tile_expert = mr.sb("tile_expert", [1, N_ST], I32)
            route_block(nc, x, alpha, slot, tile_expert, ident, xs_dram, a["cent"], a["tri"], a["prio"], a["starts"])
            experts0_block(nc, tile_expert, ident, xs_dram, ys_dram, a["w1"], a["w2"], a["affine"], a["b2"])
            combine_block(nc, x, alpha, slot, ys_dram)
        with ExitStack() as c:
            q_t = Memory(nc, c, "l1").sb("q_t", [P, 4, T])
            queries_block(nc, 1, x, q_t, ident, 4, a["wq1"], None, 64 ** -0.5, None)
            attention_block(nc, 1, x, q_t, ident, 8, a["ctx"], a["wk1"], a["wv1"], a["wo1"], None, None, a["bo1"],
                            a["hmask1"])
        acc = m.sb("acc", [P, TT, D])
        x_s = [m.sb(f"x_s{i}", [P, DC, T], F32R) for i in range(2)]
        comb = m.sb("comb", [P, E1 + 1, TT])
        tokens_block(nc, x, acc, x_s, comb, ident, x3_dram, a["gate"], a["lower"])
        experts1_block(nc, acc, x_s, comb, a["we1"], a["out"].rearrange("b s d -> (b s) d"))


def kernel(**inputs):
    import numpy as np
    import concourse.bacc as bacc
    from concourse.bass_utils import run_bass_kernel_spmd

    def chunks(w):
        w = np.asarray(w)
        return np.ascontiguousarray(w.reshape(w.shape[0] // P, P, -1).transpose(1, 0, 2))

    def column(v):
        return np.ascontiguousarray(np.asarray(v).reshape(-1, P).T)

    def hmask(dk):
        return (np.arange(P)[:, None] // dk == np.arange(P // dk)[None]).astype(np.float32)

    g = {k: np.asarray(v) for k, v in inputs.items()}
    a = {
        "x": g["x"],
        "ctx": g["ctx_1024"].transpose(0, 2, 1).reshape(NB, DC, P, NK).transpose(0, 2, 1, 3),
        "ident": np.eye(P, dtype=np.float32),
        "bq0": column(g["L0_xattn_bq"]), "bk0": column(g["L0_xattn_bk"]), "bv0": g["L0_xattn_bv"],
        "bo0": g["L0_xattn_bo"], "bo1": g["L1_xattn_bo"], "hmask0": hmask(16), "hmask1": hmask(64),
        "cent": chunks(g["L0_ffn_centroids"].T),
        "tri": np.triu(np.ones((S, S), np.float32), 1),
        "prio": np.arange(E0, 0, -1).astype(np.float32),
        "starts": (np.arange(N_ST) * SLOT_TILE).astype(np.float32),
        "w1": g["L0_ffn_w1"].reshape(E0, DC, P, F0).transpose(0, 2, 1, 3),
        "w2": g["L0_ffn_w2"].reshape(E0, FC, P, D).transpose(0, 2, 1, 3),
        "affine": np.concatenate([g["L0_ffn_b1"].reshape(E0, FC, P), g["L0_ffn_gamma"].reshape(E0, DC, P),
                                  g["L0_ffn_beta"].reshape(E0, DC, P)], 1).transpose(0, 2, 1),
        "b2": g["L0_ffn_b2"],
        "gate": chunks(g["L1_ffn_gate_w"].T),
        "lower": np.tril(np.ones((G1, G1), np.float32), -1).reshape(-1),
    }
    for n in "qkvo":
        a[f"w{n}0"] = chunks(g[f"L0_xattn_W{n}"].T)
        a[f"w{n}1"] = chunks(g[f"L1_xattn_W{n}"])
    up = [np.concatenate([g[f"L1_ffn_expert_{k}"], g[f"L1_ffn_shared_{k}_w"][None]]) for k in ("gate", "up", "down")]
    by_input = [w.transpose(0, 2, 1).reshape(E1 + 1, DC, P, P).transpose(0, 2, 1, 3).reshape(E1 + 1, P, DC * P)
                for w in up[:2]]
    a["we1"] = np.concatenate([*by_input, up[2].transpose(0, 2, 1)], 2)

    nc = bacc.Bacc("TRN2", target_bir_lowering=False, num_devices=1)
    arrays, aps = {}, {}
    for name, v in a.items():
        arrays[f"in_{name}"] = np.ascontiguousarray(v)
        aps[name] = nc.dram_tensor(f"in_{name}", arrays[f"in_{name}"].shape, F32, kind="ExternalInput").ap()
    aps["out"] = nc.dram_tensor("out_x", (NB, S, D), F32, kind="ExternalOutput").ap()
    program(nc, aps)
    r = run_bass_kernel_spmd(nc, [arrays], core_ids=[0])
    return r.results[0]["out_x"]
```

```python
from contextlib import ExitStack

import concourse.bass as bass
from concourse import mybir

F32 = mybir.dt.float32
F32R = mybir.dt.float32r
I32 = mybir.dt.int32
ALU = mybir.AluOpType
ACT = mybir.ActivationFunctionType
AX = mybir.AxisListType
ds = bass.ds

P = 128
NB, S, D = 32, 100, 256
NK = 361
KC = 3
NKP = KC * P
NKE = NK + 1
DC = D // P
T = NB * S
E0, F0, FC = 8, 1024, 8
SLOT_TILE = 256
SLOT_SHIFT = 8
N_ST = (T + E0 * (SLOT_TILE - 1)) // SLOT_TILE
SLOTS = N_ST * SLOT_TILE
E1, G1, GE = 32, 8, 4
TOP_G, TOP_K = 4, 8
TT = T // P
EPS = 1e-5
NEVER = 3.0e38


def peeled(engine, n, body):
    body(0, 0, 0)
    body(1, 0, 1)
    pairs = (n - 3) // 2
    with engine.Fori(0, pairs) as i:
        body(i * 2 + 2, i + 1, 0)
        body(i * 2 + 3, i + 1, 1)
    for k in range(2 * pairs + 2, n):
        body(k, k // 2, k % 2)


def split_product(nc, out, lhs, rhs, first, last):
    parts = ((lhs[0], rhs[0]), (lhs[0], rhs[1]), (lhs[1], rhs[0]))
    for n, (x, y) in enumerate(parts):
        ins = nc.tensor.matmul(out, x, y, start=first and n == 0, stop=last and n == len(parts) - 1)
    return ins


class Memory:

    def __init__(self, nc, ctx, stage):
        self.nc, self.ctx, self.stage = nc, ctx, stage

    def sb(self, name, shape, dt=F32):
        return self.ctx.enter_context(self.nc.sbuf_tensor(f"{self.stage}_{name}", shape, dt))

    def ps(self, name, shape=(P, 512)):
        return self.ctx.enter_context(self.nc.psum_tensor(f"{self.stage}_{name}", list(shape), F32))

    def sem(self, name):
        return self.ctx.enter_context(self.nc.semaphore(f"{self.stage}_{name}"))


def queries_block(nc, lvl, x, q_t, ident, nch, wq_dram, bq_dram, scale, x_dram, q_dram):
    G = 4
    with ExitStack() as ctx:
        m = Memory(nc, ctx, f"q{lvl}")
        wq = m.sb("wq", [P, DC, nch * P])
        bq = m.sb("bq", [P, nch])
        stats = m.sb("stats", [S, NB, 6])
        mv = m.sb("mv", [S, NB, 2])
        sd = m.sb("sd", [S, NB])
        rstd = m.sb("rstd", [S, NB])
        xn = [m.sb(f"xn{j}", [S, D]) for j in range(2)]
        xg = [m.sb(f"xg{j}", [P, DC, G * S]) for j in range(2)]
        if q_dram is not None:
            one = m.sb("one", [P, 1])
            q_g = [m.sb(f"q_g{j}", [P, nch, G * S]) for j in range(2)]
            q_s = [[m.sb(f"q_s{j}_{i}", [P, nch, G * S], F32R) for i in range(2)] for j in range(2)]
            q_high, q_low = m.sem("q_high"), m.sem("q_low")
            q_stored = [m.sem(f"q_stored{j}") for j in range(2)]
        ps_t = [m.ps(f"ps_t{j}") for j in range(2)]
        ps_q = [m.ps(f"ps_q{j}") for j in range(4)]
        loaded, stats_done, var_ready, sd_ready, rstd_ready, xn_ready, t_done, t_evac, q_done, q_evac = (
            m.sem(n) for n in ("loaded", "stats_done", "var_ready", "sd_ready", "rstd_ready", "xn_ready",
                               "t_done", "t_evac", "q_done", "q_evac"))
        n_loads = 1 + (bq_dram is not None) + (x_dram is not None)
        block = ctx.enter_context(nc.Block())

        @block.sync
        def _(sp):
            if x_dram is not None:
                sp.dma_start(x[:, :, :], x_dram.rearrange("b s d -> s b d")).then_inc(loaded, 16)
            sp.dma_start(wq[:, :, :], wq_dram).then_inc(loaded, 16)
            if bq_dram is not None:
                sp.dma_start(bq[:, :], bq_dram).then_inc(loaded, 16)
            if q_dram is None:
                return

            def store(g, half, gp):
                for i, split in enumerate((q_high, q_low)):
                    sp.wait_ge(split, g + 1 + i)
                    sp.dma_start(q_dram[i].rearrange("(c p) t -> p c t", p=P)[:, :, ds(g * (G * S), G * S)],
                                 q_s[gp][i][:, :, :].bitcast(F32)).then_inc(q_stored[gp], 16)
            peeled(nc.sync, NB // G, store)
            for gp in range(2):
                sp.wait_ge(q_stored[gp], 32 * (NB // G // 2))

        @block.gpsimd
        def _(pool):
            if q_dram is None:
                return

            nc.gpsimd.memset(one[:, :], 1.0).then_inc(q_low, 1)

            def split(g, half, gp):
                if isinstance(g, int) and g == 0:
                    pool.wait_ge(q_low, 1)
                pool.wait_ge(q_evac, g * nch + nch)
                if not isinstance(g, int) or g >= 2:
                    pool.wait_ge(q_stored[gp], half * 32)
                nc.gpsimd.tensor_tensor(q_s[gp][0][:, :, :], q_g[gp][:, :, :],
                                        one[:, :].unsqueeze(2).to_broadcast([P, nch, G * S]),
                                        ALU.mult).then_inc(q_high, 1)
                pool.wait_ge(q_high, g + 1)
                nc.gpsimd.tensor_tensor(q_s[gp][1][:, :, :], q_g[gp][:, :, :], q_s[gp][0][:, :, :].bitcast(F32),
                                        ALU.subtract).then_inc(q_low, 1)
            peeled(nc.gpsimd, NB // G, split)

        @block.vector
        def _(dve):
            dve.wait_ge(loaded, 16 * n_loads)
            with nc.vector.Fori(0, NB) as b:
                nc.vector.bn_stats(stats[:, ds(b, 1), :].rearrange("p o s -> p (o s)"),
                                   x[:, ds(b, 1), :].rearrange("p o d -> p (o d)")).then_inc(stats_done, 1)
            dve.wait_ge(stats_done, NB)
            for b in range(NB):
                last = nc.vector.bn_aggr(mv[:, b, :], stats[:, b, :])
            last.then_inc(stats_done, 1)
            dve.wait_ge(stats_done, NB + 1)
            nc.vector.tensor_scalar_add(sd[:, :], mv[:, :, 1], EPS).then_inc(var_ready, 1)
            dve.wait_ge(sd_ready, 1)
            nc.vector.reciprocal(rstd[:, :], sd[:, :]).then_inc(rstd_ready, 1)
            dve.wait_ge(rstd_ready, 1)

            def normalise(b, j):
                if not isinstance(b, int) or b >= 2:
                    dve.wait_ge(t_done, b - 1)
                nc.vector.tensor_scalar(xn[j][:, :], x[:, ds(b, 1), :].rearrange("p o d -> p (o d)"),
                                        mv[:, ds(b, 1), 0:1].rearrange("p o s -> p (o s)"), rstd[:, ds(b, 1)],
                                        ALU.subtract, ALU.mult).then_inc(xn_ready, 1)

            def evacuate(g, half, gp):
                if q_dram is not None and (not isinstance(g, int) or g >= 2):
                    dve.wait_ge(q_low, g)
                for c in range(nch):
                    dve.wait_ge(q_done, g * nch + c + 1)
                    bank = ps_q[(gp * nch + c) % 4]
                    out = q_t[:, c, ds(g * (G * S), G * S)] if q_dram is None else q_g[gp][:, c, :]
                    if bq_dram is not None:
                        ins = nc.vector.tensor_scalar(out, bank[:, 0:G * S], bq[:, c:c + 1], scale, ALU.add, ALU.mult)
                    else:
                        ins = nc.vector.tensor_scalar(out, bank[:, 0:G * S], scale, None, ALU.mult)
                    ins.then_inc(q_evac, 1)

            def group(g, half, gp):
                for k in range(G):
                    normalise(g * G + k, k % 2)
                    if k == 3 and not (isinstance(g, int) and g == 0):
                        evacuate(g - 1, None, 1 - gp)
            peeled(nc.vector, NB // G, group)
            evacuate(NB // G - 1, None, 1)

        @block.scalar
        def _(act):
            act.wait_ge(var_ready, 1)
            nc.scalar.activation(sd[:, :], sd[:, :], ACT.Sqrt).then_inc(sd_ready, 1)

            def group(g, half, gp):
                if not isinstance(g, int) or g >= 2:
                    act.wait_ge(q_done, (g - 1) * nch)
                for k in range(G):
                    act.wait_ge(t_done, g * G + k + 1)
                    nc.scalar.copy(xg[gp][:, :, k * S:(k + 1) * S],
                                   ps_t[k % 2][:, 0:DC * S].rearrange("p (c s) -> p c s", c=DC)).then_inc(t_evac, 1)
            peeled(nc.scalar, NB // G, group)

        @block.tensor
        def _(pe):
            def project(g, half, gp):
                pe.wait_ge(t_evac, (g + 1) * G)
                if not (isinstance(g, int) and g == 0):
                    pe.wait_ge(q_evac, g * nch)
                for c in range(nch):
                    bank = ps_q[(gp * nch + c) % 4]
                    for k in range(DC):
                        ins = nc.tensor.matmul(bank[:, 0:G * S], wq[:, k, c * P:(c + 1) * P], xg[gp][:, k, :],
                                               start=(k == 0), stop=(k == DC - 1))
                    ins.then_inc(q_done, 1)

            def group(g, half, gp):
                for k in range(G):
                    pe.wait_ge(xn_ready, g * G + k + 1)
                    if k >= 2 or not (isinstance(g, int) and g == 0):
                        pe.wait_ge(t_evac, g * G + k - 1)
                    for c in range(DC):
                        ins = nc.tensor.transpose(ps_t[k % 2][:, c * S:(c + 1) * S], xn[k % 2][:, c * P:(c + 1) * P],
                                                  ident[0:S, 0:S])
                    ins.then_inc(t_done, 1)
                    if k == 1 and not (isinstance(g, int) and g == 0):
                        project(g - 1, None, 1 - gp)
            pe.wait_ge(loaded, 16 * n_loads)
            peeled(nc.tensor, NB // G, group)
            project(NB // G - 1, None, 1)


def attention_block(nc, lvl, x, q_t, ident, heads, ctx_dram, wk_dram, wv_dram, wo_dram, bk_dram, bv_dram,
                    bo_dram, hmask_dram, q_dram, k_dram):
    dk = D // heads if lvl == 0 else 64
    H = heads
    nch = H * dk // P
    HPC = P // dk
    TRANSPOSE_LAG, PV_LAG = 2, 4
    stack = 3 * dk <= P // 2
    VN = max(dk, 32)
    K_STEPS = (10, 12, 14, 15)
    K_PIECES = len(K_STEPS)
    Q_PARTS, K_PARTS = (0, 1, 0), (0, 0, 1)
    if lvl == 0:
        tasks = [(0, "K", 0, 0), (2, "K", 1, 0), (5, "OT", 0, 0), (7, "OP", 0, 0), (9, "V", 0, 0), (11, "V", 1, 0),
                 (13, "V", 2, 0)]
        EVAC_LAG, X_BANKS = 1, 1
        s_bank = [h % 3 for h in range(H - 1)] + [1]
    else:
        tasks = [(0, "K", 0, 0), (1, "K", 1, 1), (2, "K", 2, 0), (3, "K", 3, 1), (5, "OT", 0, 0), (5, "V", 0, 1),
                 (6, "V", 1, 0), (7, "V", 2, 1), (7, "OP", 0, 0)]
        EVAC_LAG, X_BANKS = 0, 2
        s_bank = [h % 2 for h in range(H)]
    OT_STEP = next(s for s, k, _, _ in tasks if k == "OT")
    OP_STEP = next(s for s, k, _, _ in tasks if k == "OP")

    with ExitStack() as ctx:
        m = Memory(nc, ctx, f"a{lvl}")
        w_raw = m.sb("w_raw", [P, DC, nch * P])
        wk_s = [m.sb(f"wk_s{j}", [P, DC, nch * P], F32R) for j in range(2)]
        wv_s = [m.sb(f"wv_s{j}", [P, DC, nch * P], F32R) for j in range(2)]
        wo = m.sb("wo", [P, nch, D])
        bk = m.sb("bk", [P, nch])
        bv = m.sb("bv", [P, nch * P]) if bv_dram is not None else None
        bo = m.sb("bo", [S, D])
        QPC = hmask_dram.shape[1]
        hmask = m.sb("hmask", [P, QPC])
        ctx_t = [m.sb(f"ctx{j}", [P, DC, NKP]) for j in range(2)]
        ctx_s = [[m.sb(f"ctx{j}_s{i}", [P, DC, NKP], F32R) for i in range(2)] for j in range(2)]
        v = [m.sb(f"v{j}", [P, KC, nch * P]) for j in range(2)]
        if stack:
            kt = [[m.sb(f"kt_s{i}", [P, nch, NKE], F32R) for i in range(2)]] * 2
            k_raw = m.sb("k_raw", [P, H // 2, NKE])
            q_raw = m.sb("q_raw", [P, H // 2, S])
            ks = [m.sb(f"ks{j}", [P, H // 2, NKE], F32R) for j in range(2)]
            qs = [[m.sb(f"qs{j}", [P, H, S], F32R)] for j in range(2)]
        else:
            kt = [[m.sb(f"kt{j}_s{i}", [P, nch, NKE], F32R) for i in range(2)] for j in range(2)]
            qm = m.sb("qm", [P, H, S])
            qs = [[m.sb(f"qs{j}_s{i}", [P, H, S], F32R) for i in range(2)] for j in range(2)]
        neg_max = m.sb("neg_max", [S, 2, H])
        row_sum = m.sb("row_sum", [S, 2, H])
        row_inv = m.sb("row_inv", [S, H])
        prob = [m.sb(f"prob{j}", [S, NKP]) for j in range(4)]
        prob_t = [m.sb(f"prob_t{j}", [P, KC * S]) for j in range(4)]
        o_row = m.sb("o_row", [S, nch * P])
        o_t = m.sb("o_t", [P, nch, S])
        ps_s = [m.ps(f"ps_s{j}") for j in range(max(s_bank) + 1)]
        ps_p = [m.ps(f"ps_p{j}") for j in range(2)]
        ps_o = [m.ps(f"ps_o{j}") for j in range(2)]
        ps_x = [m.ps(f"ps_x{j}") for j in range(X_BANKS)]
        unused = ("qm_done", "q_hi") if stack else ("q_loaded", "k_stored", "k_loaded", "ks_ready")
        (loaded, cleared, w_loaded, w_ready, ctx_hi, ctx_ready, q_loaded, qm_done, q_hi, q_ready, k_done, k_hi,
         k_ready, k_stored, k_loaded, ks_ready, v_done, v_ready, xb_ready, scores_done, max_ready, prob_ready,
         pt_done, pt_ready, pv_done, inv_ready, o_ready, ot_done, ot_ready, out_done, x_ready) = (
            None if n in unused else m.sem(n) for n in
            ("loaded", "cleared", "w_loaded", "w_ready", "ctx_hi", "ctx_ready", "q_loaded", "qm_done", "q_hi",
             "q_ready", "k_done", "k_hi", "k_ready", "k_stored", "k_loaded", "ks_ready", "v_done", "v_ready",
             "xb_ready", "scores_done", "max_ready", "prob_ready", "pt_done", "pt_ready", "pv_done", "inv_ready",
             "o_ready", "ot_done", "ot_ready", "out_done", "x_ready"))
        ctx_loaded = [m.sem(f"ctx_loaded{j}") for j in range(2)]
        loads = [(wo, wo_dram), (hmask, hmask_dram)]
        if bk_dram is not None:
            loads += [(bk, bk_dram), (bv, bv_dram.partition_broadcast(P))]
        loads.append((bo, bo_dram.partition_broadcast(S)))
        LOADED = 16 * len(loads)
        CLEARED = 8 if stack else 6
        STACKED = 16 * 6

        def has_prev(b):
            return not (isinstance(b, int) and b == 0)

        def has_cur(b):
            return not (isinstance(b, int) and b >= NB)

        def has_next(b):
            return not (isinstance(b, int) and b >= NB - 1)

        def has_next2(b):
            return not (isinstance(b, int) and b >= NB - 2)

        def lagged(b, h, lag):
            if h >= lag:
                return b, h - lag, has_cur(b)
            return b - 1, H + h - lag, has_prev(b)

        def head_outputs(p):
            a = ps_o[p][0:S, 0:H * VN]
            return bass.AP(a.tensor, a.offset, [list(a.ap[0]), [VN // dk * VN, H * dk // VN], [VN + dk, VN // dk],
                                                [1, dk]])

        def other(half, p):
            return half + p

        block = ctx.enter_context(nc.Block())

        @block.sync
        def _(sp):
            def load_ctx(b, p):
                sp.dma_start(ctx_t[p][:, :, 0:NK],
                             ctx_dram[ds(b, 1)].rearrange("o p c s -> p (o c) s")).then_inc(ctx_loaded[p], 16)
            sp.dma_start(w_raw[:, :, :], wk_dram).then_inc(w_loaded, 16)
            load_ctx(0, 0)
            for dst, src in loads:
                sp.dma_start(dst[tuple(slice(None) for _ in dst.shape)], src).then_inc(loaded, 16)
            load_ctx(1, 1)
            sp.wait_ge(w_ready, 2)
            sp.dma_start(w_raw[:, :, :], wv_dram).then_inc(w_loaded, 16)

            def stacked(dram, j):
                return dram.rearrange("(pair j d) t -> j d pair t", j=2, d=dk)[j]

            def load_q(b):
                if not isinstance(b, int) or b >= 1:
                    sp.wait_ge(q_ready, b)
                for j in range(2):
                    for r, part in enumerate(Q_PARTS):
                        o = P // 2 * j + dk * r
                        sp.dma_start(q_raw[o:o + dk, :, :],
                                     stacked(q_dram[part], j)[:, :, ds(b * S, S)]).then_inc(q_loaded, 16)

            def stack_k(b):
                sp.wait_ge(k_ready, b * nch + nch)
                for part in range(2):
                    if part and (not isinstance(b, int) or b >= 1):
                        sp.wait_ge(ks_ready, b * K_PIECES)
                    sp.dma_start(k_dram[part].rearrange("(c p) n -> p c n", p=P),
                                 kt[0][part][:, :, :].bitcast(F32)).then_inc(k_stored, 16)
                sp.wait_ge(k_stored, b * 32 + 32)
                for j in range(2):
                    for r, part in enumerate(K_PARTS):
                        o = P // 2 * j + dk * r
                        sp.dma_start(k_raw[o:o + dk, :, :], stacked(k_dram[part], j)).then_inc(k_loaded, 16)

            if stack:
                sp.wait_ge(cleared, CLEARED)
                load_q(0)
                stack_k(0)
                load_q(1)

            def batch(b, half, p):
                if has_next2(b):
                    sp.wait_ge(ctx_ready, b + 1)
                    load_ctx(b + 2, p)
                if stack and has_next(b):
                    stack_k(b + 1)
                if stack and has_next2(b):
                    load_q(b + 2)
            peeled(nc.sync, NB, batch)

        @block.gpsimd
        def _(pool):
            if stack:
                nc.gpsimd.memset(q_raw[:, :, :], 0.0).then_inc(cleared, 1)
                nc.gpsimd.memset(k_raw[:, :, :], 0.0).then_inc(cleared, 1)
            pool.wait_ge(cleared, CLEARED)
            pool.wait_ge(loaded, LOADED)

            def spread_stacked_q(b, p):
                pool.wait_ge(q_loaded, b * STACKED + STACKED)
                nc.gpsimd.tensor_tensor(
                    qs[p][0][:, :, :].rearrange("p (pair j) s -> p pair j s", j=2),
                    q_raw[:, :, :].unsqueeze(2).to_broadcast([P, H // 2, 2, S]),
                    hmask[:, :].unsqueeze(1).unsqueeze(3).to_broadcast([P, H // 2, 2, S]),
                    ALU.mult).then_inc(q_ready, 1)

            def spread_q(b, p):
                if not isinstance(b, int) or b >= 1:
                    pool.wait_ge(q_hi, b)
                    pool.wait_ge(q_ready, b)
                for c in range(nch):
                    ins = nc.gpsimd.tensor_tensor(
                        qm[:, c * HPC:(c + 1) * HPC, :],
                        q_t[:, c, ds(b * S, S)].unsqueeze(1).to_broadcast([P, HPC, S]),
                        hmask[:, :].unsqueeze(2).to_broadcast([P, HPC, S]), ALU.mult)
                ins.then_inc(qm_done, 1)
                pool.wait_ge(q_hi, b + 1)
                nc.gpsimd.tensor_tensor(qs[p][1][:, :, :], qm[:, :, :], qs[p][0][:, :, :].bitcast(F32),
                                        ALU.subtract).then_inc(q_ready, 1)

            def split_ctx(b, p):
                pool.wait_ge(ctx_hi, b + 1)
                nc.gpsimd.tensor_tensor(ctx_s[p][1][:, :, :], ctx_t[p][:, :, :], ctx_s[p][0][:, :, :].bitcast(F32),
                                        ALU.subtract).then_inc(ctx_ready, 1)

            def add_bo(b):
                xb = x[:, ds(b, 1), :].rearrange("p o d -> p (o d)")
                nc.gpsimd.tensor_tensor(xb, xb, bo[:, :], ALU.add).then_inc(xb_ready, 1)

            def split_w(w_s, n):
                pool.wait_ge(w_ready, 2 * n + 1)
                nc.gpsimd.tensor_tensor(w_s[1][:, :, :], w_raw[:, :, :], w_s[0][:, :, :].bitcast(F32),
                                        ALU.subtract).then_inc(w_ready, 1)
            split_w(wk_s, 0)
            split_ctx(0, 0)
            split_w(wv_s, 1)
            (spread_stacked_q if stack else spread_q)(0, 0)
            split_ctx(1, 1)

            def batch(b, half, p):
                add_bo(b)
                if has_next(b):
                    if has_prev(b):
                        pool.wait_ge(scores_done, b * H)
                    (spread_stacked_q if stack else spread_q)(b + 1, 1 - p)
                if has_next2(b):
                    split_ctx(b + 2, p)
            peeled(nc.gpsimd, NB, batch)

        @block.vector
        def _(dve):
            for j in range(2):
                nc.vector.memset(ctx_t[j][:, :, NK:NKP], 0.0).then_inc(cleared, 1)
            for j in range(4):
                nc.vector.memset(prob[j][:, NK:NKP], 0.0).then_inc(cleared, 1)
            dve.wait_ge(cleared, CLEARED)
            dve.wait_ge(loaded, LOADED)

            def evac_v(b, p, kc):
                dve.wait_ge(v_done, b * KC + kc + 1)
                src = ps_x[next(k for _, kind, i, k in tasks if kind == "V" and i == kc)][:, 0:nch * P]
                if bv_dram is not None:
                    ins = nc.vector.tensor_tensor(v[p][:, kc, :], src, bv[:, :], ALU.add)
                else:
                    ins = nc.vector.tensor_copy(v[p][:, kc, :], src)
                ins.then_inc(v_ready, 1)

            def evac_k(b, p, c):
                dve.wait_ge(k_hi, b * nch + c + 1)
                bank = ps_x[next(k for _, kind, i, k in tasks if kind == "K" and i == c)]
                high = kt[p][0][:, c, :].bitcast(F32)
                if bk_dram is not None:
                    ins = nc.vector.scalar_tensor_tensor(kt[p][1][:, c, :], bank[:, 0:NKE], bk[:, c:c + 1], high,
                                                         ALU.add, ALU.subtract)
                else:
                    ins = nc.vector.tensor_tensor(kt[p][1][:, c, :], bank[:, 0:NKE], high, ALU.subtract)
                ins.then_inc(k_ready, 1)

            for n, (_, kind, i, _) in enumerate(tasks):
                if kind == "K":
                    evac_k(0, 0, i)
                elif kind == "V":
                    evac_v(0, 0, i)

            def step(b, half, p, h):
                g = b * H + h
                if has_cur(b):
                    dve.wait_ge(scores_done, g + 1)
                    nc.vector.tensor_reduce(neg_max[:, p, h:h + 1], ps_s[s_bank[h]][0:S, 0:NK], AX.X, ALU.max,
                                            negate=True).then_inc(max_ready, 1)
                bt, ht, exists = lagged(b, h, TRANSPOSE_LAG)
                if exists:
                    gt = bt * H + ht
                    dve.wait_ge(pt_done, gt + 1)
                    if not isinstance(gt, int) or gt >= 4:
                        dve.wait_ge(pv_done, gt - 3)
                    nc.vector.tensor_copy(prob_t[ht % 4][:, :], ps_p[ht % 2][:, 0:KC * S]).then_inc(pt_ready, 1)
                if has_prev(b) and h == 2:
                    dve.wait_ge(prob_ready, b * H)
                    if not (isinstance(b, int) and b == 1):
                        dve.wait_ge(o_ready, b - 1)
                    nc.vector.reciprocal(row_inv[:, :], row_sum[:, 1 - p, :]).then_inc(inv_ready, 1)
                if has_prev(b) and h == OT_STEP - 1:
                    dve.wait_ge(pv_done, b * H)
                    dve.wait_ge(inv_ready, b)
                    if not (isinstance(b, int) and b == 1):
                        dve.wait_ge(ot_done, b - 1)
                    by_group = [S, H * dk // VN, VN // dk, dk]
                    nc.vector.tensor_tensor(o_row[:, :].rearrange("p (g j d) -> p g j d", j=VN // dk, d=dk),
                                            head_outputs(1 - p),
                                            row_inv[:, :].rearrange("p (g j) -> p g j", j=VN // dk).unsqueeze(3)
                                            .to_broadcast(by_group),
                                            ALU.mult).then_inc(o_ready, 1)
                if has_next(b):
                    for s, kind, i, _ in tasks:
                        if s + EVAC_LAG == h and kind == "K":
                            evac_k(b + 1, 1 - p, i)
                        if s + EVAC_LAG == h and kind == "V":
                            if has_prev(b):
                                dve.wait_ge(pv_done, b * H)
                            evac_v(b + 1, 1 - p, i)
                if has_prev(b) and h == OP_STEP + EVAC_LAG:
                    dve.wait_ge(out_done, b)
                    dve.wait_ge(xb_ready, b)
                    xb = x[:, ds(b - 1, 1), :].rearrange("p o d -> p (o d)")
                    bank = ps_x[next(k for _, kind, _, k in tasks if kind == "OP")]
                    nc.vector.tensor_tensor(xb, bank[0:S, 0:D], xb, ALU.add).then_inc(x_ready, 1)

            def batch(b, half, p):
                for h in range(H):
                    step(b, half, p, h)
            peeled(nc.vector, NB, batch)
            for h in range(OP_STEP + 1 + EVAC_LAG):
                step(NB, NB // 2, 0, h)

        @block.scalar
        def _(act):
            act.wait_ge(loaded, LOADED)
            act.wait_ge(cleared, CLEARED)

            def evac_k(b, p, c):
                act.wait_ge(k_done, b * nch + c + 1)
                if stack and (not isinstance(b, int) or b >= 1):
                    act.wait_ge(k_stored, b * 32)
                bank = ps_x[next(k for _, kind, i, k in tasks if kind == "K" and i == c)]
                if bk_dram is not None:
                    ins = nc.scalar.activation(kt[p][0][:, c, :], bank[:, 0:NKE], ACT.Identity, bias=bk[:, c:c + 1])
                else:
                    ins = nc.scalar.copy(kt[p][0][:, c, :], bank[:, 0:NKE])
                ins.then_inc(k_hi, 1)

            def split_ctx(b, half, p):
                act.wait_ge(ctx_loaded[p], half * 16 + 16)
                if not isinstance(b, int) or b >= 2:
                    act.wait_ge(v_done, (b - 1) * KC)
                nc.scalar.copy(ctx_s[p][0][:, :, :], ctx_t[p][:, :, :]).then_inc(ctx_hi, 1)

            def split_q(b, p):
                act.wait_ge(qm_done, b + 1)
                nc.scalar.copy(qs[p][0][:, :, :], qm[:, :, :]).then_inc(q_hi, 1)

            def split_w(w_s, n):
                act.wait_ge(w_loaded, 16 * n + 16)
                nc.scalar.copy(w_s[0][:, :, :], w_raw[:, :, :]).then_inc(w_ready, 1)
            split_w(wk_s, 0)
            split_ctx(0, 0, 0)
            split_w(wv_s, 1)
            if not stack:
                split_q(0, 0)
            split_ctx(1, 0, 1)
            for c in range(nch):
                evac_k(0, 0, c)

            def copy_stacked_k(b, p, piece):
                if piece == 0:
                    act.wait_ge(k_loaded, b * STACKED + STACKED)
                    if not isinstance(b, int) or b >= 2:
                        act.wait_ge(scores_done, (b - 1) * H)
                pairs = slice(piece * H // 2 // K_PIECES, (piece + 1) * H // 2 // K_PIECES)
                nc.scalar.copy(ks[p][:, pairs, :], k_raw[:, pairs, :]).then_inc(ks_ready, 1)
            if stack:
                for piece in range(K_PIECES):
                    copy_stacked_k(0, 0, piece)

            def step(b, half, p, h):
                g = b * H + h
                if has_cur(b):
                    act.wait_ge(max_ready, g + 1)
                    if not isinstance(g, int) or g >= 4:
                        act.wait_ge(pt_done, g - 3)
                    if h == 0 and not (isinstance(b, int) and b < 2):
                        act.wait_ge(inv_ready, b - 1)
                    nc.scalar.activation(prob[h % 4][:, 0:NK], ps_s[s_bank[h]][0:S, 0:NK], ACT.Exp,
                                         bias=neg_max[:, p, h:h + 1],
                                         accum_out=row_sum[:, p, h:h + 1]).then_inc(prob_ready, 1)
                if has_prev(b) and h == OT_STEP:
                    act.wait_ge(ot_done, b)
                    if not (isinstance(b, int) and b == 1):
                        act.wait_ge(out_done, b - 1)
                    bank = ps_x[next(k for _, kind, _, k in tasks if kind == "OT")]
                    nc.scalar.copy(o_t[:, :, :].rearrange("p c s -> p (c s)"), bank[:, 0:nch * S]).then_inc(ot_ready, 1)
                if has_next(b):
                    for s, kind, i, _ in tasks:
                        if s == h and kind == "K":
                            evac_k(b + 1, 1 - p, i)
                    if h == H // 2 and not stack:
                        split_q(b + 1, 1 - p)
                    if h in K_STEPS and stack:
                        copy_stacked_k(b + 1, 1 - p, K_STEPS.index(h))
                if has_next2(b) and h == H - 3:
                    split_ctx(b + 2, half + 1, p)

            def batch(b, half, p):
                for h in range(H):
                    step(b, half, p, h)
            peeled(nc.scalar, NB, batch)
            for h in range(OT_STEP + 1):
                step(NB, NB // 2, 0, h)

        @block.tensor
        def _(pe):
            def evacuated(kind, i, b):
                return {"K": (k_ready, (b + 1) * nch + i + 1), "V": (v_ready, (b + 1) * KC + i + 1),
                        "OT": (ot_ready, b), "OP": (x_ready, b)}[kind]

            def bank_free(n, b):
                at, bb = n, b
                while True:
                    at -= 1
                    if at < 0:
                        at, bb = len(tasks) - 1, bb - 1
                        if isinstance(bb, int) and bb < -1:
                            return
                    _, kind, i, bank = tasks[at]
                    exists = has_next(bb) if kind in "KV" else has_prev(bb) and not (isinstance(bb, int) and bb < 0)
                    if exists and bank == tasks[n][3]:
                        pe.wait_ge(*evacuated(kind, i, bb))
                        return

            def project_k(b, half, p, c, bank):
                if c == 0:
                    pe.wait_ge(ctx_ready, b + 1)
                for k in range(DC):
                    ins = split_product(nc, bank[:, 0:NKE], [w[:, k, c * P:(c + 1) * P] for w in wk_s],
                                        [t[:, k, 0:NKE] for t in ctx_s[p]], k == 0, k == DC - 1)
                ins.then_inc(k_done, 1)

            def project_v(p, kc, bank):
                for k in range(DC):
                    ins = split_product(nc, bank[:, 0:nch * P], [t[:, k, kc * P:(kc + 1) * P] for t in ctx_s[p]],
                                        [w[:, k, :] for w in wv_s], k == 0, k == DC - 1)
                ins.then_inc(v_done, 1)

            def side(n, b, half, p):
                _, kind, i, bank_at = tasks[n]
                bank = ps_x[bank_at]
                if kind in "KV":
                    if not has_next(b):
                        return
                    bank_free(n, b)
                    if kind == "K":
                        project_k(b + 1, other(half, p), 1 - p, i, bank)
                    else:
                        project_v(1 - p, i, bank)
                    return
                if not has_prev(b):
                    return
                bank_free(n, b)
                if kind == "OT":
                    pe.wait_ge(o_ready, b)
                    for c in range(nch):
                        ins = nc.tensor.transpose(bank[:, c * S:(c + 1) * S], o_row[:, c * P:(c + 1) * P],
                                                  ident[0:S, 0:S])
                    ins.then_inc(ot_done, 1)
                else:
                    pe.wait_ge(ot_ready, b)
                    for c in range(nch):
                        ins = nc.tensor.matmul(bank[0:S, 0:D], o_t[:, c, :], wo[:, c, :], start=(c == 0),
                                               stop=(c == nch - 1))
                    ins.then_inc(out_done, 1)

            def step(b, half, p, h):
                g = b * H + h
                if has_cur(b):
                    if h == 0:
                        if not stack:
                            pe.wait_ge(k_ready, b * nch + nch)
                        pe.wait_ge(q_ready, b + 1)
                    if stack and h % (H // K_PIECES) == 0:
                        pe.wait_ge(ks_ready, b * K_PIECES + h // (H // K_PIECES) + 1)
                    ago = next(k for k in range(1, H) if s_bank[h - k] == s_bank[h])
                    if not isinstance(g, int) or g >= ago:
                        pe.wait_ge(prob_ready, g + 1 - ago)
                    out = ps_s[s_bank[h]][0:S, 0:NKE]
                    if stack:
                        ins = nc.tensor.matmul(out, qs[p][0][:, h, :], ks[p][:, h // 2, :], start=True, stop=True)
                    else:
                        ins = split_product(nc, out, [q[:, h, :] for q in qs[p]],
                                            [k[:, h // HPC, :] for k in kt[p]], True, True)
                    ins.then_inc(scores_done, 1)
                bt, ht, exists = lagged(b, h, TRANSPOSE_LAG)
                if exists:
                    gt = bt * H + ht
                    pe.wait_ge(prob_ready, gt + 1)
                    if not isinstance(gt, int) or gt >= 2:
                        pe.wait_ge(pt_ready, gt - 1)
                    for kc in range(KC):
                        ins = nc.tensor.transpose(ps_p[ht % 2][:, kc * S:(kc + 1) * S],
                                                  prob[ht % 4][:, kc * P:(kc + 1) * P], ident[0:S, 0:S])
                    ins.then_inc(pt_done, 1)
                bv_, hv, exists = lagged(b, h, PV_LAG)
                if exists:
                    gv, pv = bv_ * H + hv, p if h >= PV_LAG else 1 - p
                    if hv == 0:
                        pe.wait_ge(v_ready, bv_ * KC + KC)
                        if not (isinstance(bv_, int) and bv_ < 2):
                            pe.wait_ge(o_ready, bv_ - 1)
                    pe.wait_ge(pt_ready, gv + 1)
                    for kc in range(KC):
                        f = hv * dk // VN * VN
                        ins = nc.tensor.matmul(ps_o[pv][0:S, hv * VN:(hv + 1) * VN],
                                               prob_t[hv % 4][:, kc * S:(kc + 1) * S],
                                               v[pv][:, kc, f:f + VN], start=(kc == 0),
                                               stop=(kc == KC - 1))
                    ins.then_inc(pv_done, 1)
                for n, t in enumerate(tasks):
                    if t[0] == h:
                        side(n, b, half, p)

            pe.wait_ge(loaded, LOADED)
            pe.wait_ge(cleared, CLEARED)
            pe.wait_ge(w_ready, 4)
            for n, (_, kind, i, bank) in enumerate(tasks):
                if kind in "KV":
                    bank_free(n, -1)
                    if kind == "K":
                        project_k(0, 0, 0, i, ps_x[bank])
                    else:
                        project_v(0, i, ps_x[bank])

            def batch(b, half, p):
                for h in range(H):
                    step(b, half, p, h)
            peeled(nc.tensor, NB, batch)
            for h in range(OP_STEP + 1):
                step(NB, NB // 2, 0, h)


def norm_chain(nc, dve, x_of, n, stats, mv, sd, stats_done, var_ready, var_before, rows=S):
    with nc.vector.Fori(0, n) as b:
        nc.vector.bn_stats(stats[:, ds(b, 1), :].rearrange("p o s -> p (o s)"), x_of(b)).then_inc(stats_done, 1)
    base = var_before * (n + 1)
    dve.wait_ge(stats_done, base + n)
    for b in range(n):
        last = nc.vector.bn_aggr(mv[:, b, :], stats[:, b, :])
    last.then_inc(stats_done, 1)
    dve.wait_ge(stats_done, base + n + 1)
    nc.vector.tensor_scalar_add(sd[:, :], mv[:, :, 1], EPS).then_inc(var_ready, 1)


def route_block(nc, x, alpha, slot, tile_expert, ident, xs_dram, cent_dram, tri_dram, prio_dram, starts_dram):
    with ExitStack() as ctx:
        m = Memory(nc, ctx, "rt")
        zero = m.sb("zero", [P, SLOTS // P // 4, D])
        cent = m.sb("cent", [P, DC, E0])
        tri = m.sb("tri", [S, S])
        prio = m.sb("prio", [S, E0])
        starts = m.sb("starts", [1, N_ST])
        ones = m.sb("ones", [S, P])
        f = m.sb("f", [S, NB, D])
        fs = [m.sb(f"fs{j}", [S, D]) for j in range(2)]
        ft = [m.sb(f"ft{j}", [P, DC, S]) for j in range(2)]
        stats = m.sb("stats", [S, NB, 6])
        mv = m.sb("mv", [S, NB, 2])
        sd = m.sb("sd", [S, NB])
        rstd = m.sb("rstd", [S, NB])
        aff = m.sb("aff", [S, NB, E0])
        best = m.sb("best", [S, NB])
        hot = m.sb("hot", [S, NB, E0])
        rank = m.sb("rank", [S, NB, E0])
        total = m.sb("total", [S, E0, NB])
        before = m.sb("before", [S, E0, NB])
        count = m.sb("count", [S, E0])
        count_i = m.sb("count_i", [S, E0], I32)
        padded = m.sb("padded", [S, E0])
        end = m.sb("end", [S, E0])
        base = m.sb("base", [S, E0])
        slot_f = m.sb("slot_f", [S, NB])
        past = m.sb("past", [1, N_ST, E0])
        te_f = m.sb("te_f", [1, N_ST])
        ps_t = [m.ps(f"ps_t{j}") for j in range(2)]
        ps_a = [m.ps(f"ps_a{j}") for j in range(2)]
        ps_rank, ps_total = m.ps("ps_rank"), m.ps("ps_total")
        names = ("loaded", "zero_set", "zeroed", "stats_done", "var_ready", "sd_ready", "f_ready", "x_ready", "fs_ready",
                 "t_done", "ft_ready", "aff_done", "aff_ready", "chain", "best_ready", "hot_ready", "counted",
                 "slot_ready", "xh_ready", "scattered", "ones_set")
        (loaded, zero_set, zeroed, stats_done, var_ready, sd_ready, f_ready, x_ready, fs_ready, t_done, ft_ready,
         aff_done, aff_ready, chain, best_ready, hot_ready, counted, slot_ready, xh_ready, scattered, ones_set) = (
            m.sem(n) for n in names)
        block = ctx.enter_context(nc.Block())

        def one(t, b):
            return t[:, ds(b, 1), :].rearrange("p o d -> p (o d)")

        @block.sync
        def _(sp):
            sp.dma_start(cent[:, :, :], cent_dram).then_inc(loaded, 16)
            sp.dma_start(tri[:, :], tri_dram).then_inc(loaded, 16)
            sp.dma_start(prio[:, :], prio_dram.partition_broadcast(S)).then_inc(loaded, 16)
            sp.dma_start(starts[:, :], starts_dram.rearrange("(o n) -> o n", o=1)).then_inc(loaded, 16)
            sp.wait_ge(zero_set, 1)
            zv = xs_dram.rearrange("(q p r) d -> q p (r d)", q=4, p=P)
            for k in range(4):
                sp.dma_start(zv[k], zero[:, :, :].rearrange("p r d -> p (r d)")).then_inc(zeroed, 16)

        @block.gpsimd
        def _(pool):
            nc.gpsimd.memset(zero[:, :, :], 0.0).then_inc(zero_set, 1)
            with nc.gpsimd.Fori(0, NB) as b:
                pool.wait_ge(f_ready, b + 1)
                nc.gpsimd.tensor_tensor(one(x, b), one(x, b), one(f, b), ALU.add).then_inc(x_ready, 1)
            pool.wait_ge(zeroed, 64)
            pool.wait_ge(slot_ready, 1)
            pool.wait_ge(xh_ready, NB)
            for b in range(NB):
                nc.gpsimd.indirect_dma_start(
                    out=xs_dram, out_offset=bass.IndirectOffsetOnAxis(ap=slot[:, b:b + 1], axis=0),
                    in_=f[:, b, :], in_offset=None, bounds_check=SLOTS - 1).then_inc(scattered, 16)
            pool.wait_ge(scattered, 16 * NB)

        @block.vector
        def _(dve):
            links = [0]

            def link(ins):
                links[0] += 1
                ins.then_inc(chain, 1)
                dve.wait_ge(chain, links[0])

            nc.vector.memset(ones[:, :], 1.0).then_inc(ones_set, 1)
            norm_chain(nc, dve, lambda b: one(x, b), NB, stats, mv, sd, stats_done, var_ready, 0)
            dve.wait_ge(sd_ready, 1)
            link(nc.vector.reciprocal(rstd[:, :], sd[:, :]))
            with nc.vector.Fori(0, NB) as b:
                nc.vector.tensor_scalar(one(f, b), one(x, b), one(mv, b)[:, 0:1], rstd[:, ds(b, 1)],
                                        ALU.subtract, ALU.mult).then_inc(f_ready, 1)
            dve.wait_ge(f_ready, NB)
            norm_chain(nc, dve, lambda b: one(f, b), NB, stats, mv, sd, stats_done, var_ready, 1)

            def affinity(b, half, p):
                dve.wait_ge(aff_done, b + 1)
                nc.vector.tensor_copy(one(aff, b), ps_a[p][0:S, 0:E0]).then_inc(aff_ready, 1)
            peeled(nc.vector, NB, affinity)
            dve.wait_ge(aff_ready, NB)
            dve.wait_ge(loaded, 64)
            nc.vector.tensor_reduce(best[:, :], aff[:, :, :], AX.X, ALU.max).then_inc(best_ready, 1)
            dve.wait_ge(best_ready, 1)
            link(nc.vector.tensor_tensor(hot[:, :, :], aff[:, :, :],
                                         best[:, :].unsqueeze(2).to_broadcast([S, NB, E0]), ALU.is_equal))
            link(nc.vector.tensor_tensor(aff[:, :, :], hot[:, :, :],
                                         prio[:, :].unsqueeze(1).to_broadcast([S, NB, E0]), ALU.mult))
            link(nc.vector.tensor_reduce(slot_f[:, :], aff[:, :, :], AX.X, ALU.max))
            nc.vector.tensor_tensor(hot[:, :, :], aff[:, :, :],
                                    slot_f[:, :].unsqueeze(2).to_broadcast([S, NB, E0]),
                                    ALU.is_equal).then_inc(hot_ready, 1)
            dve.wait_ge(sd_ready, 2)
            link(nc.vector.reciprocal(rstd[:, :], sd[:, :]))
            dve.wait_ge(x_ready, NB)
            dve.wait_ge(fs_ready, NB)
            with nc.vector.Fori(0, NB) as b:
                nc.vector.tensor_scalar(one(f, b), one(f, b), one(mv, b)[:, 0:1], rstd[:, ds(b, 1)],
                                        ALU.subtract, ALU.mult).then_inc(xh_ready, 1)
            dve.wait_ge(counted, 2)
            link(nc.vector.tensor_copy(rank[:, :, :].rearrange("p b e -> p (b e)"), ps_rank[0:S, 0:NB * E0]))
            link(nc.vector.tensor_copy(total[:, :, :].rearrange("p e b -> p b e"),
                                       ps_total[0:S, 0:NB * E0].rearrange("p (b e) -> p b e", e=E0)))
            for e in range(E0):
                ins = nc.vector.tensor_tensor_scan(before[:, e, :], ones[:, 0:NB], total[:, e, :], 0.0, ALU.mult,
                                                   ALU.add)
            link(ins)
            link(nc.vector.tensor_scalar_add(count[:, :], before[:, :, NB - 1], float(SLOT_TILE - 1)))
            link(nc.vector.tensor_copy(count_i[:, :], count[:, :]))
            link(nc.vector.tensor_scalar(count_i[:, :], count_i[:, :], SLOT_SHIFT, SLOT_SHIFT,
                                         ALU.logical_shift_right, ALU.logical_shift_left))
            link(nc.vector.tensor_copy(padded[:, :], count_i[:, :]))
            link(nc.vector.tensor_tensor_scan(end[:, :], ones[:, 0:E0], padded[:, :], 0.0, ALU.mult, ALU.add))
            link(nc.vector.tensor_tensor(base[:, :], end[:, :], padded[:, :], ALU.subtract))
            link(nc.vector.tensor_tensor(before[:, :, :], before[:, :, :], total[:, :, :], ALU.subtract))
            link(nc.vector.tensor_tensor(before[:, :, :], before[:, :, :],
                                         base[:, :].unsqueeze(2).to_broadcast([S, E0, NB]), ALU.add))
            link(nc.vector.tensor_tensor(rank[:, :, :], rank[:, :, :],
                                         before[:, :, :].rearrange("p e b -> p b e"), ALU.add))
            link(nc.vector.tensor_tensor(rank[:, :, :], rank[:, :, :], hot[:, :, :], ALU.mult))
            link(nc.vector.tensor_reduce(slot_f[:, :], rank[:, :, :], AX.X, ALU.add))
            nc.vector.tensor_copy(slot[:, :], slot_f[:, :]).then_inc(slot_ready, 1)
            link(nc.vector.tensor_tensor(past[:, :, :], end[0:1, :].unsqueeze(1).to_broadcast([1, N_ST, E0]),
                                         starts[:, :].unsqueeze(2).to_broadcast([1, N_ST, E0]), ALU.is_le))
            link(nc.vector.tensor_reduce(te_f[:, :], past[:, :, :], AX.X, ALU.add))
            link(nc.vector.tensor_scalar_min(te_f[:, :], te_f[:, :], float(E0 - 1)))
            link(nc.vector.tensor_copy(tile_expert[:, :], te_f[:, :]))

        @block.scalar
        def _(act):
            for k in range(2):
                act.wait_ge(var_ready, k + 1)
                nc.scalar.activation(sd[:, :], sd[:, :], ACT.Sqrt).then_inc(sd_ready, 1)
                if k:
                    break

                def step(b, half, p):
                    act.wait_ge(f_ready, b + 1)
                    if not isinstance(b, int) or b >= 2:
                        act.wait_ge(t_done, b - 1)
                    nc.scalar.copy(fs[p][:, :], one(f, b)).then_inc(fs_ready, 1)
                    act.wait_ge(t_done, b + 1)
                    if not isinstance(b, int) or b >= 2:
                        act.wait_ge(aff_done, b - 1)
                    nc.scalar.copy(ft[p][:, :, :].rearrange("p c s -> p (c s)"),
                                   ps_t[p][:, 0:DC * S]).then_inc(ft_ready, 1)
                peeled(nc.scalar, NB, step)
            act.wait_ge(best_ready, 1)
            nc.scalar.activation(alpha[:, :], best[:, :], ACT.Sigmoid)

        @block.tensor
        def _(pe):
            pe.wait_ge(loaded, 64)

            def affinity(b, p):
                pe.wait_ge(ft_ready, b + 1)
                if not isinstance(b, int) or b >= 2:
                    pe.wait_ge(aff_ready, b - 1)
                for c in range(DC):
                    ins = nc.tensor.matmul(ps_a[p][0:S, 0:E0], ft[p][:, c, :], cent[:, c, :], start=(c == 0),
                                           stop=(c == DC - 1))
                ins.then_inc(aff_done, 1)

            def step(b, half, p):
                pe.wait_ge(fs_ready, b + 1)
                if not isinstance(b, int) or b >= 2:
                    pe.wait_ge(ft_ready, b - 1)
                for c in range(DC):
                    ins = nc.tensor.transpose(ps_t[p][:, c * S:(c + 1) * S], fs[p][:, c * P:(c + 1) * P],
                                              ident[0:S, 0:S])
                ins.then_inc(t_done, 1)
                affinity(b, p)
            peeled(nc.tensor, NB, step)
            pe.wait_ge(hot_ready, 1)
            pe.wait_ge(ones_set, 1)
            hot_flat = hot[:, :, :].rearrange("p b e -> p (b e)")
            nc.tensor.matmul(ps_rank[0:S, 0:NB * E0], tri[:, :], hot_flat, start=True, stop=True).then_inc(counted, 1)
            nc.tensor.matmul(ps_total[0:S, 0:NB * E0], ones[:, 0:S], hot_flat, start=True,
                             stop=True).then_inc(counted, 1)


def experts0_block(nc, tile_expert, ident, xs_dram, ys_dram, w1_dram, w2_dram, affine_dram, b2_dram):
    H2 = SLOT_TILE // P
    with ExitStack() as ctx:
        m = Memory(nc, ctx, "e0")
        two = range(2)
        xs = [m.sb(f"xs{j}", [P, H2, D]) for j in two]
        w1 = [m.sb(f"w1{j}", [P, DC, F0]) for j in two]
        w2 = [m.sb(f"w2{j}", [P, FC, D]) for j in two]
        affine = [m.sb(f"affine{j}", [P, FC + 2 * DC]) for j in two]
        b2 = [m.sb(f"b2{j}", [P, D]) for j in two]
        h_t = [m.sb(f"h_t{j}", [P, DC, SLOT_TILE]) for j in two]
        hid = [m.sb(f"hid{j}", [P, FC, SLOT_TILE]) for j in two]
        y = [m.sb(f"y{j}", [P, H2, D]) for j in two]
        ps_t = [m.ps(f"ps_t{j}") for j in two]
        ps_u = [m.ps(f"ps_u{j}") for j in range(4)]
        ps_y = [m.ps(f"ps_y{j}") for j in range(H2)]
        UG = FC // 4
        (t_done, h_ready, u_done, hid_ready, y_done, y_ready) = (
            m.sem(n) for n in ("t_done", "h_ready", "u_done", "hid_ready", "y_done", "y_ready"))
        xs_loaded = [m.sem(f"xs_loaded{j}") for j in two]
        w1_loaded = [m.sem(f"w1_loaded{j}") for j in two]
        w2_loaded = [m.sem(f"w2_loaded{j}") for j in two]
        stored = [m.sem(f"stored{j}") for j in two]
        block = ctx.enter_context(nc.Block())

        def later(j, n):
            return not isinstance(j, int) or j >= n

        @block.sync
        def _(sp):
            def load(j, half, p):
                if later(j, 2):
                    sp.wait_ge(y_ready, (j - 1) * H2)
                e = nc.sync.value_load(tile_expert[0:1, ds(j, 1)], min_val=0, max_val=E0 - 1)
                sp.dma_start(xs[p][:, :, :], xs_dram[ds(j * SLOT_TILE, SLOT_TILE), :].rearrange(
                    "(s p) d -> p s d", p=P)).then_inc(xs_loaded[p], 16)
                sp.dma_start(affine[p][:, :], affine_dram[ds(e, 1)].rearrange("o p n -> p (o n)")
                             ).then_inc(xs_loaded[p], 16)
                sp.dma_start(w1[p][:, :, :], w1_dram[ds(e, 1)].rearrange("o p c n -> p (o c) n")
                             ).then_inc(w1_loaded[p], 16)
                sp.dma_start(w2[p][:, :, :], w2_dram[ds(e, 1)].rearrange("o p c n -> p (o c) n")
                             ).then_inc(w2_loaded[p], 16)
                sp.dma_start(b2[p][:, :], b2_dram[ds(e, 1), :].rearrange("o d -> (o d)").partition_broadcast(P)
                             ).then_inc(w2_loaded[p], 16)
            peeled(nc.sync, N_ST, load)

        @block.gpsimd
        def _(pool):
            def store(j, half, p):
                pool.wait_ge(y_ready, (j + 1) * H2)
                pool.dma_start(ys_dram[ds(j * SLOT_TILE, SLOT_TILE), :].rearrange("(s p) d -> p s d", p=P),
                               y[p][:, :, :]).then_inc(stored[p], 16)
            peeled(nc.gpsimd, N_ST, store)
            for p in two:
                pool.wait_ge(stored[p], 16 * N_ST // 2)

        @block.vector
        def _(dve):
            def scale_in(j, half, p):
                dve.wait_ge(t_done, j + 1)
                if later(j, 2):
                    dve.wait_ge(u_done, (j - 1) * 4)
                for c in range(DC):
                    ins = nc.vector.tensor_scalar(h_t[p][:, c, :], ps_t[p][:, c * SLOT_TILE:(c + 1) * SLOT_TILE],
                                                  affine[p][:, FC + c:FC + c + 1],
                                                  affine[p][:, FC + DC + c:FC + DC + c + 1], ALU.mult, ALU.add)
                ins.then_inc(h_ready, 1)

            def tile(j, half, p):
                if not isinstance(j, int) or j < N_ST - 1:
                    scale_in(j + 1, half + p, 1 - p)
                if later(j, 2) or not isinstance(j, int):
                    dve.wait_ge(stored[p], half * 16)
                for s in range(H2):
                    dve.wait_ge(y_done, j * H2 + s + 1)
                    nc.vector.tensor_tensor(y[p][:, s, :], ps_y[s][:, 0:D], b2[p][:, :], ALU.add).then_inc(y_ready, 1)
            scale_in(0, 0, 0)
            peeled(nc.vector, N_ST, tile)

        @block.scalar
        def _(act):
            def tile(j, half, p):
                if later(j, 2):
                    act.wait_ge(y_done, (j - 1) * H2)
                for fc in range(FC):
                    act.wait_ge(u_done, j * 4 + fc // UG + 1)
                    o = fc % UG * SLOT_TILE
                    nc.scalar.activation(hid[p][:, fc, :], ps_u[fc // UG][:, o:o + SLOT_TILE], ACT.Relu,
                                         bias=affine[p][:, fc:fc + 1]).then_inc(hid_ready, 1)
            peeled(nc.scalar, N_ST, tile)

        @block.tensor
        def _(pe):
            def transposes(j, half, p):
                pe.wait_ge(xs_loaded[p], half * 32 + 32)
                if later(j, 2):
                    pe.wait_ge(h_ready, j - 1)
                for c in range(DC):
                    for s in range(H2):
                        o = c * SLOT_TILE + s * P
                        ins = nc.tensor.transpose(ps_t[p][:, o:o + P], xs[p][:, s, c * P:(c + 1) * P], ident[:, :])
                ins.then_inc(t_done, 1)

            def tile(j, half, p):
                pe.wait_ge(h_ready, j + 1)
                pe.wait_ge(w1_loaded[p], half * 16 + 16)
                for g in range(4):
                    if later(j, 1):
                        pe.wait_ge(hid_ready, j * FC + (g + 1 - 4) * UG)
                    for fc in range(g * UG, (g + 1) * UG):
                        o = fc % UG * SLOT_TILE
                        for c in range(DC):
                            ins = nc.tensor.matmul(ps_u[g][:, o:o + SLOT_TILE], w1[p][:, c, fc * P:(fc + 1) * P],
                                                   h_t[p][:, c, :], start=(c == 0), stop=(c == DC - 1))
                    ins.then_inc(u_done, 1)
                if not isinstance(j, int) or j < N_ST - 1:
                    transposes(j + 1, half + p, 1 - p)
                pe.wait_ge(hid_ready, (j + 1) * FC)
                pe.wait_ge(w2_loaded[p], half * 32 + 32)
                for s in range(H2):
                    if later(j, 1):
                        pe.wait_ge(y_ready, j * H2 + s + 1 - H2)
                    for fc in range(FC):
                        ins = nc.tensor.matmul(ps_y[s][:, 0:D], hid[p][:, fc, s * P:(s + 1) * P], w2[p][:, fc, :],
                                               start=(fc == 0), stop=(fc == FC - 1))
                    ins.then_inc(y_done, 1)
            transposes(0, 0, 0)
            peeled(nc.tensor, N_ST, tile)


def combine_block(nc, x, alpha, slot, ys_dram):
    NG = 4
    with ExitStack() as ctx:
        m = Memory(nc, ctx, "cb")
        y = m.sb("y", [S, NB, D])
        gathered = [m.sem(f"gathered{j}") for j in range(NG)]
        block = ctx.enter_context(nc.Block())

        @block.gpsimd
        def _(pool):
            for b in range(NB):
                nc.gpsimd.indirect_dma_start(
                    out=y[:, b, :], out_offset=None, in_=ys_dram,
                    in_offset=bass.IndirectOffsetOnAxis(ap=slot[:, b:b + 1], axis=0),
                    bounds_check=SLOTS - 1).then_inc(gathered[b // (NB // NG)], 16)

        @block.vector
        def _(dve):
            for j in range(NG):
                dve.wait_ge(gathered[j], 16 * NB // NG)
                for b in range(j * NB // NG, (j + 1) * NB // NG):
                    nc.vector.scalar_tensor_tensor(x[:, b, :], y[:, b, :], alpha[:, b:b + 1], x[:, b, :], ALU.mult,
                                                   ALU.add)


def tokens_block(nc, x, acc, x_s, comb, ident, x3_dram, gate_dram, lower_dram):
    with ExitStack() as ctx:
        m = Memory(nc, ctx, "tk")
        gate = m.sb("gate", [P, DC, E1])
        lower = m.sb("lower", [P, G1 * G1])
        stats = m.sb("stats", [P, TT, 6])
        mv = m.sb("mv", [P, TT, 2])
        sd = m.sb("sd", [P, TT])
        rstd = m.sb("rstd", [P, TT])
        xn = [m.sb(f"xn{j}", [P, D]) for j in range(2)]
        xf = [m.sb(f"xf{j}", [P, DC, P]) for j in range(2)]
        logit = m.sb("logit", [P, TT, E1])
        score = m.sb("score", [P, TT, E1])
        group = m.sb("group", [P, TT, G1])
        more = m.sb("more", [P, TT, G1, G1])
        same = m.sb("same", [P, TT, G1, G1])
        g_rank = m.sb("g_rank", [P, TT, G1])
        g_sel = m.sb("g_sel", [P, TT, G1])
        top = m.sb("top", [P, TT, TOP_K])
        rest = m.sb("rest", [P, TT, E1])
        den = m.sb("den", [P, TT])
        den_inv = m.sb("den_inv", [P, TT])
        ps_t = [m.ps(f"ps_t{j}") for j in range(2)]
        ps_l = [m.ps(f"ps_l{j}") for j in range(2)]
        (saved, loaded, x_loaded, stats_done, var_ready, sd_ready, rstd_ready, xn_ready, t_done, xf_ready, high_ready,
         low_ready, l_done, l_ready, score_ready, chain) = (
            m.sem(n) for n in ("saved", "loaded", "x_loaded", "stats_done", "var_ready", "sd_ready", "rstd_ready",
                               "xn_ready", "t_done", "xf_ready", "high_ready", "low_ready", "l_done", "l_ready",
                               "score_ready", "chain"))
        block = ctx.enter_context(nc.Block())

        def one(t, k):
            return t[:, ds(k, 1), :].rearrange("p o d -> p (o d)")

        @block.sync
        def _(sp):
            sp.dma_start(x3_dram.rearrange("(b s) d -> s b d", s=S), x[:, :, :]).then_inc(saved, 16)
            sp.dma_start(gate[:, :, :], gate_dram).then_inc(loaded, 16)
            sp.dma_start(lower[:, :], lower_dram.partition_broadcast(P)).then_inc(loaded, 16)
            sp.wait_ge(saved, 16)
            sp.dma_start(acc[:, :, :], x3_dram.rearrange("(t p) d -> p t d", p=P)).then_inc(x_loaded, 16)

        @block.vector
        def _(dve):
            links = [0]

            def link(ins):
                links[0] += 1
                ins.then_inc(chain, 1)
                dve.wait_ge(chain, links[0])

            dve.wait_ge(x_loaded, 16)
            norm_chain(nc, dve, lambda k: one(acc, k), TT, stats, mv, sd, stats_done, var_ready, 0)
            dve.wait_ge(sd_ready, 1)
            nc.vector.reciprocal(rstd[:, :], sd[:, :]).then_inc(rstd_ready, 1)
            dve.wait_ge(rstd_ready, 1)

            def logits(k, p):
                dve.wait_ge(l_done, k + 1)
                nc.vector.tensor_copy(one(logit, k), ps_l[p][:, 0:E1]).then_inc(l_ready, 1)

            def tile(k, half, p):
                if not isinstance(k, int) or k >= 2:
                    dve.wait_ge(t_done, k - 1)
                nc.vector.tensor_scalar(xn[p][:, :], one(acc, k), one(mv, k)[:, 0:1], rstd[:, ds(k, 1)],
                                        ALU.subtract, ALU.mult).then_inc(xn_ready, 1)
                if not isinstance(k, int) or k >= 1:
                    logits(k - 1, 1 - p)
            peeled(nc.vector, TT, tile)
            logits(TT - 1, (TT - 1) % 2)

            dve.wait_ge(score_ready, 1)
            dve.wait_ge(loaded, 32)
            link(nc.vector.tensor_reduce(group[:, :, :], score[:, :, :].rearrange("p t (g e) -> p t g e", g=G1),
                                         AX.X, ALU.add))
            of_j = group[:, :, :].unsqueeze(2).to_broadcast([P, TT, G1, G1])
            of_i = group[:, :, :].unsqueeze(3).to_broadcast([P, TT, G1, G1])
            nc.vector.tensor_tensor(more[:, :, :, :], of_j, of_i, ALU.is_gt)
            link(nc.vector.tensor_tensor(same[:, :, :, :], of_j, of_i, ALU.is_equal))
            flat = same[:, :, :, :].rearrange("p t i j -> p t (i j)")
            link(nc.vector.tensor_tensor(flat, flat, lower[:, :].unsqueeze(1).to_broadcast([P, TT, G1 * G1]), ALU.mult))
            link(nc.vector.tensor_tensor(more[:, :, :, :].rearrange("p t i j -> p (t i j)"),
                                         more[:, :, :, :].rearrange("p t i j -> p (t i j)"),
                                         same[:, :, :, :].rearrange("p t i j -> p (t i j)"), ALU.add))
            link(nc.vector.tensor_reduce(g_rank[:, :, :], more[:, :, :, :], AX.X, ALU.add))
            link(nc.vector.tensor_scalar(g_sel[:, :, :], g_rank[:, :, :], float(TOP_G), None, ALU.is_lt))
            by_group = score[:, :, :].rearrange("p t (g e) -> p (t g) e", g=G1)
            link(nc.vector.tensor_tensor(by_group, by_group,
                                         g_sel[:, :, :].rearrange("p t g -> p (t g)").unsqueeze(2).to_broadcast(
                                             [P, TT * G1, GE]), ALU.mult))
            for k in range(TT):
                ins = nc.vector.max(top[:, k, :], score[:, k, :])
            link(ins)
            for k in range(TT):
                ins = nc.vector.match_replace(rest[:, k, :], top[:, k, :], score[:, k, :], -1.0)
            link(ins)
            link(nc.vector.tensor_tensor(rest[:, :, :], rest[:, :, :], score[:, :, :], ALU.not_equal))
            link(nc.vector.tensor_tensor(score[:, :, :], score[:, :, :], rest[:, :, :], ALU.mult))
            link(nc.vector.tensor_reduce(den[:, :], score[:, :, :], AX.X, ALU.add))
            link(nc.vector.tensor_scalar_max(den[:, :], den[:, :], 1e-12))
            link(nc.vector.reciprocal(den_inv[:, :], den[:, :]))
            nc.vector.tensor_tensor(comb[:, 0:E1, :].rearrange("p e t -> p t e"), score[:, :, :],
                                    den_inv[:, :].unsqueeze(2).to_broadcast([P, TT, E1]), ALU.mult)
            nc.vector.memset(comb[:, E1, :], 1.0)

        @block.gpsimd
        def _(pool):
            def low_part(k, half, p):
                pool.wait_ge(xf_ready, k + 1)
                pool.wait_ge(high_ready, k + 1)
                nc.gpsimd.tensor_tensor(x_s[1][:, :, ds(k * P, P)], xf[p][:, :, :],
                                        x_s[0][:, :, ds(k * P, P)].bitcast(F32), ALU.subtract).then_inc(low_ready, 1)
            peeled(nc.gpsimd, TT, low_part)

        @block.scalar
        def _(act):
            act.wait_ge(var_ready, 1)
            nc.scalar.activation(sd[:, :], sd[:, :], ACT.Sqrt).then_inc(sd_ready, 1)

            def tile(k, half, p):
                act.wait_ge(t_done, k + 1)
                if not isinstance(k, int) or k >= 2:
                    act.wait_ge(l_done, k - 1)
                    act.wait_ge(low_ready, k - 1)
                src = ps_t[p][:, 0:DC * P].rearrange("p (c s) -> p c s", c=DC)
                nc.scalar.copy(x_s[0][:, :, ds(k * P, P)], src).then_inc(high_ready, 1)
                nc.scalar.copy(xf[p][:, :, :], src).then_inc(xf_ready, 1)
            peeled(nc.scalar, TT, tile)
            act.wait_ge(l_ready, TT)
            nc.scalar.activation(score[:, :, :].rearrange("p t e -> p (t e)"),
                                 logit[:, :, :].rearrange("p t e -> p (t e)"), ACT.Sigmoid).then_inc(score_ready, 1)

        @block.tensor
        def _(pe):
            pe.wait_ge(loaded, 32)

            def logits(k, p):
                pe.wait_ge(xf_ready, k + 1)
                if not isinstance(k, int) or k >= 1:
                    pe.wait_ge(l_ready, k)
                for c in range(DC):
                    ins = nc.tensor.matmul(ps_l[p][:, 0:E1], xf[p][:, c, :], gate[:, c, :], start=(c == 0),
                                           stop=(c == DC - 1))
                ins.then_inc(l_done, 1)

            def tile(k, half, p):
                pe.wait_ge(xn_ready, k + 1)
                if not isinstance(k, int) or k >= 2:
                    pe.wait_ge(xf_ready, k - 1)
                for c in range(DC):
                    ins = nc.tensor.transpose(ps_t[p][:, c * P:(c + 1) * P], xn[p][:, c * P:(c + 1) * P], ident[:, :])
                ins.then_inc(t_done, 1)
                if not isinstance(k, int) or k >= 1:
                    logits(k - 1, 1 - p)
            peeled(nc.tensor, TT, tile)
            logits(TT - 1, (TT - 1) % 2)


def experts1_block(nc, acc, x_s, comb, w_dram, out_dram):
    NE = E1 + 1
    UNITS = [4, 4, 4, 4, 3, 3, 3]
    NU = len(UNITS)
    START = [sum(UNITS[:u]) for u in range(NU)]
    SPLIT_W = 3
    with ExitStack() as ctx:
        m = Memory(nc, ctx, "e1")
        two = range(2)
        W = 2 * DC * P + D
        w = [m.sb(f"w{j}", [P, W]) for j in two]
        w_s = [[m.sb(f"w{j}_s{i}", [P, W], F32R) for i in two] for j in two]
        wt = [m.sb(f"wt{j}", [P, TT]) for j in two]
        sg = [m.sb(f"sg{j}", [P, 512]) for j in two]
        hid = [m.sb(f"hid{j}", [P, 512]) for j in two]
        hid_s = [[m.sb(f"hid{j}_s{i}", [P, 512], F32R) for i in two] for j in two]
        ps_g = [m.ps(f"ps_g{j}") for j in two]
        ps_u = [m.ps(f"ps_u{j}") for j in two]
        ps_d = [m.ps(f"ps_d{j}") for j in range(4)]
        (w_high, w_low, g_done, u_done, s_ready, hid_ready, hid_high, hid_low, d_done, wt_ready, acc_ready, stored) = (
            m.sem(n) for n in ("w_high", "w_low", "g_done", "u_done", "s_ready", "hid_ready", "hid_high", "hid_low",
                               "d_done", "wt_ready", "acc_ready", "stored"))
        w_loaded = [m.sem(f"w_loaded{j}") for j in two]
        block = ctx.enter_context(nc.Block())

        def later(e, n):
            return not isinstance(e, int) or e >= n

        def before(e, u):
            if u:
                return e, u - 1
            return (e - 1, NU - 1) if later(e, 1) else None

        @block.sync
        def _(sp):
            def load(e, half, p):
                if later(e, 2):
                    sp.wait_ge(w_low, e - 1)
                sp.dma_start(w[p][:, :], w_dram[ds(e, 1)].rearrange("o p n -> p (o n)")).then_inc(w_loaded[p], 16)
            peeled(nc.sync, NE, load)
            out = out_dram.rearrange("(t p) d -> p t d", p=P)
            for u in range(NU):
                end = START[u] + UNITS[u]
                sp.wait_ge(acc_ready, (NE - 1) * TT + end)
                sp.dma_start(out[:, START[u]:end, :], acc[:, START[u]:end, :]).then_inc(stored, 16)
            sp.wait_ge(stored, 16 * NU)

        @block.gpsimd
        def _(pool):
            def split_w(e, p):
                pool.wait_ge(w_high, e + 1)
                nc.gpsimd.tensor_tensor(w_s[p][1][:, :], w[p][:, :], w_s[p][0][:, :].bitcast(F32),
                                        ALU.subtract).then_inc(w_low, 1)

            def expert(e, half, p):
                for u in range(NU):
                    n, q = e * NU + u, (p * NU + u) % 2
                    cols = UNITS[u] * P
                    pool.wait_ge(hid_high, n + 1)
                    nc.gpsimd.tensor_tensor(hid_s[q][1][:, 0:cols], hid[q][:, 0:cols],
                                            hid_s[q][0][:, 0:cols].bitcast(F32), ALU.subtract).then_inc(hid_low, 1)
                    if u == SPLIT_W and not (isinstance(e, int) and e == NE - 1):
                        split_w(e + 1, 1 - p)
            split_w(0, 0)
            peeled(nc.gpsimd, NE, expert)

        @block.vector
        def _(dve):
            def accumulate(e, p, u):
                for k in range(UNITS[u]):
                    t = START[u] + k
                    dve.wait_ge(d_done, e * TT + t + 1)
                    nc.vector.scalar_tensor_tensor(acc[:, t, :], ps_d[k][:, 0:D], wt[p][:, t:t + 1], acc[:, t, :],
                                                   ALU.mult, ALU.add).then_inc(acc_ready, 1)

            def expert(e, half, p):
                if later(e, 2):
                    dve.wait_ge(acc_ready, (e - 1) * TT)
                nc.vector.tensor_copy(wt[p][:, :], comb[:, ds(e, 1), :].rearrange("p o t -> p (o t)")
                                      ).then_inc(wt_ready, 1)
                dve.wait_ge(wt_ready, e + 1)
                for u in range(NU):
                    n, q = e * NU + u, (p * NU + u) % 2
                    cols = UNITS[u] * P
                    dve.wait_ge(s_ready, n + 1)
                    dve.wait_ge(u_done, n + 1)
                    if not isinstance(n, int) or n >= 2:
                        dve.wait_ge(hid_low, n - 1)
                    nc.vector.tensor_tensor(hid[q][:, 0:cols], sg[q][:, 0:cols], ps_u[q][:, 0:cols],
                                            ALU.mult).then_inc(hid_ready, 1)
                    prev = before(e, u)
                    if prev:
                        accumulate(prev[0], p if u else 1 - p, prev[1])
            peeled(nc.vector, NE, expert)
            accumulate(NE - 1, (NE - 1) % 2, NU - 1)

        @block.scalar
        def _(act):
            def split_w(e, half, p):
                act.wait_ge(w_loaded[p], half * 16 + 16)
                if later(e, 2) or not isinstance(e, int):
                    act.wait_ge(d_done, (e - 1) * TT)
                nc.scalar.copy(w_s[p][0][:, :], w[p][:, :]).then_inc(w_high, 1)

            def expert(e, half, p):
                for u in range(NU):
                    n, q = e * NU + u, (p * NU + u) % 2
                    cols = UNITS[u] * P
                    act.wait_ge(g_done, n + 1)
                    if not isinstance(n, int) or n >= 2:
                        act.wait_ge(hid_ready, n - 1)
                    nc.scalar.activation(sg[q][:, 0:cols], ps_g[q][:, 0:cols], ACT.Silu).then_inc(s_ready, 1)
                    act.wait_ge(hid_ready, n + 1)
                    if not isinstance(n, int) or n >= 2:
                        bu = before(e, u)
                        be, bu = before(*bu)
                        act.wait_ge(d_done, be * TT + START[bu] + UNITS[bu])
                    nc.scalar.copy(hid_s[q][0][:, 0:cols], hid[q][:, 0:cols]).then_inc(hid_high, 1)
                    if u == SPLIT_W and not (isinstance(e, int) and e == NE - 1):
                        split_w(e + 1, half + p, 1 - p)
            split_w(0, 0, 0)
            peeled(nc.scalar, NE, expert)

        @block.tensor
        def _(pe):
            def down(e, p, u):
                q = (p * NU + u) % 2
                pe.wait_ge(hid_low, e * NU + u + 1)
                for k in range(UNITS[u]):
                    t = START[u] + k
                    at = before(e, u)
                    while at and UNITS[at[1]] <= k:
                        at = before(*at)
                    if at:
                        pe.wait_ge(acc_ready, at[0] * TT + START[at[1]] + k + 1)
                    split_product(nc, ps_d[k][:, 0:D], [h[:, k * P:(k + 1) * P] for h in hid_s[q]],
                                  [v[:, 2 * DC * P:] for v in w_s[p]], True, True).then_inc(d_done, 1)

            def expert(e, half, p):
                pe.wait_ge(w_low, e + 1)
                for u in range(NU):
                    n, q = e * NU + u, (p * NU + u) % 2
                    cols, t0 = UNITS[u] * P, START[u] * P
                    for k, (bank, sem_done) in enumerate(((ps_g[q], g_done), (ps_u[q], u_done))):
                        if not isinstance(n, int) or n >= 2:
                            pe.wait_ge((s_ready, hid_ready)[k], n - 1)
                        for c in range(DC):
                            o = (k * DC + c) * P
                            ins = split_product(nc, bank[:, 0:cols], [v[:, o:o + P] for v in w_s[p]],
                                                [v[:, c, t0:t0 + cols] for v in x_s], c == 0, c == DC - 1)
                        ins.then_inc(sem_done, 1)
                    prev = before(e, u)
                    if prev:
                        down(prev[0], p if u else 1 - p, prev[1])
            peeled(nc.tensor, NE, expert)
            down(NE - 1, (NE - 1) % 2, NU - 1)


def program(nc, a):
    xs_dram = nc.dram_tensor("sorted_in", [SLOTS, D], F32).ap()
    ys_dram = nc.dram_tensor("sorted_out", [SLOTS, D], F32).ap()
    x3_dram = nc.dram_tensor("x3", [T, D], F32).ap()
    q_dram = nc.dram_tensor("q_parts", [2, D, T], F32).ap()
    k_dram = nc.dram_tensor("k_parts", [2, D, NKE], F32).ap()
    with ExitStack() as ctx:
        m = Memory(nc, ctx, "all")
        ident = m.sb("ident", [P, P])
        loaded = m.sem("loaded")
        x = m.sb("x", [S, NB, D])
        with nc.Block() as block:
            @block.sync
            def _(sp):
                sp.dma_start(ident[:, :], a["ident"]).then_inc(loaded, 16)
                sp.wait_ge(loaded, 16)
        queries_block(nc, 0, x, None, ident, 2, a["wq0"], a["bq0"], 16 ** -0.5, a["x"], q_dram)
        attention_block(nc, 0, x, None, ident, 16, a["ctx"], a["wk0"], a["wv0"], a["wo0"], a["bk0"], a["bv0"],
                        a["bo0"], a["hmask"], q_dram, k_dram)
        with ExitStack() as c:
            mr = Memory(nc, c, "r")
            alpha = mr.sb("alpha", [S, NB])
            slot = mr.sb("slot", [S, NB], I32)
            tile_expert = mr.sb("tile_expert", [1, N_ST], I32)
            route_block(nc, x, alpha, slot, tile_expert, ident, xs_dram, a["cent"], a["tri"], a["prio"], a["starts"])
            experts0_block(nc, tile_expert, ident, xs_dram, ys_dram, a["w1"], a["w2"], a["affine"], a["b2"])
            combine_block(nc, x, alpha, slot, ys_dram)
        with ExitStack() as c:
            q_t = Memory(nc, c, "l1").sb("q_t", [P, 4, T])
            queries_block(nc, 1, x, q_t, ident, 4, a["wq1"], None, 64 ** -0.5, None, None)
            attention_block(nc, 1, x, q_t, ident, 8, a["ctx"], a["wk1"], a["wv1"], a["wo1"], None, None, a["bo1"],
                            a["hmask"], None, None)
        acc = m.sb("acc", [P, TT, D])
        x_s = [m.sb(f"x_s{i}", [P, DC, T], F32R) for i in range(2)]
        comb = m.sb("comb", [P, E1 + 1, TT])
        tokens_block(nc, x, acc, x_s, comb, ident, x3_dram, a["gate"], a["lower"])
        experts1_block(nc, acc, x_s, comb, a["we1"], a["out"].rearrange("b s d -> (b s) d"))


def kernel(**inputs):
    import numpy as np
    import concourse.bacc as bacc
    from concourse.bass_utils import run_bass_kernel_spmd

    def chunks(w):
        w = np.asarray(w)
        return np.ascontiguousarray(w.reshape(w.shape[0] // P, P, -1).transpose(1, 0, 2))

    def column(v):
        return np.ascontiguousarray(np.asarray(v).reshape(-1, P).T)

    g = {k: np.asarray(v) for k, v in inputs.items()}
    a = {
        "x": g["x"],
        "ctx": g["ctx_1024"].transpose(0, 2, 1).reshape(NB, DC, P, NK).transpose(0, 2, 1, 3),
        "ident": np.eye(P, dtype=np.float32),
        "bq0": column(g["L0_xattn_bq"]), "bk0": column(g["L0_xattn_bk"]), "bv0": g["L0_xattn_bv"],
        "bo0": g["L0_xattn_bo"], "bo1": g["L1_xattn_bo"], 
        "hmask": (np.arange(P)[:, None] // 64 == np.arange(2)[None]).astype(np.float32),
        "cent": chunks(g["L0_ffn_centroids"].T),
        "tri": np.triu(np.ones((S, S), np.float32), 1),
        "prio": np.arange(E0, 0, -1).astype(np.float32),
        "starts": (np.arange(N_ST) * SLOT_TILE).astype(np.float32),
        "w1": g["L0_ffn_w1"].reshape(E0, DC, P, F0).transpose(0, 2, 1, 3),
        "w2": g["L0_ffn_w2"].reshape(E0, FC, P, D).transpose(0, 2, 1, 3),
        "affine": np.concatenate([g["L0_ffn_b1"].reshape(E0, FC, P), g["L0_ffn_gamma"].reshape(E0, DC, P),
                                  g["L0_ffn_beta"].reshape(E0, DC, P)], 1).transpose(0, 2, 1),
        "b2": g["L0_ffn_b2"],
        "gate": chunks(g["L1_ffn_gate_w"].T),
        "lower": np.tril(np.ones((G1, G1), np.float32), -1).reshape(-1),
    }
    for n in "qkvo":
        a[f"w{n}0"] = chunks(g[f"L0_xattn_W{n}"].T)
        a[f"w{n}1"] = chunks(g[f"L1_xattn_W{n}"])
    up = [np.concatenate([g[f"L1_ffn_expert_{k}"], g[f"L1_ffn_shared_{k}_w"][None]]) for k in ("gate", "up", "down")]
    by_input = [w.transpose(0, 2, 1).reshape(E1 + 1, DC, P, P).transpose(0, 2, 1, 3).reshape(E1 + 1, P, DC * P)
                for w in up[:2]]
    a["we1"] = np.concatenate([*by_input, up[2].transpose(0, 2, 1)], 2)

    nc = bacc.Bacc("TRN2", target_bir_lowering=False, num_devices=1)
    arrays, aps = {}, {}
    for name, v in a.items():
        arrays[f"in_{name}"] = np.ascontiguousarray(v)
        aps[name] = nc.dram_tensor(f"in_{name}", arrays[f"in_{name}"].shape, F32, kind="ExternalInput").ap()
    aps["out"] = nc.dram_tensor("out_x", (NB, S, D), F32, kind="ExternalOutput").ap()
    program(nc, aps)
    r = run_bass_kernel_spmd(nc, [arrays], core_ids=[0])
    return r.results[0]["out_x"]
```

```python
from contextlib import ExitStack

import concourse.bass as bass
from concourse import mybir

F32 = mybir.dt.float32
F32R = mybir.dt.float32r
I32 = mybir.dt.int32
ALU = mybir.AluOpType
ACT = mybir.ActivationFunctionType
AX = mybir.AxisListType
ds = bass.ds

P = 128
NB, S, D = 32, 100, 256
NK = 361
KC = 3
NKP = KC * P
NKE = NK + 1
DC = D // P
T = NB * S
E0, F0, FC = 8, 1024, 8
SLOT_TILE = 256
SLOT_SHIFT = 8
N_ST = (T + E0 * (SLOT_TILE - 1)) // SLOT_TILE
SLOTS = N_ST * SLOT_TILE
E1, G1, GE = 32, 8, 4
TOP_G, TOP_K = 4, 8
TT = T // P
EPS = 1e-5


def peeled(engine, n, body):
    body(0, 0, 0)
    body(1, 0, 1)
    pairs = (n - 3) // 2
    with engine.Fori(0, pairs) as i:
        body(i * 2 + 2, i + 1, 0)
        body(i * 2 + 3, i + 1, 1)
    for k in range(2 * pairs + 2, n):
        body(k, k // 2, k % 2)


def split_product(nc, out, lhs, rhs, first, last):
    parts = ((lhs[0], rhs[0]), (lhs[0], rhs[1]), (lhs[1], rhs[0]))
    for n, (x, y) in enumerate(parts):
        ins = nc.tensor.matmul(out, x, y, start=first and n == 0, stop=last and n == len(parts) - 1)
    return ins


class Memory:

    def __init__(self, nc, ctx, stage):
        self.nc, self.ctx, self.stage = nc, ctx, stage

    def sb(self, name, shape, dt=F32):
        return self.ctx.enter_context(self.nc.sbuf_tensor(f"{self.stage}_{name}", shape, dt))

    def ps(self, name, shape=(P, 512)):
        return self.ctx.enter_context(self.nc.psum_tensor(f"{self.stage}_{name}", list(shape), F32))

    def sem(self, name):
        return self.ctx.enter_context(self.nc.semaphore(f"{self.stage}_{name}"))


def queries_block(nc, lvl, x, q_t, ident, nch, wq_dram, bq_dram, scale, x_dram, q_dram, stats, ident_dram):
    G = 4
    with ExitStack() as ctx:
        m = Memory(nc, ctx, f"q{lvl}")
        wq = m.sb("wq", [P, DC, nch * P])
        bq = m.sb("bq", [P, nch])
        mv = m.sb("mv", [S, NB, 2])
        sd = m.sb("sd", [S, NB])
        rstd = m.sb("rstd", [S, NB])
        xn = [m.sb(f"xn{j}", [S, D]) for j in range(2)]
        xg = [m.sb(f"xg{j}", [P, DC, G * S]) for j in range(2)]
        if q_dram is not None:
            one = m.sb("one", [P, 1])
            q_g = [m.sb(f"q_g{j}", [P, nch, G * S]) for j in range(2)]
            q_s = [[m.sb(f"q_s{j}_{i}", [P, nch, G * S], F32R) for i in range(2)] for j in range(2)]
            q_high, q_low = m.sem("q_high"), m.sem("q_low")
            q_stored = [m.sem(f"q_stored{j}") for j in range(2)]
        ps_t = [m.ps(f"ps_t{j}") for j in range(2)]
        ps_q = [m.ps(f"ps_q{j}") for j in range(4)]
        loaded, stats_done, var_ready, sd_ready, xn_ready, t_done, t_evac, q_done, q_evac = (
            m.sem(n) for n in ("loaded", "stats_done", "var_ready", "sd_ready", "xn_ready",
                               "t_done", "t_evac", "q_done", "q_evac"))
        n_loads = 1 + (bq_dram is not None) + (ident_dram is not None)
        XG = NB // 4
        x_loaded = [m.sem(f"x_loaded{j}") for j in range(NB // XG)] if x_dram is not None else None
        block = ctx.enter_context(nc.Block())

        @block.sync
        def _(sp):
            if ident_dram is not None:
                sp.dma_start(ident[:, :], ident_dram).then_inc(loaded, 16)
            if x_dram is not None:
                for j in range(NB // XG):
                    of_j = slice(j * XG, (j + 1) * XG)
                    sp.dma_start(x[:, of_j, :], x_dram[of_j].rearrange("b s d -> s b d")).then_inc(x_loaded[j], 16)
            sp.dma_start(wq[:, :, :], wq_dram).then_inc(loaded, 16)
            if bq_dram is not None:
                sp.dma_start(bq[:, :], bq_dram).then_inc(loaded, 16)
            if q_dram is None:
                return

            def store(g, half, gp):
                for i, split in enumerate((q_high, q_low)):
                    sp.wait_ge(split, g + 1 + i)
                    sp.dma_start(q_dram[i].rearrange("(c p) t -> p c t", p=P)[:, :, ds(g * (G * S), G * S)],
                                 q_s[gp][i][:, :, :].bitcast(F32)).then_inc(q_stored[gp], 16)
            peeled(nc.sync, NB // G, store)
            for gp in range(2):
                sp.wait_ge(q_stored[gp], 32 * (NB // G // 2))

        @block.gpsimd
        def _(pool):
            if q_dram is None:
                return

            nc.gpsimd.memset(one[:, :], 1.0).then_inc(q_low, 1)

            def split(g, half, gp):
                if isinstance(g, int) and g == 0:
                    pool.wait_ge(q_low, 1)
                pool.wait_ge(q_evac, g * nch + nch)
                if not isinstance(g, int) or g >= 2:
                    pool.wait_ge(q_stored[gp], half * 32)
                nc.gpsimd.tensor_tensor(q_s[gp][0][:, :, :], q_g[gp][:, :, :],
                                        one[:, :].unsqueeze(2).to_broadcast([P, nch, G * S]),
                                        ALU.mult).then_inc(q_high, 1)
                pool.wait_ge(q_high, g + 1)
                nc.gpsimd.tensor_tensor(q_s[gp][1][:, :, :], q_g[gp][:, :, :], q_s[gp][0][:, :, :].bitcast(F32),
                                        ALU.subtract).then_inc(q_low, 1)
            peeled(nc.gpsimd, NB // G, split)

        @block.vector
        def _(dve):
            if x_dram is not None:
                for j in range(NB // XG):
                    dve.wait_ge(x_loaded[j], 16)
                    for b in range(j * XG, (j + 1) * XG):
                        nc.vector.bn_stats(stats[:, b, :], x[:, b, :]).then_inc(stats_done, 1)
                dve.wait_ge(stats_done, NB)
            dve.wait_ge(loaded, 16 * n_loads)
            for b in range(NB):
                last = nc.vector.bn_aggr(mv[:, b, :], stats[:, b, :])
            last.then_inc(stats_done, 1)
            dve.wait_ge(stats_done, 1 if x_dram is None else NB + 1)
            nc.vector.tensor_scalar_add(sd[:, :], mv[:, :, 1], EPS).then_inc(var_ready, 1)
            dve.wait_ge(sd_ready, 1)
            nc.vector.reciprocal(rstd[:, :], sd[:, :]).then_inc(stats_done, 1)
            dve.wait_ge(stats_done, 2 if x_dram is None else NB + 2)

            def normalise(b, j):
                if not isinstance(b, int) or b >= 2:
                    dve.wait_ge(t_done, b - 1)
                nc.vector.tensor_scalar(xn[j][:, :], x[:, ds(b, 1), :].rearrange("p o d -> p (o d)"),
                                        mv[:, ds(b, 1), 0:1].rearrange("p o s -> p (o s)"), rstd[:, ds(b, 1)],
                                        ALU.subtract, ALU.mult).then_inc(xn_ready, 1)

            def evacuate(g, half, gp):
                if q_dram is not None and (not isinstance(g, int) or g >= 2):
                    dve.wait_ge(q_low, g)
                for c in range(nch):
                    dve.wait_ge(q_done, g * nch + c + 1)
                    bank = ps_q[(gp * nch + c) % 4]
                    out = q_t[:, c, ds(g * (G * S), G * S)] if q_dram is None else q_g[gp][:, c, :]
                    if bq_dram is not None:
                        ins = nc.vector.tensor_scalar(out, bank[:, 0:G * S], bq[:, c:c + 1], scale, ALU.add, ALU.mult)
                    else:
                        ins = nc.vector.tensor_scalar(out, bank[:, 0:G * S], scale, None, ALU.mult)
                    ins.then_inc(q_evac, 1)

            def group(g, half, gp):
                for k in range(G):
                    normalise(g * G + k, k % 2)
                    if k == 3 and not (isinstance(g, int) and g == 0):
                        evacuate(g - 1, None, 1 - gp)
            peeled(nc.vector, NB // G, group)
            evacuate(NB // G - 1, None, 1)

        @block.scalar
        def _(act):
            act.wait_ge(var_ready, 1)
            nc.scalar.activation(sd[:, :], sd[:, :], ACT.Sqrt).then_inc(sd_ready, 1)

            def group(g, half, gp):
                if not isinstance(g, int) or g >= 2:
                    act.wait_ge(q_done, (g - 1) * nch)
                for k in range(G):
                    act.wait_ge(t_done, g * G + k + 1)
                    nc.scalar.copy(xg[gp][:, :, k * S:(k + 1) * S],
                                   ps_t[k % 2][:, 0:DC * S].rearrange("p (c s) -> p c s", c=DC)).then_inc(t_evac, 1)
            peeled(nc.scalar, NB // G, group)

        @block.tensor
        def _(pe):
            def project(g, half, gp):
                pe.wait_ge(t_evac, (g + 1) * G)
                if not (isinstance(g, int) and g == 0):
                    pe.wait_ge(q_evac, g * nch)
                for c in range(nch):
                    bank = ps_q[(gp * nch + c) % 4]
                    for k in range(DC):
                        ins = nc.tensor.matmul(bank[:, 0:G * S], wq[:, k, c * P:(c + 1) * P], xg[gp][:, k, :],
                                               start=(k == 0), stop=(k == DC - 1))
                    ins.then_inc(q_done, 1)

            def group(g, half, gp):
                for k in range(G):
                    pe.wait_ge(xn_ready, g * G + k + 1)
                    if k >= 2 or not (isinstance(g, int) and g == 0):
                        pe.wait_ge(t_evac, g * G + k - 1)
                    for c in range(DC):
                        ins = nc.tensor.transpose(ps_t[k % 2][:, c * S:(c + 1) * S], xn[k % 2][:, c * P:(c + 1) * P],
                                                  ident[0:S, 0:S])
                    ins.then_inc(t_done, 1)
                    if k == 1 and not (isinstance(g, int) and g == 0):
                        project(g - 1, None, 1 - gp)
            pe.wait_ge(loaded, 16 * n_loads)
            peeled(nc.tensor, NB // G, group)
            project(NB // G - 1, None, 1)


def attention_block(nc, lvl, x, q_t, ident, heads, ctx_dram, wk_dram, wv_dram, wo_dram, bk_dram, bv_dram,
                    bo_dram, hmask_dram, q_dram, k_dram, stats):
    dk = D // heads if lvl == 0 else 64
    H = heads
    nch = H * dk // P
    HPC = P // dk
    TRANSPOSE_LAG, PV_LAG = 2, 4
    stack = 3 * dk <= P // 2
    VN = max(dk, 32)
    K_AHEAD = 2 if stack else 1
    CTX_STEP = 5 if stack else heads - 3
    K_STEPS = (8, 9, 11, 13)
    K_PIECES = len(K_STEPS)
    Q_PARTS, K_PARTS = (0, 1, 0), (0, 0, 1)
    if lvl == 0:
        tasks = [(3, "V", 0, 0), (5, "OT", 0, 0), (6, "OP", 0, 0), (8, "V", 1, 0), (10, "V", 2, 0), (12, "K", 0, 0),
                 (14, "K", 1, 0)]
        EVAC_LAG, X_BANKS = 1, 1
        s_bank = [h % 3 for h in range(H - 1)] + [1]
    else:
        tasks = [(0, "K", 0, 0), (1, "K", 1, 1), (2, "K", 2, 0), (4, "K", 3, 1), (5, "OT", 0, 0), (5, "V", 0, 1),
                 (6, "V", 1, 0), (7, "V", 2, 1), (7, "OP", 0, 0)]
        EVAC_LAG, X_BANKS = 0, 2
        s_bank = [h % 2 for h in range(H)]
    OT_STEP = next(s for s, k, _, _ in tasks if k == "OT")
    OP_STEP = next(s for s, k, _, _ in tasks if k == "OP")

    with ExitStack() as ctx:
        m = Memory(nc, ctx, f"a{lvl}")
        w_raw = m.sb("w_raw", [P, DC, nch * P])
        wk_s = [m.sb(f"wk_s{j}", [P, DC, nch * P], F32R) for j in range(2)]
        wv_s = [m.sb(f"wv_s{j}", [P, DC, nch * P], F32R) for j in range(2)]
        wo = m.sb("wo", [P, nch, D])
        bk = m.sb("bk", [P, nch])
        bv = m.sb("bv", [P, nch * P]) if bv_dram is not None else None
        bo = m.sb("bo", [S, D])
        hmask = m.sb("hmask", [P, 2])
        ctx_t = [m.sb(f"ctx{j}", [P, DC, NKP]) for j in range(2)]
        ctx_s = [[m.sb(f"ctx{j}_s{i}", [P, DC, NKP], F32R) for i in range(2)] for j in range(2)]
        v = [m.sb(f"v{j}", [P, KC, nch * P]) for j in range(2)]
        if stack:
            kt = [[m.sb(f"kt_s{i}", [P, nch, NKE], F32R) for i in range(2)]] * 2
            k_raw = m.sb("k_raw", [P, H // 2, NKE])
            q_raw = m.sb("q_raw", [P, H // 2, S])
            ks = [m.sb(f"ks{j}", [P, H // 2, NKE], F32R) for j in range(2)]
            qs = [[m.sb(f"qs{j}", [P, H, S], F32R)] for j in range(2)]
        else:
            kt = [[m.sb(f"kt{j}_s{i}", [P, nch, NKE], F32R) for i in range(2)] for j in range(2)]
            qm = m.sb("qm", [P, H, S])
            qs = [[m.sb(f"qs{j}_s{i}", [P, H, S], F32R) for i in range(2)] for j in range(2)]
        neg_max = m.sb("neg_max", [S, 2, H])
        row_sum = m.sb("row_sum", [S, 2, H])
        row_inv = m.sb("row_inv", [S, H])
        prob = [m.sb(f"prob{j}", [S, NKP]) for j in range(4)]
        prob_t = [m.sb(f"prob_t{j}", [P, KC * S]) for j in range(4)]
        o_row = m.sb("o_row", [S, nch * P])
        o_t = m.sb("o_t", [P, nch, S])
        ps_s = [m.ps(f"ps_s{j}") for j in range(max(s_bank) + 1)]
        ps_p = [m.ps(f"ps_p{j}") for j in range(2)]
        ps_o = [m.ps(f"ps_o{j}") for j in range(2)]
        ps_x = [m.ps(f"ps_x{j}") for j in range(X_BANKS)]
        unused = ("qm_done", "q_hi") if stack else ("q_loaded", "k_stored", "k_loaded", "ks_ready")
        (loaded, cleared, w_loaded, w_ready, ctx_hi, ctx_ready, q_loaded, qm_done, q_hi, q_ready, k_done, k_hi,
         k_ready, k_stored, k_loaded, ks_ready, v_done, v_ready, xb_ready, scores_done, max_ready, prob_ready,
         pt_done, pt_ready, pv_done, inv_ready, o_ready, ot_done, ot_ready, out_done, x_ready) = (
            None if n in unused else m.sem(n) for n in
            ("loaded", "cleared", "w_loaded", "w_ready", "ctx_hi", "ctx_ready", "q_loaded", "qm_done", "q_hi",
             "q_ready", "k_done", "k_hi", "k_ready", "k_stored", "k_loaded", "ks_ready", "v_done", "v_ready",
             "xb_ready", "scores_done", "max_ready", "prob_ready", "pt_done", "pt_ready", "pv_done", "inv_ready",
             "o_ready", "ot_done", "ot_ready", "out_done", "x_ready"))
        ctx_loaded = [m.sem(f"ctx_loaded{j}") for j in range(2)]
        loads = [(wo, wo_dram), (hmask, hmask_dram)]
        if bk_dram is not None:
            loads += [(bk, bk_dram), (bv, bv_dram.partition_broadcast(P))]
        loads.append((bo, bo_dram.partition_broadcast(S)))
        LOADED = 16 * len(loads)
        CLEARED = 8 if stack else 6
        STACKED = 16 * 6

        def has_prev(b):
            return not (isinstance(b, int) and b == 0)

        def has_cur(b):
            return not (isinstance(b, int) and b >= NB)

        def has_next(b):
            return not (isinstance(b, int) and b >= NB - 1)

        def has_next2(b):
            return not (isinstance(b, int) and b >= NB - 2)

        def has_k(b):
            return has_next2(b) if K_AHEAD == 2 else has_next(b)

        def lagged(b, h, lag):
            if h >= lag:
                return b, h - lag, has_cur(b)
            return b - 1, H + h - lag, has_prev(b)

        def head_outputs(p):
            a = ps_o[p][0:S, 0:H * VN]
            return bass.AP(a.tensor, a.offset, [list(a.ap[0]), [VN // dk * VN, H * dk // VN], [VN + dk, VN // dk],
                                                [1, dk]])

        def load_ctx(engine, b, p):
            engine.dma_start(ctx_t[p][:, :, 0:NK],
                             ctx_dram[ds(b, 1)].rearrange("o p c s -> p (o c) s")).then_inc(ctx_loaded[p], 16)

        block = ctx.enter_context(nc.Block())

        @block.sync
        def _(sp):
            sp.dma_start(w_raw[:, :, :], wk_dram).then_inc(w_loaded, 16)
            if not stack:
                load_ctx(sp, 0, 0)
            for dst, src in loads:
                sp.dma_start(dst[tuple(slice(None) for _ in dst.shape)], src).then_inc(loaded, 16)
            if not stack:
                load_ctx(sp, 1, 1)
            sp.wait_ge(w_ready, 2)
            sp.dma_start(w_raw[:, :, :], wv_dram).then_inc(w_loaded, 16)

            def stacked(dram, j):
                return dram.rearrange("(pair j d) t -> j d pair t", j=2, d=dk)[j]

            def load_q(b):
                if not isinstance(b, int) or b >= 1:
                    sp.wait_ge(q_ready, b)
                for j in range(2):
                    for r, part in enumerate(Q_PARTS):
                        o = P // 2 * j + dk * r
                        sp.dma_start(q_raw[o:o + dk, :, :],
                                     stacked(q_dram[part], j)[:, :, ds(b * S, S)]).then_inc(q_loaded, 16)

            def stack_k(b):
                sp.wait_ge(k_ready, b * nch + nch)
                for part in range(2):
                    if part and (not isinstance(b, int) or b >= 1):
                        sp.wait_ge(ks_ready, b * K_PIECES)
                    sp.dma_start(k_dram[part].rearrange("(c p) n -> p c n", p=P),
                                 kt[0][part][:, :, :].bitcast(F32)).then_inc(k_stored, 16)
                sp.wait_ge(k_stored, b * 32 + 32)
                for j in range(2):
                    for r, part in enumerate(K_PARTS):
                        o = P // 2 * j + dk * r
                        sp.dma_start(k_raw[o:o + dk, :, :], stacked(k_dram[part], j)).then_inc(k_loaded, 16)

            if stack:
                sp.wait_ge(cleared, CLEARED)
                load_q(0)
                stack_k(0)
                load_q(1)
                stack_k(1)

            def batch(b, half, p):
                if not stack and has_next2(b):
                    sp.wait_ge(ctx_ready, b + 1)
                    load_ctx(sp, b + 2, p)
                if stack and has_next2(b):
                    load_q(b + 2)
                    stack_k(b + 2)
            peeled(nc.sync, NB, batch)

        @block.gpsimd
        def _(pool):
            if stack:
                load_ctx(pool, 0, 0)
                load_ctx(pool, 1, 1)
            pool.wait_ge(cleared, CLEARED)
            pool.wait_ge(loaded, LOADED)

            def spread_stacked_q(b, p):
                pool.wait_ge(q_loaded, b * STACKED + STACKED)
                nc.gpsimd.tensor_tensor(
                    qs[p][0][:, :, :].rearrange("p (pair j) s -> p pair j s", j=2),
                    q_raw[:, :, :].unsqueeze(2).to_broadcast([P, H // 2, 2, S]),
                    hmask[:, :].unsqueeze(1).unsqueeze(3).to_broadcast([P, H // 2, 2, S]),
                    ALU.mult).then_inc(q_ready, 1)

            def spread_q(b, p):
                if not isinstance(b, int) or b >= 1:
                    pool.wait_ge(q_hi, b)
                    pool.wait_ge(q_ready, b)
                for c in range(nch):
                    ins = nc.gpsimd.tensor_tensor(
                        qm[:, c * HPC:(c + 1) * HPC, :],
                        q_t[:, c, ds(b * S, S)].unsqueeze(1).to_broadcast([P, HPC, S]),
                        hmask[:, :].unsqueeze(2).to_broadcast([P, HPC, S]), ALU.mult)
                ins.then_inc(qm_done, 1)
                pool.wait_ge(q_hi, b + 1)
                nc.gpsimd.tensor_tensor(qs[p][1][:, :, :], qm[:, :, :], qs[p][0][:, :, :].bitcast(F32),
                                        ALU.subtract).then_inc(q_ready, 1)

            def split_ctx(b, p):
                pool.wait_ge(ctx_hi, b + 1)
                nc.gpsimd.tensor_tensor(ctx_s[p][1][:, :, :], ctx_t[p][:, :, :], ctx_s[p][0][:, :, :].bitcast(F32),
                                        ALU.subtract).then_inc(ctx_ready, 1)

            def add_bo(b):
                xb = x[:, ds(b, 1), :].rearrange("p o d -> p (o d)")
                nc.gpsimd.tensor_tensor(xb, xb, bo[:, :], ALU.add).then_inc(xb_ready, 1)

            def split_w(w_s, n):
                pool.wait_ge(w_ready, 2 * n + 1)
                nc.gpsimd.tensor_tensor(w_s[1][:, :, :], w_raw[:, :, :], w_s[0][:, :, :].bitcast(F32),
                                        ALU.subtract).then_inc(w_ready, 1)
            split_w(wk_s, 0)
            split_ctx(0, 0)
            split_w(wv_s, 1)
            (spread_stacked_q if stack else spread_q)(0, 0)
            split_ctx(1, 1)

            def batch(b, half, p):
                if stack and has_next2(b):
                    pool.wait_ge(ctx_ready, b + 1)
                    load_ctx(pool, b + 2, p)
                add_bo(b)
                if has_next(b):
                    if has_prev(b):
                        pool.wait_ge(scores_done, b * H)
                    (spread_stacked_q if stack else spread_q)(b + 1, 1 - p)
                if has_next2(b):
                    split_ctx(b + 2, p)
            peeled(nc.gpsimd, NB, batch)

        @block.vector
        def _(dve):
            for j in range(2):
                nc.vector.memset(ctx_t[j][:, :, NK:NKP], 0.0).then_inc(cleared, 1)
            if stack:
                nc.vector.memset(q_raw[:, :, :], 0.0).then_inc(cleared, 1)
                nc.vector.memset(k_raw[:, :, :], 0.0).then_inc(cleared, 1)
            for j in range(4):
                nc.vector.memset(prob[j][:, NK:NKP], 0.0).then_inc(cleared, 1)
            dve.wait_ge(cleared, CLEARED)
            dve.wait_ge(loaded, LOADED)

            def evac_v(b, p, kc):
                dve.wait_ge(v_done, b * KC + kc + 1)
                src = ps_x[next(k for _, kind, i, k in tasks if kind == "V" and i == kc)][:, 0:nch * P]
                if bv_dram is not None:
                    ins = nc.vector.tensor_tensor(v[p][:, kc, :], src, bv[:, :], ALU.add)
                else:
                    ins = nc.vector.tensor_copy(v[p][:, kc, :], src)
                ins.then_inc(v_ready, 1)

            def evac_k(b, p, c):
                dve.wait_ge(k_hi, b * nch + c + 1)
                bank = ps_x[next(k for _, kind, i, k in tasks if kind == "K" and i == c)]
                high = kt[p][0][:, c, :].bitcast(F32)
                if bk_dram is not None:
                    ins = nc.vector.scalar_tensor_tensor(kt[p][1][:, c, :], bank[:, 0:NKE], bk[:, c:c + 1], high,
                                                         ALU.add, ALU.subtract)
                else:
                    ins = nc.vector.tensor_tensor(kt[p][1][:, c, :], bank[:, 0:NKE], high, ALU.subtract)
                ins.then_inc(k_ready, 1)

            if K_AHEAD == 2:
                for c in range(nch):
                    evac_k(0, 0, c)
            for _, kind, i, _ in tasks:
                if kind == "K":
                    evac_k(K_AHEAD - 1, K_AHEAD - 1, i)
                elif kind == "V":
                    evac_v(0, 0, i)

            def step(b, half, p, h):
                g = b * H + h
                if has_cur(b):
                    dve.wait_ge(scores_done, g + 1)
                    nc.vector.tensor_reduce(neg_max[:, p, h:h + 1], ps_s[s_bank[h]][0:S, 0:NK], AX.X, ALU.max,
                                            negate=True).then_inc(max_ready, 1)
                bt, ht, exists = lagged(b, h, TRANSPOSE_LAG)
                if exists:
                    gt = bt * H + ht
                    dve.wait_ge(pt_done, gt + 1)
                    if not isinstance(gt, int) or gt >= 4:
                        dve.wait_ge(pv_done, gt - 3)
                    nc.vector.tensor_copy(prob_t[ht % 4][:, :], ps_p[ht % 2][:, 0:KC * S]).then_inc(pt_ready, 1)
                if has_prev(b) and h == 2:
                    dve.wait_ge(prob_ready, b * H)
                    if not (isinstance(b, int) and b == 1):
                        dve.wait_ge(o_ready, b - 1)
                    nc.vector.reciprocal(row_inv[:, :], row_sum[:, 1 - p, :]).then_inc(inv_ready, 1)
                if has_prev(b) and h == OT_STEP - 1:
                    dve.wait_ge(pv_done, b * H)
                    dve.wait_ge(inv_ready, b)
                    if not (isinstance(b, int) and b == 1):
                        dve.wait_ge(ot_done, b - 1)
                    by_group = [S, H * dk // VN, VN // dk, dk]
                    nc.vector.tensor_tensor(o_row[:, :].rearrange("p (g j d) -> p g j d", j=VN // dk, d=dk),
                                            head_outputs(1 - p),
                                            row_inv[:, :].rearrange("p (g j) -> p g j", j=VN // dk).unsqueeze(3)
                                            .to_broadcast(by_group),
                                            ALU.mult).then_inc(o_ready, 1)
                if has_k(b):
                    for s, kind, i, _ in tasks:
                        if s + EVAC_LAG == h and kind == "K":
                            evac_k(b + K_AHEAD, (p + K_AHEAD) % 2, i)
                if has_next(b):
                    for s, kind, i, _ in tasks:
                        if s + EVAC_LAG == h and kind == "V":
                            if has_prev(b):
                                dve.wait_ge(pv_done, b * H)
                            evac_v(b + 1, 1 - p, i)
                if has_prev(b) and h == OP_STEP + EVAC_LAG:
                    dve.wait_ge(out_done, b)
                    dve.wait_ge(xb_ready, b)
                    xb = x[:, ds(b - 1, 1), :].rearrange("p o d -> p (o d)")
                    bank = ps_x[next(k for _, kind, _, k in tasks if kind == "OP")]
                    nc.vector.tensor_tensor(xb, bank[0:S, 0:D], xb, ALU.add).then_inc(x_ready, 1)
                if stats is not None and has_prev(b) and h == OP_STEP + EVAC_LAG + 1:
                    dve.wait_ge(x_ready, b)
                    nc.vector.bn_stats(stats[:, ds(b - 1, 1), :].rearrange("p o s -> p (o s)"),
                                       x[:, ds(b - 1, 1), :].rearrange("p o d -> p (o d)"))

            def batch(b, half, p):
                for h in range(H):
                    step(b, half, p, h)
            peeled(nc.vector, NB, batch)
            for h in range(OP_STEP + 2 + EVAC_LAG):
                step(NB, NB // 2, 0, h)

        @block.scalar
        def _(act):
            act.wait_ge(loaded, LOADED)
            act.wait_ge(cleared, CLEARED)

            def evac_k(b, p, c):
                act.wait_ge(k_done, b * nch + c + 1)
                if stack and (not isinstance(b, int) or b >= 1):
                    act.wait_ge(k_stored, b * 32)
                bank = ps_x[next(k for _, kind, i, k in tasks if kind == "K" and i == c)]
                if bk_dram is not None:
                    ins = nc.scalar.activation(kt[p][0][:, c, :], bank[:, 0:NKE], ACT.Identity, bias=bk[:, c:c + 1])
                else:
                    ins = nc.scalar.copy(kt[p][0][:, c, :], bank[:, 0:NKE])
                ins.then_inc(k_hi, 1)

            def split_ctx(b, half, p):
                act.wait_ge(ctx_loaded[p], half * 16 + 16)
                if not isinstance(b, int) or b >= 2:
                    act.wait_ge(v_done, (b - 1) * KC)
                nc.scalar.copy(ctx_s[p][0][:, :, :], ctx_t[p][:, :, :]).then_inc(ctx_hi, 1)

            def split_q(b, p):
                act.wait_ge(qm_done, b + 1)
                nc.scalar.copy(qs[p][0][:, :, :], qm[:, :, :]).then_inc(q_hi, 1)

            def split_w(w_s, n):
                act.wait_ge(w_loaded, 16 * n + 16)
                nc.scalar.copy(w_s[0][:, :, :], w_raw[:, :, :]).then_inc(w_ready, 1)
            split_w(wk_s, 0)
            split_ctx(0, 0, 0)
            split_w(wv_s, 1)
            if not stack:
                split_q(0, 0)
            split_ctx(1, 0, 1)
            for c in range(nch):
                evac_k(0, 0, c)

            def copy_stacked_k(b, p, piece):
                if piece == 0:
                    act.wait_ge(k_loaded, b * STACKED + STACKED)
                    if not isinstance(b, int) or b >= 2:
                        act.wait_ge(scores_done, (b - 1) * H)
                pairs = slice(piece * H // 2 // K_PIECES, (piece + 1) * H // 2 // K_PIECES)
                nc.scalar.copy(ks[p][:, pairs, :], k_raw[:, pairs, :]).then_inc(ks_ready, 1)
            if stack:
                for piece in range(K_PIECES):
                    copy_stacked_k(0, 0, piece)
                for c in range(nch):
                    evac_k(1, 1, c)

            def step(b, half, p, h):
                g = b * H + h
                if has_cur(b):
                    act.wait_ge(max_ready, g + 1)
                    if not isinstance(g, int) or g >= 4:
                        act.wait_ge(pt_done, g - 3)
                    if h == 0 and not (isinstance(b, int) and b < 2):
                        act.wait_ge(inv_ready, b - 1)
                    nc.scalar.activation(prob[h % 4][:, 0:NK], ps_s[s_bank[h]][0:S, 0:NK], ACT.Exp,
                                         bias=neg_max[:, p, h:h + 1],
                                         accum_out=row_sum[:, p, h:h + 1]).then_inc(prob_ready, 1)
                if has_prev(b) and h == OT_STEP:
                    act.wait_ge(ot_done, b)
                    if not (isinstance(b, int) and b == 1):
                        act.wait_ge(out_done, b - 1)
                    bank = ps_x[next(k for _, kind, _, k in tasks if kind == "OT")]
                    nc.scalar.copy(o_t[:, :, :].rearrange("p c s -> p (c s)"), bank[:, 0:nch * S]).then_inc(ot_ready, 1)
                if has_k(b):
                    for s, kind, i, _ in tasks:
                        if s == h and kind == "K":
                            evac_k(b + K_AHEAD, (p + K_AHEAD) % 2, i)
                if has_next(b):
                    if h == H // 2 and not stack:
                        split_q(b + 1, 1 - p)
                    if h in K_STEPS and stack:
                        copy_stacked_k(b + 1, 1 - p, K_STEPS.index(h))
                if has_next2(b) and h == CTX_STEP:
                    split_ctx(b + 2, half + 1, p)

            def batch(b, half, p):
                for h in range(H):
                    step(b, half, p, h)
            peeled(nc.scalar, NB, batch)
            for h in range(OT_STEP + 1):
                step(NB, NB // 2, 0, h)

        @block.tensor
        def _(pe):
            def evacuated(kind, i, b):
                return {"K": (k_ready, (b + K_AHEAD) * nch + i + 1), "V": (v_ready, (b + 1) * KC + i + 1),
                        "OT": (ot_ready, b), "OP": (x_ready, b)}[kind]

            def bank_free(n, b):
                at, bb = n, b
                while True:
                    at -= 1
                    if at < 0:
                        at, bb = len(tasks) - 1, bb - 1
                        if isinstance(bb, int) and bb < -1:
                            return
                    _, kind, i, bank = tasks[at]
                    exists = has_k(bb) if kind == "K" else has_next(bb) if kind == "V" else has_prev(bb) and not (isinstance(bb, int) and bb < 0)
                    if exists and bank == tasks[n][3]:
                        pe.wait_ge(*evacuated(kind, i, bb))
                        return

            def project_k(b, p, c, bank):
                if c == 0:
                    pe.wait_ge(ctx_ready, b + 1)
                for k in range(DC):
                    ins = split_product(nc, bank[:, 0:NKE], [w[:, k, c * P:(c + 1) * P] for w in wk_s],
                                        [t[:, k, 0:NKE] for t in ctx_s[p]], k == 0, k == DC - 1)
                ins.then_inc(k_done, 1)

            def project_v(p, kc, bank):
                for k in range(DC):
                    ins = split_product(nc, bank[:, 0:nch * P], [t[:, k, kc * P:(kc + 1) * P] for t in ctx_s[p]],
                                        [w[:, k, :] for w in wv_s], k == 0, k == DC - 1)
                ins.then_inc(v_done, 1)

            def side(n, b, half, p):
                _, kind, i, bank_at = tasks[n]
                bank = ps_x[bank_at]
                if kind in "KV":
                    if not (has_k(b) if kind == "K" else has_next(b)):
                        return
                    bank_free(n, b)
                    if kind == "K":
                        project_k(b + K_AHEAD, (p + K_AHEAD) % 2, i, bank)
                    else:
                        project_v(1 - p, i, bank)
                    return
                if not has_prev(b):
                    return
                bank_free(n, b)
                if kind == "OT":
                    pe.wait_ge(o_ready, b)
                    for c in range(nch):
                        ins = nc.tensor.transpose(bank[:, c * S:(c + 1) * S], o_row[:, c * P:(c + 1) * P],
                                                  ident[0:S, 0:S])
                    ins.then_inc(ot_done, 1)
                else:
                    pe.wait_ge(ot_ready, b)
                    for c in range(nch):
                        ins = nc.tensor.matmul(bank[0:S, 0:D], o_t[:, c, :], wo[:, c, :], start=(c == 0),
                                               stop=(c == nch - 1))
                    ins.then_inc(out_done, 1)

            def step(b, half, p, h):
                g = b * H + h
                if has_cur(b):
                    if h == 0:
                        if not stack:
                            pe.wait_ge(k_ready, b * nch + nch)
                        pe.wait_ge(q_ready, b + 1)
                    if stack and h % (H // K_PIECES) == 0:
                        pe.wait_ge(ks_ready, b * K_PIECES + h // (H // K_PIECES) + 1)
                    ago = next(k for k in range(1, H) if s_bank[h - k] == s_bank[h])
                    if not isinstance(g, int) or g >= ago:
                        pe.wait_ge(prob_ready, g + 1 - ago)
                    out = ps_s[s_bank[h]][0:S, 0:NKE]
                    if stack:
                        ins = nc.tensor.matmul(out, qs[p][0][:, h, :], ks[p][:, h // 2, :], start=True, stop=True)
                    else:
                        ins = split_product(nc, out, [q[:, h, :] for q in qs[p]],
                                            [k[:, h // HPC, :] for k in kt[p]], True, True)
                    ins.then_inc(scores_done, 1)
                bt, ht, exists = lagged(b, h, TRANSPOSE_LAG)
                if exists:
                    gt = bt * H + ht
                    pe.wait_ge(prob_ready, gt + 1)
                    if not isinstance(gt, int) or gt >= 2:
                        pe.wait_ge(pt_ready, gt - 1)
                    for kc in range(KC):
                        ins = nc.tensor.transpose(ps_p[ht % 2][:, kc * S:(kc + 1) * S],
                                                  prob[ht % 4][:, kc * P:(kc + 1) * P], ident[0:S, 0:S])
                    ins.then_inc(pt_done, 1)
                bv_, hv, exists = lagged(b, h, PV_LAG)
                if exists:
                    gv, pv = bv_ * H + hv, p if h >= PV_LAG else 1 - p
                    if hv == 0:
                        pe.wait_ge(v_ready, bv_ * KC + KC)
                        if not (isinstance(bv_, int) and bv_ < 2):
                            pe.wait_ge(o_ready, bv_ - 1)
                    pe.wait_ge(pt_ready, gv + 1)
                    for kc in range(KC):
                        f = hv * dk // VN * VN
                        ins = nc.tensor.matmul(ps_o[pv][0:S, hv * VN:(hv + 1) * VN],
                                               prob_t[hv % 4][:, kc * S:(kc + 1) * S],
                                               v[pv][:, kc, f:f + VN], start=(kc == 0),
                                               stop=(kc == KC - 1))
                    ins.then_inc(pv_done, 1)
                for n, t in enumerate(tasks):
                    if t[0] == h:
                        side(n, b, half, p)

            pe.wait_ge(loaded, LOADED)
            pe.wait_ge(cleared, CLEARED)
            if K_AHEAD == 2:
                pe.wait_ge(w_ready, 2)
                for c in range(nch):
                    if c:
                        pe.wait_ge(k_ready, c)
                    project_k(0, 0, c, ps_x[0])
                pe.wait_ge(k_ready, nch)
            pe.wait_ge(w_ready, 4)
            for n, (_, kind, i, bank) in enumerate(tasks):
                if kind in "KV":
                    bank_free(n, -1)
                    if kind == "K":
                        project_k(K_AHEAD - 1, K_AHEAD - 1, i, ps_x[bank])
                    else:
                        project_v(0, i, ps_x[bank])

            def batch(b, half, p):
                for h in range(H):
                    step(b, half, p, h)
            peeled(nc.tensor, NB, batch)
            for h in range(OP_STEP + 1):
                step(NB, NB // 2, 0, h)


def variances(nc, dve, n, stats, mv, sd, stats_done, stats_before, var_ready):
    for b in range(n):
        last = nc.vector.bn_aggr(mv[:, b, :], stats[:, b, :])
    last.then_inc(stats_done, 1)
    dve.wait_ge(stats_done, stats_before + 1)
    nc.vector.tensor_scalar_add(sd[:, :], mv[:, :, 1], EPS).then_inc(var_ready, 1)


class ExpertWeights:

    def __init__(self, nc, ctx, tile_expert, w1_dram, w2_dram):
        m = Memory(nc, ctx, "w0")
        self.nc, self.tile_expert, self.w1_dram, self.w2_dram = nc, tile_expert, w1_dram, w2_dram
        two = range(2)
        self.w1 = [m.sb(f"w1{j}", [P, DC, F0]) for j in two]
        self.w2 = [m.sb(f"w2{j}", [P, FC, D]) for j in two]
        self.w1_s = [[m.sb(f"w1{j}_s{i}", [P, DC, F0], F32R) for i in two] for j in two]
        self.w2_s = [[m.sb(f"w2{j}_s{i}", [P, FC, D], F32R) for i in two] for j in two]
        self.w_high, self.w_low = m.sem("w_high"), m.sem("w_low")
        self.w1_loaded = [m.sem(f"w1_loaded{j}") for j in two]
        self.w2_loaded = [m.sem(f"w2_loaded{j}") for j in two]

    def expert(self, j):
        return self.nc.sync.value_load(self.tile_expert[0:1, ds(j, 1)], min_val=0, max_val=E0 - 1)

    def load_w1(self, e, p):
        self.nc.sync.dma_start(self.w1[p][:, :, :], self.w1_dram[ds(e, 1)].rearrange("o p c n -> p (o c) n")
                               ).then_inc(self.w1_loaded[p], 16)

    def load_w2(self, e, p):
        self.nc.sync.dma_start(self.w2[p][:, :, :], self.w2_dram[ds(e, 1)].rearrange("o p c n -> p (o c) n")
                               ).then_inc(self.w2_loaded[p], 16)

    def pieces(self, weight):
        flat = weight[:, :, :].rearrange("p c n -> p (c n)")
        half = DC * F0 // 2
        return [flat[:, i * half:(i + 1) * half] for i in range(2)]

    def high_parts(self, weight, parts):
        for w, high in zip(self.pieces(weight), self.pieces(parts[0])):
            self.nc.scalar.copy(high, w).then_inc(self.w_high, 1)

    def low_parts(self, engine, tensor_tensor, count, weight, parts):
        for i, (w, high, low) in enumerate(zip(self.pieces(weight), self.pieces(parts[0]), self.pieces(parts[1]))):
            engine.wait_ge(self.w_high, count + i + 1)
            tensor_tensor(low, w, high.bitcast(F32), ALU.subtract).then_inc(self.w_low, 1)


def route_block(nc, weights, x, stats, alpha, slot, tile_expert, ident, xs_dram, cent_dram, tri_dram, prio_dram, starts_dram):
    G = 4
    NG = NB // G
    with ExitStack() as ctx:
        m = Memory(nc, ctx, "rt")
        zero = m.sb("zero", [P, SLOTS // P // 4, D])
        cent = m.sb("cent", [P, DC, E0])
        tri = m.sb("tri", [S, S])
        prio = m.sb("prio", [S, E0])
        starts = m.sb("starts", [1, N_ST])
        ones = m.sb("ones", [S, P])
        f = m.sb("f", [S, NB, D])
        fs = [m.sb(f"fs{j}", [S, G, D]) for j in range(2)]
        ft = [m.sb(f"ft{j}", [P, G, DC, S]) for j in range(2)]
        f_stats = m.sb("f_stats", [S, NB, 6])
        mv = m.sb("mv", [S, NB, 2])
        sd = m.sb("sd", [S, NB])
        rstd = m.sb("rstd", [S, NB])
        aff = m.sb("aff", [S, NB, E0])
        best = m.sb("best", [S, NB])
        hot = m.sb("hot", [S, NB, E0])
        rank = m.sb("rank", [S, NB, E0])
        total = m.sb("total", [S, E0, NB])
        before = m.sb("before", [S, E0, NB])
        count = m.sb("count", [S, E0])
        count_i = m.sb("count_i", [S, E0], I32)
        padded = m.sb("padded", [S, E0])
        end = m.sb("end", [S, E0])
        base = m.sb("base", [S, E0])
        slot_f = m.sb("slot_f", [S, NB])
        past = m.sb("past", [1, N_ST, E0])
        te_f = m.sb("te_f", [1, N_ST])
        ps_t = [m.ps(f"ps_t{j}") for j in range(2)]
        ps_a = [m.ps(f"ps_a{j}") for j in range(2)]
        ps_rank, ps_total = m.ps("ps_rank"), m.ps("ps_total")
        names = ("loaded", "zero_set", "zeroed", "stats_done", "var_ready", "sd_ready", "f_ready", "x_ready", "fs_ready",
                 "t_done", "ft_ready", "aff_done", "aff_ready", "chain", "best_ready", "hot_ready", "counted",
                 "slot_ready", "xh_ready", "scattered")
        (loaded, zero_set, zeroed, stats_done, var_ready, sd_ready, f_ready, x_ready, fs_ready, t_done, ft_ready,
         aff_done, aff_ready, chain, best_ready, hot_ready, counted, slot_ready, xh_ready, scattered) = (
            m.sem(n) for n in names)
        block = ctx.enter_context(nc.Block())

        def one(t, b):
            return t[:, ds(b, 1), :].rearrange("p o d -> p (o d)")

        def some(t, g):
            return t[:, ds(g * G, G), :].rearrange("p b d -> p (b d)")

        def unrolled(step):
            for g in range(NG):
                step(g, g // 2, g % 2)

        @block.sync
        def _(sp):
            sp.dma_start(cent[:, :, :], cent_dram).then_inc(loaded, 16)
            sp.dma_start(tri[:, :], tri_dram).then_inc(loaded, 16)
            sp.dma_start(prio[:, :], prio_dram.partition_broadcast(S)).then_inc(loaded, 16)
            sp.dma_start(starts[:, :], starts_dram.rearrange("(o n) -> o n", o=1)).then_inc(loaded, 16)
            sp.wait_ge(zero_set, 1)
            zv = xs_dram.rearrange("(q p r) d -> q p (r d)", q=4, p=P)
            for k in range(4):
                sp.dma_start(zv[k], zero[:, :, :].rearrange("p r d -> p (r d)")).then_inc(zeroed, 16)
            sp.wait_ge(slot_ready, 1)
            e = weights.expert(0)
            weights.load_w1(e, 0)
            weights.load_w2(e, 0)
            weights.load_w1(weights.expert(1), 1)

        @block.gpsimd
        def _(pool):
            nc.gpsimd.memset(zero[:, :, :], 0.0).then_inc(zero_set, 1)

            def add_f(g, half, p):
                pool.wait_ge(f_ready, g * G + G)
                nc.gpsimd.tensor_tensor(some(x, g), some(x, g), some(f, g), ALU.add).then_inc(x_ready, 1)
            unrolled(add_f)
            pool.wait_ge(zeroed, 64)
            pool.wait_ge(slot_ready, 1)
            for b in range(NB):
                pool.wait_ge(xh_ready, b + 1)
                nc.gpsimd.indirect_dma_start(
                    out=xs_dram, out_offset=bass.IndirectOffsetOnAxis(ap=slot[:, b:b + 1], axis=0),
                    in_=f[:, b, :], in_offset=None, bounds_check=SLOTS - 1).then_inc(scattered, 16)
            pool.wait_ge(scattered, 16 * NB)

        @block.vector
        def _(dve):
            links = [0]

            def link(ins):
                links[0] += 1
                ins.then_inc(chain, 1)
                dve.wait_ge(chain, links[0])

            link(nc.vector.memset(ones[:, :], 1.0))
            variances(nc, dve, NB, stats, mv, sd, stats_done, 0, var_ready)
            dve.wait_ge(sd_ready, 1)
            link(nc.vector.reciprocal(rstd[:, :], sd[:, :]))

            def f_statistics(g):
                dve.wait_ge(f_ready, g * G + G)
                for k in range(G):
                    nc.vector.bn_stats(one(f_stats, g * G + k), one(f, g * G + k)).then_inc(stats_done, 1)

            def affinity(g, p):
                dve.wait_ge(aff_done, g + 1)
                nc.vector.tensor_copy(some(aff, g), ps_a[p][0:S, 0:G * E0]).then_inc(aff_ready, 1)

            def step(g, half, p):
                for k in range(G):
                    b = g * G + k
                    nc.vector.tensor_scalar(one(f, b), one(x, b), one(mv, b)[:, 0:1], rstd[:, ds(b, 1)],
                                            ALU.subtract, ALU.mult).then_inc(f_ready, 1)
                if not isinstance(g, int) or g >= 1:
                    f_statistics(g - 1)
                if not isinstance(g, int) or g >= 2:
                    affinity(g - 2, p)
            unrolled(step)
            f_statistics(NG - 1)
            dve.wait_ge(stats_done, NB + 1)
            variances(nc, dve, NB, f_stats, mv, sd, stats_done, NB + 1, var_ready)
            for g in (NG - 2, NG - 1):
                affinity(g, g % 2)
            dve.wait_ge(aff_ready, NG)
            dve.wait_ge(loaded, 64)
            nc.vector.tensor_reduce(best[:, :], aff[:, :, :], AX.X, ALU.max).then_inc(best_ready, 1)
            dve.wait_ge(best_ready, 1)
            link(nc.vector.tensor_tensor(hot[:, :, :], aff[:, :, :],
                                         best[:, :].unsqueeze(2).to_broadcast([S, NB, E0]), ALU.is_equal))
            link(nc.vector.tensor_tensor(aff[:, :, :], hot[:, :, :],
                                         prio[:, :].unsqueeze(1).to_broadcast([S, NB, E0]), ALU.mult))
            link(nc.vector.tensor_reduce(slot_f[:, :], aff[:, :, :], AX.X, ALU.max))
            nc.vector.tensor_tensor(hot[:, :, :], aff[:, :, :],
                                    slot_f[:, :].unsqueeze(2).to_broadcast([S, NB, E0]),
                                    ALU.is_equal).then_inc(hot_ready, 1)
            dve.wait_ge(counted, 2)
            link(nc.vector.tensor_copy(rank[:, :, :].rearrange("p b e -> p (b e)"), ps_rank[0:S, 0:NB * E0]))
            link(nc.vector.tensor_copy(total[:, :, :].rearrange("p e b -> p b e"),
                                       ps_total[0:S, 0:NB * E0].rearrange("p (b e) -> p b e", e=E0)))
            for e in range(E0):
                ins = nc.vector.tensor_tensor_scan(before[:, e, :], ones[:, 0:NB], total[:, e, :], 0.0, ALU.mult,
                                                   ALU.add)
            link(ins)
            link(nc.vector.tensor_scalar_add(count[:, :], before[:, :, NB - 1], float(SLOT_TILE - 1)))
            link(nc.vector.tensor_copy(count_i[:, :], count[:, :]))
            link(nc.vector.tensor_scalar(count_i[:, :], count_i[:, :], SLOT_SHIFT, SLOT_SHIFT,
                                         ALU.logical_shift_right, ALU.logical_shift_left))
            link(nc.vector.tensor_copy(padded[:, :], count_i[:, :]))
            link(nc.vector.tensor_tensor_scan(end[:, :], ones[:, 0:E0], padded[:, :], 0.0, ALU.mult, ALU.add))
            link(nc.vector.tensor_tensor(base[:, :], end[:, :], padded[:, :], ALU.subtract))
            link(nc.vector.tensor_tensor(before[:, :, :], before[:, :, :], total[:, :, :], ALU.subtract))
            link(nc.vector.tensor_tensor(before[:, :, :], before[:, :, :],
                                         base[:, :].unsqueeze(2).to_broadcast([S, E0, NB]), ALU.add))
            link(nc.vector.tensor_tensor(rank[:, :, :], rank[:, :, :],
                                         before[:, :, :].rearrange("p e b -> p b e"), ALU.add))
            link(nc.vector.tensor_tensor(rank[:, :, :], rank[:, :, :], hot[:, :, :], ALU.mult))
            link(nc.vector.tensor_reduce(slot_f[:, :], rank[:, :, :], AX.X, ALU.add))
            nc.vector.tensor_copy(slot[:, :], slot_f[:, :])
            link(nc.vector.tensor_tensor(past[:, :, :], end[0:1, :].unsqueeze(1).to_broadcast([1, N_ST, E0]),
                                         starts[:, :].unsqueeze(2).to_broadcast([1, N_ST, E0]), ALU.is_le))
            link(nc.vector.tensor_reduce(te_f[:, :], past[:, :, :], AX.X, ALU.add))
            link(nc.vector.tensor_scalar_min(te_f[:, :], te_f[:, :], float(E0 - 1)))
            nc.vector.tensor_copy(tile_expert[:, :], te_f[:, :]).then_inc(slot_ready, 1)
            dve.wait_ge(sd_ready, 2)
            link(nc.vector.reciprocal(rstd[:, :], sd[:, :]))
            dve.wait_ge(x_ready, NG)
            dve.wait_ge(fs_ready, NG)
            for b in range(NB):
                nc.vector.tensor_scalar(f[:, b, :], f[:, b, :], mv[:, b, 0:1], rstd[:, b:b + 1],
                                        ALU.subtract, ALU.mult).then_inc(xh_ready, 1)
            for n, (w, parts) in enumerate(((weights.w1[0], weights.w1_s[0]), (weights.w2[0], weights.w2_s[0]),
                                            (weights.w1[1], weights.w1_s[1]))):
                weights.low_parts(dve, nc.vector.tensor_tensor, 2 * n, w, parts)

        @block.scalar
        def _(act):
            for k in range(2):
                act.wait_ge(var_ready, k + 1)
                nc.scalar.activation(sd[:, :], sd[:, :], ACT.Sqrt).then_inc(sd_ready, 1)
                if k:
                    break

                def take_f(g, half, p):
                    act.wait_ge(f_ready, g * G + G)
                    if not isinstance(g, int) or g >= 2:
                        act.wait_ge(t_done, (g - 1) * 2)
                    nc.scalar.copy(fs[p][:, :, :].rearrange("p b d -> p (b d)"), some(f, g)).then_inc(fs_ready, 1)

                def take_ft(g, half, p):
                    for i in range(2):
                        act.wait_ge(t_done, g * 2 + i + 1)
                        if i == 0 and (not isinstance(g, int) or g >= 2):
                            act.wait_ge(aff_done, g - 1)
                        nc.scalar.copy(ft[p][:, 2 * i:2 * i + 2, :, :].rearrange("p b c s -> p (b c s)"),
                                       ps_t[i][:, 0:2 * DC * S]).then_inc(ft_ready, 1)

                def step(g, half, p):
                    take_f(g, half, p)
                    if not isinstance(g, int) or g >= 1:
                        take_ft(g - 1, None, 1 - p)
                unrolled(step)
                take_ft(NG - 1, None, (NG - 1) % 2)
            act.wait_ge(best_ready, 1)
            nc.scalar.activation(alpha[:, :], best[:, :], ACT.Sigmoid)
            for loaded_w, w, parts in ((weights.w1_loaded[0], weights.w1[0], weights.w1_s[0]),
                                       (weights.w2_loaded[0], weights.w2[0], weights.w2_s[0]),
                                       (weights.w1_loaded[1], weights.w1[1], weights.w1_s[1])):
                act.wait_ge(loaded_w, 16)
                weights.high_parts(w, parts)

        @block.tensor
        def _(pe):
            pe.wait_ge(loaded, 64)

            def affinity(g, p):
                pe.wait_ge(ft_ready, g * 2 + 2)
                if not isinstance(g, int) or g >= 2:
                    pe.wait_ge(aff_ready, g - 1)
                for b in range(G):
                    for c in range(DC):
                        ins = nc.tensor.matmul(ps_a[p][0:S, b * E0:(b + 1) * E0], ft[p][:, b, c, :], cent[:, c, :],
                                               start=(c == 0), stop=(c == DC - 1))
                ins.then_inc(aff_done, 1)

            def step(g, half, p):
                pe.wait_ge(fs_ready, g + 1)
                for i in range(2):
                    if not isinstance(g, int) or g >= 1:
                        pe.wait_ge(ft_ready, (g - 1) * 2 + i + 1)
                    for b in range(2):
                        for c in range(DC):
                            o = (b * DC + c) * S
                            ins = nc.tensor.transpose(ps_t[i][:, o:o + S], fs[p][:, 2 * i + b, c * P:(c + 1) * P],
                                                      ident[0:S, 0:S])
                    ins.then_inc(t_done, 1)
                if not isinstance(g, int) or g >= 1:
                    affinity(g - 1, 1 - p)
            unrolled(step)
            affinity(NG - 1, (NG - 1) % 2)
            pe.wait_ge(hot_ready, 1)
            hot_flat = hot[:, :, :].rearrange("p b e -> p (b e)")
            nc.tensor.matmul(ps_rank[0:S, 0:NB * E0], tri[:, :], hot_flat, start=True, stop=True).then_inc(counted, 1)
            nc.tensor.matmul(ps_total[0:S, 0:NB * E0], ones[:, 0:S], hot_flat, start=True,
                             stop=True).then_inc(counted, 1)


def experts0_block(nc, weights, ident, xs_dram, ys_dram, affine_dram, b2_dram):
    H2 = SLOT_TILE // P
    UG = FC // 4
    with ExitStack() as ctx:
        m = Memory(nc, ctx, "e0")
        two = range(2)
        xs = [m.sb(f"xs{j}", [P, H2, D]) for j in two]
        w1, w2, w1_s, w2_s = weights.w1, weights.w2, weights.w1_s, weights.w2_s
        w_low, w1_loaded, w2_loaded = weights.w_low, weights.w1_loaded, weights.w2_loaded
        affine = [m.sb(f"affine{j}", [P, FC + 2 * DC]) for j in two]
        b2 = [m.sb(f"b2{j}", [P, D]) for j in two]
        h_t = m.sb("h_t", [P, DC, SLOT_TILE])
        h_s = [[m.sb(f"h{j}_s{i}", [P, DC, SLOT_TILE], F32R) for i in two] for j in two]
        hid = [m.sb(f"hid{j}", [P, FC, SLOT_TILE]) for j in two]
        hid_s = [[m.sb(f"hid{j}_s{i}", [P, FC, SLOT_TILE], F32R) for i in two] for j in two]
        y = [m.sb(f"y{j}", [P, H2, D]) for j in two]
        ps_t = [m.ps(f"ps_t{j}") for j in two]
        ps_u = [m.ps(f"ps_u{j}") for j in range(4)]
        ps_y = [m.ps(f"ps_y{j}") for j in range(H2)]
        (t_done, h_ready, u_done, hid_ready, hid_high, hid_low, y_done, y_ready) = (
            m.sem(n) for n in ("t_done", "h_ready", "u_done", "hid_ready", "hid_high", "hid_low",
                               "y_done", "y_ready"))
        xs_loaded = [m.sem(f"xs_loaded{j}") for j in two]
        b2_loaded = m.sem("b2_loaded")
        stored = [m.sem(f"stored{j}") for j in two]
        block = ctx.enter_context(nc.Block())

        def later(j, n):
            return not isinstance(j, int) or j >= n

        def exists(j):
            return not isinstance(j, int) or j < N_ST

        @block.sync
        def _(sp):
            def load_up(j, p):
                e = weights.expert(j)
                if later(j, 2):
                    sp.wait_ge(w_low, (j - 2) * 4 + 2)
                    weights.load_w1(e, p)
                if later(j, 2):
                    sp.wait_ge(hid_ready, (j - 1) * FC)
                sp.dma_start(xs[p][:, :, :], xs_dram[ds(j * SLOT_TILE, SLOT_TILE), :].rearrange(
                    "(s p) d -> p s d", p=P)).then_inc(xs_loaded[p], 16)
                if later(j, 2):
                    sp.wait_ge(b2_loaded, (j - 1) * 16)
                sp.dma_start(affine[p][:, :], affine_dram[ds(e, 1)].rearrange("o p n -> p (o n)")
                             ).then_inc(xs_loaded[p], 16)

            def load_down(j, p):
                e = weights.expert(j)
                if later(j, 2):
                    sp.wait_ge(w_low, (j - 2) * 4 + 4)
                weights.load_w2(e, p)

            def load_b2(j, p):
                e = weights.expert(j)
                if later(j, 2):
                    sp.wait_ge(y_ready, (j - 1) * H2)
                sp.dma_start(b2[p][:, :], b2_dram[ds(e, 1), :].rearrange("o d -> (o d)").partition_broadcast(P)
                             ).then_inc(b2_loaded, 16)

            def tile(j, half, p):
                if exists(j + 1):
                    load_down(j + 1, 1 - p)
                if exists(j + 2):
                    load_up(j + 2, p)
                elif exists(j + 1):
                    sp.wait_ge(b2_loaded, (j + 1) * 16)
                if exists(j + 1):
                    load_b2(j + 1, 1 - p)
            load_up(0, 0)
            load_b2(0, 0)
            load_up(1, 1)
            peeled(nc.sync, N_ST, tile)

        @block.gpsimd
        def _(pool):
            def tile(j, half, p):
                if exists(j + 1):
                    weights.low_parts(pool, nc.gpsimd.tensor_tensor, j * 4 + 6, w2[1 - p], w2_s[1 - p])
                if exists(j + 2):
                    weights.low_parts(pool, nc.gpsimd.tensor_tensor, j * 4 + 8, w1[p], w1_s[p])
                pool.wait_ge(y_ready, (j + 1) * H2)
                pool.dma_start(ys_dram[ds(j * SLOT_TILE, SLOT_TILE), :].rearrange("(s p) d -> p s d", p=P),
                               y[p][:, :, :]).then_inc(stored[p], 16)
            peeled(nc.gpsimd, N_ST, tile)
            for p in two:
                pool.wait_ge(stored[p], 16 * N_ST // 2)

        @block.vector
        def _(dve):
            def scale_in(j, p):
                dve.wait_ge(t_done, j + 1)
                if later(j, 1):
                    dve.wait_ge(h_ready, j * 3)
                if later(j, 2):
                    dve.wait_ge(u_done, (j - 1) * 4)
                for c in range(DC):
                    ins = nc.vector.tensor_scalar(h_t[:, c, :], ps_t[p][:, c * SLOT_TILE:(c + 1) * SLOT_TILE],
                                                  affine[p][:, FC + c:FC + c + 1],
                                                  affine[p][:, FC + DC + c:FC + DC + c + 1], ALU.mult, ALU.add)
                ins.then_inc(h_ready, 1)
                dve.wait_ge(h_ready, j * 3 + 1)
                nc.vector.tensor_copy(h_s[p][0][:, :, :], h_t[:, :, :]).then_inc(h_ready, 1)
                dve.wait_ge(h_ready, j * 3 + 2)
                nc.vector.tensor_tensor(h_s[p][1][:, :, :], h_t[:, :, :], h_s[p][0][:, :, :].bitcast(F32),
                                        ALU.subtract).then_inc(h_ready, 1)

            def hid_low_parts(j, p):
                if later(j, 2):
                    dve.wait_ge(y_done, (j - 1) * H2)
                for i in two:
                    dve.wait_ge(hid_high, j * 2 + i + 1)
                    of_i = slice(i * FC // 2, (i + 1) * FC // 2)
                    nc.vector.tensor_tensor(hid_s[p][1][:, of_i, :], hid[p][:, of_i, :],
                                            hid_s[p][0][:, of_i, :].bitcast(F32), ALU.subtract).then_inc(hid_low, 1)

            def tile(j, half, p):
                if exists(j + 2):
                    scale_in(j + 2, p)
                if exists(j + 1):
                    hid_low_parts(j + 1, 1 - p)
                if later(j, 2):
                    dve.wait_ge(stored[p], half * 16)
                dve.wait_ge(b2_loaded, (j + 1) * 16)
                for s in range(H2):
                    dve.wait_ge(y_done, j * H2 + s + 1)
                    nc.vector.tensor_tensor(y[p][:, s, :], ps_y[s][:, 0:D], b2[p][:, :], ALU.add).then_inc(y_ready, 1)
            scale_in(0, 0)
            scale_in(1, 1)
            hid_low_parts(0, 0)
            peeled(nc.vector, N_ST, tile)

        @block.scalar
        def _(act):
            def split(j, half, p, which):
                weight, parts, loaded = ((w1[p], w1_s[p], w1_loaded[p]), (w2[p], w2_s[p], w2_loaded[p]))[which]
                act.wait_ge(loaded, half * 16 + 16)
                if later(j, 2):
                    act.wait_ge(*((u_done, (j - 1) * 4), (y_done, (j - 1) * H2))[which])
                weights.high_parts(weight, parts)

            def relu(j, p):
                if later(j, 2):
                    act.wait_ge(hid_low, (j - 1) * 2)
                    act.wait_ge(y_done, (j - 1) * H2)
                for i in two:
                    for fc in range(i * FC // 2, (i + 1) * FC // 2):
                        act.wait_ge(u_done, j * 4 + fc // UG + 1)
                        o = fc % UG * SLOT_TILE
                        nc.scalar.activation(hid[p][:, fc, :], ps_u[fc // UG][:, o:o + SLOT_TILE], ACT.Relu,
                                             bias=affine[p][:, fc:fc + 1]).then_inc(hid_ready, 1)
                    act.wait_ge(hid_ready, j * FC + (i + 1) * FC // 2)
                    of_i = slice(i * FC // 2, (i + 1) * FC // 2)
                    nc.scalar.copy(hid_s[p][0][:, of_i, :], hid[p][:, of_i, :]).then_inc(hid_high, 1)

            def tile(j, half, p):
                if exists(j + 1):
                    split(j + 1, half + p, 1 - p, 1)
                if exists(j + 2):
                    split(j + 2, half + 1, p, 0)
                if exists(j + 1):
                    relu(j + 1, 1 - p)
            relu(0, 0)
            peeled(nc.scalar, N_ST, tile)

        @block.tensor
        def _(pe):
            def transposes(j, half, p):
                pe.wait_ge(xs_loaded[p], half * 32 + 32)
                if later(j, 2):
                    pe.wait_ge(h_ready, (j - 1) * 3)
                for c in range(DC):
                    for s in range(H2):
                        o = c * SLOT_TILE + s * P
                        ins = nc.tensor.transpose(ps_t[p][:, o:o + P], xs[p][:, s, c * P:(c + 1) * P], ident[:, :])
                ins.then_inc(t_done, 1)

            def up(j, p):
                pe.wait_ge(h_ready, j * 3 + 3)
                pe.wait_ge(w_low, j * 4 + 2)
                for g in range(4):
                    if later(j, 1):
                        pe.wait_ge(hid_ready, j * FC + (g + 1 - 4) * UG)
                    for fc in range(g * UG, (g + 1) * UG):
                        o = fc % UG * SLOT_TILE
                        for c in range(DC):
                            ins = split_product(nc, ps_u[g][:, o:o + SLOT_TILE],
                                                [w[:, c, fc * P:(fc + 1) * P] for w in w1_s[p]],
                                                [h[:, c, :] for h in h_s[p]], c == 0, c == DC - 1)
                    ins.then_inc(u_done, 1)

            def down(j, p):
                pe.wait_ge(hid_low, j * 2 + 2)
                pe.wait_ge(w_low, j * 4 + 4)
                for s in range(H2):
                    if later(j, 1):
                        pe.wait_ge(y_ready, j * H2 + s + 1 - H2)
                    for fc in range(FC):
                        ins = split_product(nc, ps_y[s][:, 0:D], [h[:, fc, s * P:(s + 1) * P] for h in hid_s[p]],
                                            [w[:, fc, :] for w in w2_s[p]], fc == 0, fc == FC - 1)
                    ins.then_inc(y_done, 1)

            def tile(j, half, p):
                if exists(j + 1):
                    up(j + 1, 1 - p)
                if exists(j + 2):
                    transposes(j + 2, half + 1, p)
                down(j, p)
            transposes(0, 0, 0)
            transposes(1, 0, 1)
            up(0, 0)
            peeled(nc.tensor, N_ST, tile)


def combine_block(nc, x, stats, alpha, slot, ys_dram):
    NG = 4
    with ExitStack() as ctx:
        m = Memory(nc, ctx, "cb")
        y = m.sb("y", [S, NB, D])
        x_ready = m.sem("x_ready")
        gathered = [m.sem(f"gathered{j}") for j in range(NG)]
        block = ctx.enter_context(nc.Block())

        @block.gpsimd
        def _(pool):
            for b in range(NB):
                nc.gpsimd.indirect_dma_start(
                    out=y[:, b, :], out_offset=None, in_=ys_dram,
                    in_offset=bass.IndirectOffsetOnAxis(ap=slot[:, b:b + 1], axis=0),
                    bounds_check=SLOTS - 1).then_inc(gathered[b // (NB // NG)], 16)

        @block.vector
        def _(dve):
            def statistics(b):
                dve.wait_ge(x_ready, b + 1)
                nc.vector.bn_stats(stats[:, b, :], x[:, b, :])

            for j in range(NG):
                dve.wait_ge(gathered[j], 16 * NB // NG)
                for b in range(j * NB // NG, (j + 1) * NB // NG):
                    nc.vector.scalar_tensor_tensor(x[:, b, :], y[:, b, :], alpha[:, b:b + 1], x[:, b, :], ALU.mult,
                                                   ALU.add).then_inc(x_ready, 1)
                    if b:
                        statistics(b - 1)
            statistics(NB - 1)


def tokens_block(nc, x, acc, x_s, comb, ident, x3_dram, gate_dram, lower_dram):
    R = 4
    LT = 512 // E1
    with ExitStack() as ctx:
        m = Memory(nc, ctx, "tk")
        gate = m.sb("gate", [P, DC, E1])
        lower = m.sb("lower", [P, G1 * G1])
        stats = m.sb("stats", [P, TT, 6])
        mv = m.sb("mv", [P, TT, 2])
        sd = m.sb("sd", [P, TT])
        rstd = m.sb("rstd", [P, TT])
        xn = [m.sb(f"xn{j}", [P, D]) for j in range(R)]
        xf = [m.sb(f"xf{j}", [P, DC, P]) for j in range(R)]
        logit = m.sb("logit", [P, TT, E1])
        score = m.sb("score", [P, TT, E1])
        group = m.sb("group", [P, TT, G1])
        more = m.sb("more", [P, TT, G1, G1])
        same = m.sb("same", [P, TT, G1, G1])
        g_rank = m.sb("g_rank", [P, TT, G1])
        g_sel = m.sb("g_sel", [P, TT, G1])
        top = m.sb("top", [P, TT, TOP_K])
        rest = m.sb("rest", [P, TT, E1])
        den = m.sb("den", [P, TT])
        den_inv = m.sb("den_inv", [P, TT])
        ps_t = [m.ps(f"ps_t{j}") for j in range(R)]
        ps_l = [m.ps(f"ps_l{j}") for j in range(2)]
        (loaded, x_loaded, stats_done, var_ready, sd_ready, xn_ready, t_done, high_ready,
         low_ready, l_done, l_ready, score_ready, chain) = (
            m.sem(n) for n in ("loaded", "x_loaded", "stats_done", "var_ready", "sd_ready",
                               "xn_ready", "t_done", "high_ready", "low_ready", "l_done", "l_ready",
                               "score_ready", "chain"))
        block = ctx.enter_context(nc.Block())

        @block.sync
        def _(sp):
            sp.dma_start(x3_dram.rearrange("(b s) d -> s b d", s=S), x[:, :, :]).then_inc(x_loaded, 16)
            sp.dma_start(gate[:, :, :], gate_dram).then_inc(loaded, 16)
            sp.dma_start(lower[:, :], lower_dram.partition_broadcast(P)).then_inc(loaded, 16)
            sp.wait_ge(x_loaded, 16)
            sp.dma_start(acc[:, :, :], x3_dram.rearrange("(t p) d -> p t d", p=P)).then_inc(x_loaded, 16)

        @block.vector
        def _(dve):
            links = [0]

            def link(ins):
                links[0] += 1
                ins.then_inc(chain, 1)
                dve.wait_ge(chain, links[0])

            dve.wait_ge(x_loaded, 32)
            for k in range(TT):
                nc.vector.bn_stats(stats[:, k, :], acc[:, k, :]).then_inc(stats_done, 1)
            dve.wait_ge(stats_done, TT)
            variances(nc, dve, TT, stats, mv, sd, stats_done, TT, var_ready)
            dve.wait_ge(sd_ready, 1)
            nc.vector.reciprocal(rstd[:, :], sd[:, :]).then_inc(stats_done, 1)
            dve.wait_ge(stats_done, TT + 2)

            for k in range(TT):
                if k >= R:
                    dve.wait_ge(t_done, k + 1 - R)
                nc.vector.tensor_scalar(xn[k % R][:, :], acc[:, k, :], mv[:, k, 0:1], rstd[:, k:k + 1],
                                        ALU.subtract, ALU.mult).then_inc(xn_ready, 1)
            for j in range(2):
                tiles = slice(j * LT, min((j + 1) * LT, TT))
                dve.wait_ge(l_done, tiles.stop)
                nc.vector.tensor_copy(logit[:, tiles, :].rearrange("p t e -> p (t e)"),
                                      ps_l[j][:, 0:(tiles.stop - tiles.start) * E1]).then_inc(l_ready, 1)

            dve.wait_ge(score_ready, 1)
            dve.wait_ge(loaded, 32)
            link(nc.vector.tensor_reduce(group[:, :, :], score[:, :, :].rearrange("p t (g e) -> p t g e", g=G1),
                                         AX.X, ALU.add))
            of_j = group[:, :, :].unsqueeze(2).to_broadcast([P, TT, G1, G1])
            of_i = group[:, :, :].unsqueeze(3).to_broadcast([P, TT, G1, G1])
            nc.vector.tensor_tensor(more[:, :, :, :], of_j, of_i, ALU.is_gt)
            link(nc.vector.tensor_tensor(same[:, :, :, :], of_j, of_i, ALU.is_equal))
            flat = same[:, :, :, :].rearrange("p t i j -> p t (i j)")
            link(nc.vector.tensor_tensor(flat, flat, lower[:, :].unsqueeze(1).to_broadcast([P, TT, G1 * G1]), ALU.mult))
            link(nc.vector.tensor_tensor(more[:, :, :, :].rearrange("p t i j -> p (t i j)"),
                                         more[:, :, :, :].rearrange("p t i j -> p (t i j)"),
                                         same[:, :, :, :].rearrange("p t i j -> p (t i j)"), ALU.add))
            link(nc.vector.tensor_reduce(g_rank[:, :, :], more[:, :, :, :], AX.X, ALU.add))
            link(nc.vector.tensor_scalar(g_sel[:, :, :], g_rank[:, :, :], float(TOP_G), None, ALU.is_lt))
            by_group = score[:, :, :].rearrange("p t (g e) -> p (t g) e", g=G1)
            link(nc.vector.tensor_tensor(by_group, by_group,
                                         g_sel[:, :, :].rearrange("p t g -> p (t g)").unsqueeze(2).to_broadcast(
                                             [P, TT * G1, GE]), ALU.mult))
            for k in range(TT):
                ins = nc.vector.max(top[:, k, :], score[:, k, :])
            link(ins)
            for k in range(TT):
                ins = nc.vector.match_replace(rest[:, k, :], top[:, k, :], score[:, k, :], -1.0)
            link(ins)
            link(nc.vector.tensor_tensor(rest[:, :, :], rest[:, :, :], score[:, :, :], ALU.not_equal))
            link(nc.vector.tensor_tensor(score[:, :, :], score[:, :, :], rest[:, :, :], ALU.mult))
            link(nc.vector.tensor_reduce(den[:, :], score[:, :, :], AX.X, ALU.add))
            link(nc.vector.tensor_scalar_max(den[:, :], den[:, :], 1e-12))
            link(nc.vector.reciprocal(den_inv[:, :], den[:, :]))
            nc.vector.tensor_tensor(comb[:, 0:E1, :].rearrange("p e t -> p t e"), score[:, :, :],
                                    den_inv[:, :].unsqueeze(2).to_broadcast([P, TT, E1]), ALU.mult)
            nc.vector.memset(comb[:, E1, :], 1.0)

        @block.gpsimd
        def _(pool):
            for k in range(TT):
                pool.wait_ge(high_ready, 2 * k + 2)
                at = slice(k * P, (k + 1) * P)
                nc.gpsimd.tensor_tensor(x_s[1][:, :, at], xf[k % R][:, :, :], x_s[0][:, :, at].bitcast(F32),
                                        ALU.subtract).then_inc(low_ready, 1)

        @block.scalar
        def _(act):
            act.wait_ge(var_ready, 1)
            nc.scalar.activation(sd[:, :], sd[:, :], ACT.Sqrt).then_inc(sd_ready, 1)

            for k in range(TT):
                act.wait_ge(t_done, k + 1)
                if k >= R:
                    act.wait_ge(l_done, k + 1 - R)
                    act.wait_ge(low_ready, k + 1 - R)
                src = ps_t[k % R][:, 0:DC * P].rearrange("p (c s) -> p c s", c=DC)
                nc.scalar.copy(xf[k % R][:, :, :], src).then_inc(high_ready, 1)
                nc.scalar.copy(x_s[0][:, :, k * P:(k + 1) * P], src).then_inc(high_ready, 1)
            act.wait_ge(l_ready, 2)
            nc.scalar.activation(score[:, :, :].rearrange("p t e -> p (t e)"),
                                 logit[:, :, :].rearrange("p t e -> p (t e)"), ACT.Sigmoid).then_inc(score_ready, 1)

        @block.tensor
        def _(pe):
            pe.wait_ge(loaded, 32)

            def logits(k):
                pe.wait_ge(high_ready, 2 * k + 1)
                o = k % LT * E1
                for c in range(DC):
                    ins = nc.tensor.matmul(ps_l[k // LT][:, o:o + E1], xf[k % R][:, c, :], gate[:, c, :],
                                           start=(c == 0), stop=(c == DC - 1))
                ins.then_inc(l_done, 1)

            for k in range(TT):
                pe.wait_ge(xn_ready, k + 1)
                if k >= R:
                    pe.wait_ge(high_ready, 2 * (k + 1 - R))
                for c in range(DC):
                    ins = nc.tensor.transpose(ps_t[k % R][:, c * P:(c + 1) * P], xn[k % R][:, c * P:(c + 1) * P],
                                              ident[:, :])
                ins.then_inc(t_done, 1)
                if k >= 2:
                    logits(k - 2)
            for k in (TT - 2, TT - 1):
                logits(k)


def experts1_block(nc, acc, x_s, comb, w_dram, out_dram):
    NE = E1 + 1
    UNITS = [4, 4, 4, 4, 3, 3, 3]
    NU = len(UNITS)
    START = [sum(UNITS[:u]) for u in range(NU)]
    SPLIT_W = 3
    with ExitStack() as ctx:
        m = Memory(nc, ctx, "e1")
        two = range(2)
        W = 2 * DC * P + D
        w = [m.sb(f"w{j}", [P, W]) for j in two]
        w_s = [[m.sb(f"w{j}_s{i}", [P, W], F32R) for i in two] for j in two]
        wt = [m.sb(f"wt{j}", [P, TT]) for j in two]
        sg = [m.sb(f"sg{j}", [P, 512]) for j in two]
        hid = [m.sb(f"hid{j}", [P, 512]) for j in two]
        hid_s = [[m.sb(f"hid{j}_s{i}", [P, 512], F32R) for i in two] for j in two]
        ps_g = [m.ps(f"ps_g{j}") for j in two]
        ps_u = [m.ps(f"ps_u{j}") for j in two]
        ps_d = [m.ps(f"ps_d{j}") for j in range(4)]
        (w_high, w_low, g_done, u_done, s_ready, hid_ready, hid_high, hid_low, d_done, wt_ready, acc_ready, stored) = (
            m.sem(n) for n in ("w_high", "w_low", "g_done", "u_done", "s_ready", "hid_ready", "hid_high", "hid_low",
                               "d_done", "wt_ready", "acc_ready", "stored"))
        w_loaded = [m.sem(f"w_loaded{j}") for j in two]
        block = ctx.enter_context(nc.Block())

        def later(e, n):
            return not isinstance(e, int) or e >= n

        def before(e, u):
            if u:
                return e, u - 1
            return (e - 1, NU - 1) if later(e, 1) else None

        @block.sync
        def _(sp):
            def load(e, half, p):
                if later(e, 2):
                    sp.wait_ge(w_low, e - 1)
                sp.dma_start(w[p][:, :], w_dram[ds(e, 1)].rearrange("o p n -> p (o n)")).then_inc(w_loaded[p], 16)
            peeled(nc.sync, NE, load)
            out = out_dram.rearrange("(t p) d -> p t d", p=P)
            for u in range(NU):
                end = START[u] + UNITS[u]
                sp.wait_ge(acc_ready, (NE - 1) * TT + end)
                sp.dma_start(out[:, START[u]:end, :], acc[:, START[u]:end, :]).then_inc(stored, 16)
            sp.wait_ge(stored, 16 * NU)

        @block.gpsimd
        def _(pool):
            def split_w(e, p):
                pool.wait_ge(w_high, e + 1)
                nc.gpsimd.tensor_tensor(w_s[p][1][:, :], w[p][:, :], w_s[p][0][:, :].bitcast(F32),
                                        ALU.subtract).then_inc(w_low, 1)

            def expert(e, half, p):
                for u in range(NU):
                    n, q = e * NU + u, (p * NU + u) % 2
                    cols = UNITS[u] * P
                    pool.wait_ge(hid_high, n + 1)
                    nc.gpsimd.tensor_tensor(hid_s[q][1][:, 0:cols], hid[q][:, 0:cols],
                                            hid_s[q][0][:, 0:cols].bitcast(F32), ALU.subtract).then_inc(hid_low, 1)
                    if u == SPLIT_W and not (isinstance(e, int) and e == NE - 1):
                        split_w(e + 1, 1 - p)
            split_w(0, 0)
            peeled(nc.gpsimd, NE, expert)

        @block.vector
        def _(dve):
            def accumulate(e, p, u):
                for k in range(UNITS[u]):
                    t = START[u] + k
                    dve.wait_ge(d_done, e * TT + t + 1)
                    nc.vector.scalar_tensor_tensor(acc[:, t, :], ps_d[k][:, 0:D], wt[p][:, t:t + 1], acc[:, t, :],
                                                   ALU.mult, ALU.add).then_inc(acc_ready, 1)

            def expert(e, half, p):
                if later(e, 2):
                    dve.wait_ge(acc_ready, (e - 1) * TT)
                nc.vector.tensor_copy(wt[p][:, :], comb[:, ds(e, 1), :].rearrange("p o t -> p (o t)")
                                      ).then_inc(wt_ready, 1)
                dve.wait_ge(wt_ready, e + 1)
                for u in range(NU):
                    n, q = e * NU + u, (p * NU + u) % 2
                    cols = UNITS[u] * P
                    dve.wait_ge(s_ready, n + 1)
                    dve.wait_ge(u_done, n + 1)
                    if not isinstance(n, int) or n >= 2:
                        dve.wait_ge(hid_low, n - 1)
                    nc.vector.tensor_tensor(hid[q][:, 0:cols], sg[q][:, 0:cols], ps_u[q][:, 0:cols],
                                            ALU.mult).then_inc(hid_ready, 1)
                    prev = before(e, u)
                    if prev:
                        accumulate(prev[0], p if u else 1 - p, prev[1])
            peeled(nc.vector, NE, expert)
            accumulate(NE - 1, (NE - 1) % 2, NU - 1)

        @block.scalar
        def _(act):
            def split_w(e, half, p):
                act.wait_ge(w_loaded[p], half * 16 + 16)
                if later(e, 2) or not isinstance(e, int):
                    act.wait_ge(d_done, (e - 1) * TT)
                nc.scalar.copy(w_s[p][0][:, :], w[p][:, :]).then_inc(w_high, 1)

            def expert(e, half, p):
                for u in range(NU):
                    n, q = e * NU + u, (p * NU + u) % 2
                    cols = UNITS[u] * P
                    act.wait_ge(g_done, n + 1)
                    if not isinstance(n, int) or n >= 2:
                        act.wait_ge(hid_ready, n - 1)
                    nc.scalar.activation(sg[q][:, 0:cols], ps_g[q][:, 0:cols], ACT.Silu).then_inc(s_ready, 1)
                    act.wait_ge(hid_ready, n + 1)
                    if not isinstance(n, int) or n >= 2:
                        bu = before(e, u)
                        be, bu = before(*bu)
                        act.wait_ge(d_done, be * TT + START[bu] + UNITS[bu])
                    nc.scalar.copy(hid_s[q][0][:, 0:cols], hid[q][:, 0:cols]).then_inc(hid_high, 1)
                    if u == SPLIT_W and not (isinstance(e, int) and e == NE - 1):
                        split_w(e + 1, half + p, 1 - p)
            split_w(0, 0, 0)
            peeled(nc.scalar, NE, expert)

        @block.tensor
        def _(pe):
            def down(e, p, u):
                q = (p * NU + u) % 2
                pe.wait_ge(hid_low, e * NU + u + 1)
                for k in range(UNITS[u]):
                    t = START[u] + k
                    at = before(e, u)
                    while at and UNITS[at[1]] <= k:
                        at = before(*at)
                    if at:
                        pe.wait_ge(acc_ready, at[0] * TT + START[at[1]] + k + 1)
                    split_product(nc, ps_d[k][:, 0:D], [h[:, k * P:(k + 1) * P] for h in hid_s[q]],
                                  [v[:, 2 * DC * P:] for v in w_s[p]], True, True).then_inc(d_done, 1)

            def expert(e, half, p):
                pe.wait_ge(w_low, e + 1)
                for u in range(NU):
                    n, q = e * NU + u, (p * NU + u) % 2
                    cols, t0 = UNITS[u] * P, START[u] * P
                    for k, (bank, sem_done) in enumerate(((ps_g[q], g_done), (ps_u[q], u_done))):
                        if not isinstance(n, int) or n >= 2:
                            pe.wait_ge((s_ready, hid_ready)[k], n - 1)
                        for c in range(DC):
                            o = (k * DC + c) * P
                            ins = split_product(nc, bank[:, 0:cols], [v[:, o:o + P] for v in w_s[p]],
                                                [v[:, c, t0:t0 + cols] for v in x_s], c == 0, c == DC - 1)
                        ins.then_inc(sem_done, 1)
                    prev = before(e, u)
                    if prev:
                        down(prev[0], p if u else 1 - p, prev[1])
            peeled(nc.tensor, NE, expert)
            down(NE - 1, (NE - 1) % 2, NU - 1)


def program(nc, a):
    xs_dram = nc.dram_tensor("sorted_in", [SLOTS, D], F32).ap()
    ys_dram = nc.dram_tensor("sorted_out", [SLOTS, D], F32).ap()
    x3_dram = nc.dram_tensor("x3", [T, D], F32).ap()
    q_dram = nc.dram_tensor("q_parts", [2, D, T], F32).ap()
    k_dram = nc.dram_tensor("k_parts", [2, D, NKE], F32).ap()
    with ExitStack() as ctx:
        m = Memory(nc, ctx, "all")
        ident = m.sb("ident", [P, P])
        x = m.sb("x", [S, NB, D])
        stats = m.sb("stats", [S, NB, 6])
        queries_block(nc, 0, x, None, ident, 2, a["wq0"], a["bq0"], 16 ** -0.5, a["x"], q_dram, stats,
                      a["ident"])
        attention_block(nc, 0, x, None, ident, 16, a["ctx"], a["wk0"], a["wv0"], a["wo0"], a["bk0"], a["bv0"],
                        a["bo0"], a["hmask"], q_dram, k_dram, stats)
        with ExitStack() as c:
            mr = Memory(nc, c, "r")
            alpha = mr.sb("alpha", [S, NB])
            slot = mr.sb("slot", [S, NB], I32)
            tile_expert = mr.sb("tile_expert", [1, N_ST], I32)
            weights = ExpertWeights(nc, c, tile_expert, a["w1"], a["w2"])
            route_block(nc, weights, x, stats, alpha, slot, tile_expert, ident, xs_dram, a["cent"], a["tri"], a["prio"], a["starts"])
            experts0_block(nc, weights, ident, xs_dram, ys_dram, a["affine"], a["b2"])
            combine_block(nc, x, stats, alpha, slot, ys_dram)
        with ExitStack() as c:
            q_t = Memory(nc, c, "l1").sb("q_t", [P, 4, T])
            queries_block(nc, 1, x, q_t, ident, 4, a["wq1"], None, 64 ** -0.5, None, None, stats, None)
            attention_block(nc, 1, x, q_t, ident, 8, a["ctx"], a["wk1"], a["wv1"], a["wo1"], None, None, a["bo1"],
                            a["hmask"], None, None, None)
        acc = m.sb("acc", [P, TT, D])
        x_s = [m.sb(f"x_s{i}", [P, DC, T], F32R) for i in range(2)]
        comb = m.sb("comb", [P, E1 + 1, TT])
        tokens_block(nc, x, acc, x_s, comb, ident, x3_dram, a["gate"], a["lower"])
        experts1_block(nc, acc, x_s, comb, a["we1"], a["out"].rearrange("b s d -> (b s) d"))


def kernel(**inputs):
    import numpy as np
    import concourse.bacc as bacc
    from concourse.bass_utils import run_bass_kernel_spmd

    def chunks(w):
        w = np.asarray(w)
        return np.ascontiguousarray(w.reshape(w.shape[0] // P, P, -1).transpose(1, 0, 2))

    def column(v):
        return np.ascontiguousarray(np.asarray(v).reshape(-1, P).T)

    g = {k: np.asarray(v) for k, v in inputs.items()}
    a = {
        "x": g["x"],
        "ctx": g["ctx_1024"].transpose(0, 2, 1).reshape(NB, DC, P, NK).transpose(0, 2, 1, 3),
        "ident": np.eye(P, dtype=np.float32),
        "bq0": column(g["L0_xattn_bq"]), "bk0": column(g["L0_xattn_bk"]), "bv0": g["L0_xattn_bv"],
        "bo0": g["L0_xattn_bo"], "bo1": g["L1_xattn_bo"], 
        "hmask": (np.arange(P)[:, None] // 64 == np.arange(2)[None]).astype(np.float32),
        "cent": chunks(g["L0_ffn_centroids"].T),
        "tri": np.triu(np.ones((S, S), np.float32), 1),
        "prio": np.arange(E0, 0, -1).astype(np.float32),
        "starts": (np.arange(N_ST) * SLOT_TILE).astype(np.float32),
        "w1": g["L0_ffn_w1"].reshape(E0, DC, P, F0).transpose(0, 2, 1, 3),
        "w2": g["L0_ffn_w2"].reshape(E0, FC, P, D).transpose(0, 2, 1, 3),
        "affine": np.concatenate([g["L0_ffn_b1"].reshape(E0, FC, P), g["L0_ffn_gamma"].reshape(E0, DC, P),
                                  g["L0_ffn_beta"].reshape(E0, DC, P)], 1).transpose(0, 2, 1),
        "b2": g["L0_ffn_b2"],
        "gate": chunks(g["L1_ffn_gate_w"].T),
        "lower": np.tril(np.ones((G1, G1), np.float32), -1).reshape(-1),
    }
    for n in "qkvo":
        a[f"w{n}0"] = chunks(g[f"L0_xattn_W{n}"].T)
        a[f"w{n}1"] = chunks(g[f"L1_xattn_W{n}"])
    up = [np.concatenate([g[f"L1_ffn_expert_{k}"], g[f"L1_ffn_shared_{k}_w"][None]]) for k in ("gate", "up", "down")]
    by_input = [w.transpose(0, 2, 1).reshape(E1 + 1, DC, P, P).transpose(0, 2, 1, 3).reshape(E1 + 1, P, DC * P)
                for w in up[:2]]
    a["we1"] = np.concatenate([*by_input, up[2].transpose(0, 2, 1)], 2)

    nc = bacc.Bacc("TRN2", target_bir_lowering=False, num_devices=1)
    arrays, aps = {}, {}
    for name, v in a.items():
        arrays[f"in_{name}"] = np.ascontiguousarray(v)
        aps[name] = nc.dram_tensor(f"in_{name}", arrays[f"in_{name}"].shape, F32, kind="ExternalInput").ap()
    aps["out"] = nc.dram_tensor("out_x", (NB, S, D), F32, kind="ExternalOutput").ap()
    program(nc, aps)
    r = run_bass_kernel_spmd(nc, [arrays], core_ids=[0])
    return r.results[0]["out_x"]
```
